# Optimizing a Trainium2 kernel written in Bass

```python
import numpy as np
import jax
import jax.numpy as jnp

def _softmax(x, axis=-1):
    return jax.nn.softmax(x, axis=axis)

def _gelu(x):
    return jax.nn.gelu(x, approximate=True)

def _silu(x):
    return jax.nn.silu(x)

def _sigmoid(x):
    return jax.nn.sigmoid(x)

def _layernorm(x, axis=-1, eps=1e-05):
    m = jnp.mean(x, axis=axis, keepdims=True)
    v = jnp.var(x, axis=axis, keepdims=True)
    return (x - m) / jnp.sqrt(v + eps)

def _scatter_add(tgt, idx, src, axis=0):
    return tgt.at[idx].add(src)

def _segment_sum(src, seg, n):
    return jax.ops.segment_sum(src, seg, n)
kernel_name = 'mk_xattn_ffn_d2_seqx_r8_077297'

def setup_inputs(seed: int=0):
    np.random.seed(seed)
    _w = jnp.asarray

    def _rec_inputs():
        import jax
        import jax.numpy as jnp
        _rk = jax.random.key(seed)
        x = 7.22e-05 + 1 * jax.random.normal(jax.random.fold_in(_rk, 1), (64, 64, 256), jnp.float32)
        _lenS = 64 - jax.random.randint(jax.random.fold_in(_rk, 7), (64,), 0, max(1, 64 // 4) + 1, jnp.int32)
        _lenS2 = 64 - jax.random.randint(jax.random.fold_in(_rk, 8), (64,), 0, max(1, 64 // 4) + 1, jnp.int32)
        _ctx_2048P = jax.random.normal(jax.random.fold_in(_rk, 11), (64, 16, 256), jnp.float32)
        _ctx_2048c = jax.random.dirichlet(jax.random.fold_in(_rk, 511), 0.3 * jnp.ones((16,), jnp.float32), (64, 64))
        _ctx_2048t = jnp.einsum('bsk,bkd->bsd', _ctx_2048c, _ctx_2048P)
        _ctx_2048t = _ctx_2048t * jax.lax.rsqrt(jnp.mean(jnp.square(_ctx_2048t)) + 1e-12) * 0.953939
        ctx_2048 = 4.13588e-05 + 0.999923 * (_ctx_2048t + 0.3 * jax.random.normal(jax.random.fold_in(_rk, 611), (64, 64, 256), jnp.float32))
        return (x, ctx_2048)
    x, ctx_2048 = _rec_inputs()

    def _L0_xattn_setup():
        import jax, jax.numpy as jnp
        import numpy as np
        N_HEAD = 8
        key = jax.random.key(seed)
        k1, k2, k3 = jax.random.split(key, 3)
        B, D, L = (4, 128, 256)
        q = jax.random.normal(k1, (B, D, L), dtype=jnp.float32)
        k = jax.random.normal(k2, (B, D, L), dtype=jnp.float32)
        v = jax.random.normal(k3, (B, D, L), dtype=jnp.float32)
        gamma = jnp.ones((), dtype=jnp.float32)
        return {'q': q, 'k': k, 'v': v, 'gamma': gamma}
    _L0_xattn_all = _L0_xattn_setup()
    _L0_xattn_in = {k: v for k, v in _L0_xattn_all.items() if k in ('gamma',)}
    del _L0_xattn_all

    def _L0_ffn_setup():
        import jax, jax.numpy as jnp
        import numpy as np
        from jax import lax
        TOP_K = 4
        ROUTED_SCALING = 1.0
        RENORMALIZE = True

        def _swiglu_ffn(x, wg, wu, wd):
            return jax.nn.silu(x @ wg.T) * (x @ wu.T) @ wd.T
        key = jax.random.key(seed)
        ks = jax.random.split(key, 9)
        H, I, E = (256, 128, 16)
        s = 0.02
        return {'hidden_states': jax.random.normal(ks[0], (2, 128, H), jnp.float32), 'gate_w': jax.random.normal(ks[1], (E, H), jnp.float32) * s, 'expert_bias': jax.random.normal(ks[2], (E,), jnp.float32) * s, 'w_gate': jax.random.normal(ks[3], (E, I, H), jnp.float32) * s, 'w_up': jax.random.normal(ks[4], (E, I, H), jnp.float32) * s, 'w_down': jax.random.normal(ks[5], (E, H, I), jnp.float32) * s, 'sw_gate': jax.random.normal(ks[6], (I, H), jnp.float32) * s, 'sw_up': jax.random.normal(ks[7], (I, H), jnp.float32) * s, 'sw_down': jax.random.normal(ks[8], (H, I), jnp.float32) * s}
    _L0_ffn_all = _L0_ffn_setup()
    _L0_ffn_in = {k: v for k, v in _L0_ffn_all.items() if k in ('gate_w', 'expert_bias', 'w_gate', 'w_up', 'w_down', 'sw_gate', 'sw_up', 'sw_down')}
    del _L0_ffn_all

    def _L1_xattn_setup():
        import jax, jax.numpy as jnp
        import numpy as np
        NUM_HEADS = 8

        def _proj(W, x):
            return jnp.einsum('oi,bin->bon', W, x)

        def _split_heads(x, h):
            B, D, N = x.shape
            return x.reshape(B, D, h, N // h).transpose(2, 0, 1, 3)

        def _mha(XQ, XK, XV, Wq, Wk, Wv, Wo):
            B, D, N = XQ.shape
            h = NUM_HEADS
            Nh = N // h
            q = _split_heads(_proj(Wq, XQ), h)
            k = _split_heads(_proj(Wk, XK), h)
            v = _split_heads(_proj(Wv, XV), h)
            scores = jnp.einsum('hbdn,hben->hbde', q, k) / jnp.sqrt(jnp.asarray(Nh, q.dtype))
            p = jax.nn.softmax(scores, axis=-1)
            out = jnp.einsum('hbde,hben->hbdn', p, v)
            attn_heads = out.transpose(1, 2, 0, 3).reshape(B, D, N)
            return _proj(Wo, XQ - attn_heads)
        key = jax.random.key(seed)
        ks = jax.random.split(key, 7)
        B, D, N = (16, 64, 256)
        sc = 1.0 / np.sqrt(D)
        return {'X_Query': jax.random.normal(ks[0], (B, D, N), jnp.float32), 'X_Key': jax.random.normal(ks[1], (B, D, N), jnp.float32), 'X_Value': jax.random.normal(ks[2], (B, D, N), jnp.float32), 'W_q': jax.random.normal(ks[3], (D, D), jnp.float32) * sc, 'W_k': jax.random.normal(ks[4], (D, D), jnp.float32) * sc, 'W_v': jax.random.normal(ks[5], (D, D), jnp.float32) * sc, 'W_o': jax.random.normal(ks[6], (D, D), jnp.float32) * sc}
    _L1_xattn_all = _L1_xattn_setup()
    _L1_xattn_in = {k: v for k, v in _L1_xattn_all.items() if k in ('W_q', 'W_k', 'W_v', 'W_o')}
    del _L1_xattn_all

    def _L1_ffn_setup():
        import jax, jax.numpy as jnp
        import numpy as np
        EPS = 1e-05

        def _rmsnorm(x, eps=1e-06):
            return x * jax.lax.rsqrt(jnp.mean(x * x, axis=-1, keepdims=True) + eps)

        def _act_quant(x):
            scale = 127.0 / jnp.clip(jnp.max(jnp.abs(x), axis=-1, keepdims=True), EPS)
            return jnp.clip(jnp.round(x * scale), -128, 127) / scale

        def _weight_quant(w):
            scale = 1.0 / jnp.clip(jnp.mean(jnp.abs(w)), EPS)
            return jnp.clip(jnp.round(w * scale), -1, 1) / scale

        def _ste(a, q):
            return a + jax.lax.stop_gradient(q - a)

        def _bitlinear(x, w):
            xn = _rmsnorm(x)
            xq = _ste(xn, _act_quant(xn))
            wq = _ste(w, _weight_quant(w))
            return jnp.einsum('bsd,hd->bsh', xq, wq)
        key = jax.random.key(seed)
        k_x, k1, k2, k3 = jax.random.split(key, 4)
        B, S, D, H = (4, 512, 256, 704)
        return {'x': jax.random.normal(k_x, (B, S, D), dtype=jnp.float32), 'w1': jax.random.normal(k1, (H, D), dtype=jnp.float32) * 0.02, 'w2': jax.random.normal(k2, (H, D), dtype=jnp.float32) * 0.02, 'w3': jax.random.normal(k3, (D, H), dtype=jnp.float32) * 0.02}
    _L1_ffn_all = _L1_ffn_setup()
    _L1_ffn_in = {k: v for k, v in _L1_ffn_all.items() if k in ('w1', 'w2', 'w3')}
    del _L1_ffn_all
    return {'x': x, 'ctx_2048': ctx_2048, 'L0_xattn_gamma': _L0_xattn_in['gamma'], 'L0_ffn_gate_w': _L0_ffn_in['gate_w'], 'L0_ffn_expert_bias': _L0_ffn_in['expert_bias'], 'L0_ffn_w_gate': _L0_ffn_in['w_gate'], 'L0_ffn_w_up': _L0_ffn_in['w_up'], 'L0_ffn_w_down': _L0_ffn_in['w_down'], 'L0_ffn_sw_gate': _L0_ffn_in['sw_gate'], 'L0_ffn_sw_up': _L0_ffn_in['sw_up'], 'L0_ffn_sw_down': _L0_ffn_in['sw_down'], 'L1_xattn_W_q': _L1_xattn_in['W_q'], 'L1_xattn_W_k': _L1_xattn_in['W_k'], 'L1_xattn_W_v': _L1_xattn_in['W_v'], 'L1_xattn_W_o': _L1_xattn_in['W_o'], 'L1_ffn_w1': _L1_ffn_in['w1'], 'L1_ffn_w2': _L1_ffn_in['w2'], 'L1_ffn_w3': _L1_ffn_in['w3']}

def reference(x, ctx_2048, L0_xattn_gamma, L0_ffn_gate_w, L0_ffn_expert_bias, L0_ffn_w_gate, L0_ffn_w_up, L0_ffn_w_down, L0_ffn_sw_gate, L0_ffn_sw_up, L0_ffn_sw_down, L1_xattn_W_q, L1_xattn_W_k, L1_xattn_W_v, L1_xattn_W_o, L1_ffn_w1, L1_ffn_w2, L1_ffn_w3):
    import jax
    import jax.numpy as jnp

    def _L0_xattn_ref(q, k, v, gamma):
        import jax, jax.numpy as jnp
        import numpy as np
        N_HEAD = 8
        B, Dq, Lq = q.shape
        Dv, Lk = (v.shape[-2], v.shape[-1])
        h = N_HEAD
        dq = Dq // h
        dv = Dv // h
        qh = q.reshape(B, h, dq, Lq)
        kh = k.reshape(B, h, dq, Lk)
        vh = v.reshape(B, h, dv, Lk)
        scale = 1.0 / jnp.sqrt(jnp.asarray(dq, dtype=q.dtype))
        qk = jnp.einsum('bhdq,bhdl->bhql', qh, kh) * scale
        sm = jax.nn.softmax(qk, axis=-1)
        ret = jnp.einsum('bhql,bhdl->bhdq', sm, vh)
        ret = ret.reshape(B, Dv, Lq)
        return gamma * ret

    def _L0_ffn_ref(hidden_states, gate_w, expert_bias, w_gate, w_up, w_down, sw_gate, sw_up, sw_down):
        import jax, jax.numpy as jnp
        import numpy as np
        from jax import lax
        TOP_K = 4
        ROUTED_SCALING = 1.0
        RENORMALIZE = True

        def _swiglu_ffn(x, wg, wu, wd):
            return jax.nn.silu(x @ wg.T) * (x @ wu.T) @ wd.T
        orig_shape = hidden_states.shape
        H = orig_shape[-1]
        x = hidden_states.reshape(-1, H)
        T = x.shape[0]
        logits = x.astype(jnp.float32) @ gate_w.T
        scores = jax.nn.sigmoid(logits)
        _, topk_idx = lax.top_k(scores + expert_bias[None, :], TOP_K)
        topk_w = jnp.take_along_axis(scores, topk_idx, axis=-1)
        if RENORMALIZE:
            topk_w = topk_w / jnp.sum(topk_w, axis=-1, keepdims=True)
        topk_w = topk_w * ROUTED_SCALING
        E = gate_w.shape[0]
        combine = jnp.zeros((T, E), dtype=x.dtype).at[jnp.arange(T)[:, None], topk_idx].set(topk_w.astype(x.dtype))

        def step(acc, ws):
            wg, wu, wd, cw = ws
            return (acc + cw[:, None] * _swiglu_ffn(x, wg, wu, wd), None)
        routed, _ = lax.scan(step, jnp.zeros_like(x), (w_gate, w_up, w_down, combine.T))
        shared = _swiglu_ffn(x, sw_gate, sw_up, sw_down)
        return (routed + shared).reshape(orig_shape)

    def _L1_xattn_ref(X_Query, X_Key, X_Value, W_q, W_k, W_v, W_o):
        import jax, jax.numpy as jnp
        import numpy as np
        NUM_HEADS = 8

        def _proj(W, x):
            return jnp.einsum('oi,bin->bon', W, x)

        def _split_heads(x, h):
            B, D, N = x.shape
            return x.reshape(B, D, h, N // h).transpose(2, 0, 1, 3)

        def _mha(XQ, XK, XV, Wq, Wk, Wv, Wo):
            B, D, N = XQ.shape
            h = NUM_HEADS
            Nh = N // h
            q = _split_heads(_proj(Wq, XQ), h)
            k = _split_heads(_proj(Wk, XK), h)
            v = _split_heads(_proj(Wv, XV), h)
            scores = jnp.einsum('hbdn,hben->hbde', q, k) / jnp.sqrt(jnp.asarray(Nh, q.dtype))
            p = jax.nn.softmax(scores, axis=-1)
            out = jnp.einsum('hbde,hben->hbdn', p, v)
            attn_heads = out.transpose(1, 2, 0, 3).reshape(B, D, N)
            return _proj(Wo, XQ - attn_heads)
        return _mha(X_Query, X_Key, X_Value, W_q, W_k, W_v, W_o)

    def _L1_ffn_ref(x, w1, w2, w3):
        import jax, jax.numpy as jnp
        import numpy as np
        EPS = 1e-05

        def _rmsnorm(x, eps=1e-06):
            return x * jax.lax.rsqrt(jnp.mean(x * x, axis=-1, keepdims=True) + eps)

        def _act_quant(x):
            scale = 127.0 / jnp.clip(jnp.max(jnp.abs(x), axis=-1, keepdims=True), EPS)
            return jnp.clip(jnp.round(x * scale), -128, 127) / scale

        def _weight_quant(w):
            scale = 1.0 / jnp.clip(jnp.mean(jnp.abs(w)), EPS)
            return jnp.clip(jnp.round(w * scale), -1, 1) / scale

        def _ste(a, q):
            return a + jax.lax.stop_gradient(q - a)

        def _bitlinear(x, w):
            xn = _rmsnorm(x)
            xq = _ste(xn, _act_quant(xn))
            wq = _ste(w, _weight_quant(w))
            return jnp.einsum('bsd,hd->bsh', xq, wq)
        gate = jax.nn.silu(_bitlinear(x, w1))
        up = _bitlinear(x, w2)
        return _bitlinear(gate * up, w3)
    x = x + _L0_xattn_ref(_layernorm(x, axis=-1), ctx_2048, ctx_2048, L0_xattn_gamma)
    x = x + _L0_ffn_ref(_layernorm(x, axis=-1), L0_ffn_gate_w, L0_ffn_expert_bias, L0_ffn_w_gate, L0_ffn_w_up, L0_ffn_w_down, L0_ffn_sw_gate, L0_ffn_sw_up, L0_ffn_sw_down)
    x = x + _L1_xattn_ref(_layernorm(x, axis=-1), ctx_2048, ctx_2048, L1_xattn_W_q, L1_xattn_W_k, L1_xattn_W_v, L1_xattn_W_o)
    x = x + _L1_ffn_ref(_layernorm(x, axis=-1), L1_ffn_w1, L1_ffn_w2, L1_ffn_w3)
    return x

_drawn_inputs = setup_inputs


def setup_inputs(seed=0):
    import zlib

    import numpy as np

    out = dict(_drawn_inputs(seed))
    spreads = {}
    factors = {'L0_ffn_gate_w': 8.0,
     'L0_ffn_expert_bias': 8.0,
     'L0_ffn_w_gate': 8.0,
     'L0_ffn_w_up': 8.0,
     'L0_ffn_w_down': 8.0,
     'L0_ffn_sw_gate': 6.035,
     'L0_ffn_sw_up': 5.964,
     'L0_ffn_sw_down': 5.985}
    for name, (base, spread) in spreads.items():
        noise = np.random.default_rng([zlib.crc32(name.encode()), seed]).standard_normal(out[name].shape)
        drawn = base * np.exp(spread * noise) if base else spread * noise
        out[name] = jnp.asarray(drawn.astype(out[name].dtype))
    for name, factor in factors.items():
        out[name] = (out[name] * factor).astype(out[name].dtype)
    return out
```

```python
from contextlib import ExitStack

import concourse.bass as bass
from concourse import mybir

F32 = mybir.dt.float32
F32R = mybir.dt.float32r
BF16 = mybir.dt.bfloat16
ALU = mybir.AluOpType
ACT = mybir.ActivationFunctionType
AX = mybir.AxisListType

P = 128
MAGIC = 1.5 * 2.0**23
LN_EPS = 1e-5
RMS_EPS = 1e-6
QUANT_EPS = 1e-5
TOP_K = 4


class Signal:

    def __init__(self, sem, per, unit=1):
        self.sem, self.per, self.unit = sem, per, unit

    def at(self, q, k=0):
        return (q * self.per + (k + 1)) * self.unit


class Steps:

    def __init__(self, eng, chain, q):
        self.eng, self.chain, self.q, self.k = eng, chain, q, 0

    def done(self, ins):
        ins.then_inc(self.chain.sem, 1)
        self.eng.wait_ge(self.chain.sem, self.chain.at(self.q, self.k))
        self.k += 1

    def end(self):
        assert self.k == self.chain.per, (self.k, self.chain.per)


def first(q):
    return isinstance(q, int) and q == 0


def body_plan():
    plan = [("R", 0), ("A", 0), ("R", 1), ("R", 2), ("R", 3)]
    slot = 0
    for n in range(17):
        plan.append(("E", n))
        plan.append(("H", slot))
        slot += 1
    plan.append(("T", 0))
    rest = [("C", 0, 0), ("C", 0, 1), ("C", 0, 2), ("C", 1, 0), ("C", 1, 1), ("C", 1, 2),
            ("D", 0, 0), ("D", 0, 1), ("D", 0, 2), ("D", 1, 0), ("D", 1, 1), ("D", 1, 2)]
    for n, item in enumerate(rest):
        plan.append(item)
        if slot < 26:
            plan.append(("H", slot))
            slot += 1
    assert slot == 26
    return plan


def program(nc, x, ctx, gamma, gate_w, bias, w_gu, w_d, wq, wk, wv, wo, w1, w2, w3, out):
    B, D, L = x.shape
    QB = 4
    NQ = B // QB
    T = 2
    H0 = 8
    DH = D // H0
    NE = gate_w.shape[2]
    NX = NE + 1
    HID = w1.shape[2]
    HC = HID // 2
    HK = (HID + P - 1) // P
    HR = HID - (HK - 1) * P
    NH1 = 8
    NW = L // NH1
    assert T * P == QB * D and L == 2 * P and P == 2 * D and DH == 8

    x_q = x.rearrange("(q t b) d l -> q (b d) t l", t=T, b=2)
    c_q = ctx.rearrange("(q t b) d l -> q (b d) t l", t=T, b=2)
    o_q = out.rearrange("(q t b) d l -> q (b d) t l", t=T, b=2)

    rows = nc.dram_tensor("rows", (2, 16, 3, DH, T * L), F32).ap()

    with ExitStack() as stack:
        def sb(name, shape, dt=F32):
            return stack.enter_context(nc.sbuf_tensor(name, shape, dt))

        def sig(name, per=1, unit=1):
            return Signal(stack.enter_context(nc.semaphore(name)), per, unit)

        wgu_h = sb("wgu_h", [P, NX, 2, 2, P], F32R)
        wgu_l = sb("wgu_l", [P, NX, 2, 2, P], F32R)
        wd = sb("wd", [P, NX, L])
        gw = sb("gw", [P, 2, NE])
        gw_h = sb("gw_h", [P, 2, NE], F32R)
        gw_l = sb("gw_l", [P, 2, NE], F32R)
        bias_b = sb("bias_b", [P, NE])
        gamma_b = sb("gamma_b", [P, 1])
        proj = sb("proj", [P, 4, P])
        w1q = sb("w1q", [P, 2, HID], BF16)
        w2q = sb("w2q", [P, 2, HID], BF16)
        w3q = sb("w3q", [P, HK, L], BF16)
        w3tail = sb("w3tail", [P, L])
        wabs = sb("wabs", [P, 4])
        wmean = sb("wmean", [P, 4])
        wscale = sb("wscale", [P, 4])
        ident = sb("ident", [P, P])
        ident_bf = sb("ident_bf", [P, P], BF16)
        ones = sb("ones", [P, P])
        ones_pad = sb("ones_pad", [P, 4, 32])
        lower = sb("lower", [P, NE, NE])
        pick = sb("pick", [2 * NE, NE, P], F32R)
        mhalf = sb("mhalf", [P, T])
        spare = sb("spare", [P, 1])

        xin = sb("xin", [P, T, L])
        ctxa = sb("ctxa", [P, T, L])
        xres = sb("xres", [P, T, L])
        a_st = sb("a_st", [P, T, 6])
        a_mv = sb("a_mv", [P, T, 2])
        a_ve = sb("a_ve", [P, T])
        a_rstd = sb("a_rstd", [P, T])
        qaug = sb("qaug", [P, 4, T, L], F32R)
        kaug = sb("kaug", [P, 4, T, L], F32R)
        vpad = sb("vpad", [P, T * 2, 4 * 136])
        mneg = sb("mneg", [P, T, 2, 16])
        mhl = sb("mhl", [P, T, 2, 2, 16])
        mT = sb("mT", [32, T, L])
        E = [sb(f"E{i}", [P, 4, 2, L]) for i in range(2)]
        rden = sb("rden", [P, L])
        attn = sb("attn", [P, L])
        x1 = sb("x1", [P, T, L])
        x1b = sb("x1b", [P, T, L])
        b_st = sb("b_st", [P, T, 6])
        b_mv = sb("b_mv", [P, T, 2])
        b_ve = sb("b_ve", [P, T])
        b_rstd = sb("b_rstd", [P, T])
        y = sb("y", [P, T, L])
        yT_h = sb("yT_h", [P, 2, T * P], F32R)
        yT_l = sb("yT_l", [P, 2, T * P], F32R)
        sc_e = sb("sc_e", [P, T, NE])
        score = sb("score", [P, T, NE])
        sel = sb("sel", [P, T, NE])
        rank = sb("rank", [P, T, NE])
        cw = sb("cw", [P, T, NE])
        csum = sb("csum", [P, T])
        crec = sb("crec", [P, T])
        cwhl = sb("cwhl", [P, T, 2, NE])
        cwT = sb("cwT", [2 * NE, T * P], F32R)
        cwb = sb("cwb", [P, NE, T * P])
        th_all = sb("th_all", [P, 2 * L])
        g1_all = sb("g1_all", [P, 2 * L])
        th, g1 = ([a[:, i * L:(i + 1) * L] for i in range(2)] for a in (th_all, g1_all))
        th2, hg = th_all[:, 0:HC], g1_all[:, 0:HC]
        g2 = [sb(f"g2_{i}", [P, L]) for i in range(2)]
        h = [sb(f"h{i}", [P, L]) for i in range(3)]
        ctxb = sb("ctxb", [P, T, L])
        x2 = sb("x2", [P, T, L])
        c_st = sb("c_st", [P, T, 6])
        c_mv = sb("c_mv", [P, T, 2])
        c_ve = sb("c_ve", [P, T])
        c_rstd = sb("c_rstd", [P, T])
        z = sb("z", [P, T, L])
        qT = sb("qT", [P, 2 * P])
        kmask = sb("kmask", [P, 2, 4, P])
        v1 = sb("v1", [P, L])
        smx = sb("smx", [P, NH1])
        ppad = sb("ppad", [P, NH1, 2, D])
        ssum = sb("ssum", [P, NH1])
        srec = sb("srec", [P, NH1])
        u = sb("u", [P, L])
        x3 = sb("x3", [P, T, L])
        d_st = sb("d_st", [P, T, 6])
        d_mv = sb("d_mv", [P, T, 2])
        d_ve = sb("d_ve", [P, T])
        d_rstd = sb("d_rstd", [P, T])
        rs = sb("rs", [P, 2, T, 8])
        qb = sb("qb", [P, L], BF16)
        qbT = sb("qbT", [P, 2, P], BF16)
        hb = sb("hb", [P, HID], BF16)
        hbT = sb("hbT", [P, HK, P], BF16)
        xo = sb("xo", [P, T, L])

        S1 = stack.enter_context(nc.psum_tensor("S1", [P, 2, 512], F32))
        S2 = stack.enter_context(nc.psum_tensor("S2", [P, 2, 512], F32))
        OD = stack.enter_context(nc.psum_tensor("OD", [P, 512], F32))
        GU = [stack.enter_context(nc.psum_tensor(f"GU{i}", [P, 512], F32)) for i in range(2)]
        Y = stack.enter_context(nc.psum_tensor("Y", [P, 512], F32))

        const_in = sig("const_in", 1, 16)
        l1w_in = sig("l1w_in", 1, 16)
        gu_in = [sig(f"gu_in{i}", 1, 16) for i in range(2)]
        wd_in = sig("wd_in", 1, 16)
        zeroed = sig("zeroed")
        ident_ok = sig("ident_ok")
        pool_setup = sig("pool_setup", 12)
        setup_steps = sig("setup_steps", 64)
        wsum_ready = sig("wsum_ready")
        wsum_done = sig("wsum_done")
        split_h = sig("split_h", 8)
        split_l = sig("split_l", 8)
        dve_const = sig("dve_const", 1)
        xin_in = sig("xin_in", 1, 16)
        ctxa_in = sig("ctxa_in", 1, 16)
        xres_in = sig("xres_in", 1, 16)
        ctxb_in = sig("ctxb_in", 1, 16)
        rows_out = sig("rows_out", 6, 16)
        aug_in = sig("aug_in", 8, 16)
        max_in = sig("max_in", 4, 16)
        out_sent = sig("out_sent", 1, 16)
        a_steps = sig("a_steps", 2)
        a_var = sig("a_var")
        a_rs = sig("a_rs")
        xn_ready = sig("xn_ready")
        xh_ready = sig("xh_ready")
        ch_ready = sig("ch_ready")
        xl_ready = sig("xl_ready")
        cl_ready = sig("cl_ready")
        vt_ready = sig("vt_ready")
        vpad_ready = sig("vpad_ready")
        s1_ready = sig("s1_ready", 16)
        s1_read = sig("s1_read", 16)
        max_steps = sig("max_steps", 2)
        mhl_ready = sig("mhl_ready", 2)
        mt_ready = sig("mt_ready", 2)
        mt_copied = sig("mt_copied", 2)
        s2_ready = sig("s2_ready", 16)
        exp_ready = sig("exp_ready", 16)
        pv_done = sig("pv_done", 8)
        fin_steps = sig("fin_steps", 4)
        x1_ready = sig("x1_ready", 2)
        x1b_ready = sig("x1b_ready")
        b_steps = sig("b_steps", 2)
        b_var = sig("b_var")
        b_rs = sig("b_rs")
        y_ready = sig("y_ready")
        yt_ready = sig("yt_ready")
        yth_ready = sig("yth_ready")
        ytl_ready = sig("ytl_ready")
        logits_ready = sig("logits_ready")
        e_ready = sig("e_ready")
        route_steps = sig("route_steps", 13)
        cwhl_ready = sig("cwhl_ready")
        cwt_ready = sig("cwt_ready")
        cwt_copied = sig("cwt_copied")
        bc_ready = sig("bc_ready", 8)
        bc_copied = sig("bc_copied", 8)
        gu_ready = sig("gu_ready", NX)
        th_ready = sig("th_ready", NX)
        g1_ready = sig("g1_ready", NX)
        g2_ready = sig("g2_ready", NX - 1)
        h_ready = sig("h_ready", NX)
        down_done = sig("down_done", NX)
        x2_ready = sig("x2_ready")
        c_steps = sig("c_steps", 2)
        c_var = sig("c_var")
        c_rs = sig("c_rs")
        z_ready = sig("z_ready")
        qv_ready = sig("qv_ready", 2)
        k_ready = sig("k_ready", 2)
        qt_copied = sig("qt_copied", 2)
        k_copied = sig("k_copied", 2)
        v_copied = sig("v_copied", 2)
        sc_ready = sig("sc_ready", 2)
        smax_steps = sig("smax_steps", 2)
        ssub_ready = sig("ssub_ready", 2)
        p_ready = sig("p_ready", 2)
        srec_steps = sig("srec_steps", 4)
        pt_ready = sig("pt_ready", 2)
        pt_copied0 = sig("pt_copied0", 2)
        pt_copied1 = sig("pt_copied1", 2)
        av_ready = sig("av_ready", 2)
        av_steps = sig("av_steps", 2)
        u_ready = sig("u_ready", 2)
        o_ready = sig("o_ready", 2)
        x3_ready = sig("x3_ready", 2)
        d_steps = sig("d_steps", 4)
        d_var = sig("d_var", 2)
        d_rs = sig("d_rs", 2)
        w_ready = sig("w_ready", 2)
        ss_ready = sig("ss_ready", 4)
        ms_ready = sig("ms_ready", 4)
        rms_ready = sig("rms_ready", 4)
        q1_steps = sig("q1_steps", 16)
        q2_steps = sig("q2_steps", 12)
        qb_ready = sig("qb_ready", 2)
        qt_ready = sig("qt_ready", 2)
        qbt_copied = sig("qbt_copied", 2)
        hid_ready = sig("hid_ready", 4)
        up_ready = sig("up_ready", 4)
        th2_ready = sig("th2_ready", 4)
        hg_ready = sig("hg_ready", 4)
        hc_ready = sig("hc_ready", 4)
        hb_ready = sig("hb_ready", 2)
        hbt_ready = sig("hbt_ready", 2)
        hbt_copied = sig("hbt_copied", 2)
        dn_ready = sig("dn_ready", 2)
        xo_ready = sig("xo_ready", 2)

        after = cwb[:, :, :].rearrange("p a b -> p (a b)")
        ends = [0, NH1 * P, NH1 * P + NH1 * D, NH1 * P + NH1 * D + HID, NH1 * P + NH1 * D + 2 * HID,
                NH1 * P + NH1 * D + 3 * HID]
        pT = after[:, ends[0]:ends[1]].rearrange("p (h d) -> p h d", h=NH1)
        ssub = after[:, ends[1]:ends[2]].rearrange("p (h e) -> p h e", h=NH1)
        junk, qv, hid = (after[:, ends[i]:ends[i + 1]] for i in (2, 3, 4))
        av = after[:, ends[5]:ends[5] + L]
        w = y
        cmp_gt, cmp_eq = (after[:, i * T * NE * NE:(i + 1) * T * NE * NE]
                          .rearrange("p (t i j) -> p t i j", t=T, i=NE) for i in range(2))
        E0, E1 = (e[:, :, :, :].rearrange("p a b c -> p (a b c)") for e in E)
        xh, xl, ch, cl = (E0[:, i * T * L:(i + 1) * T * L].rearrange("p (t l) -> p t l", t=T).bitcast(F32R)
                          for i in range(4))
        xn = E1[:, 0:T * L].rearrange("p (t l) -> p t l", t=T)
        stage = [e[:, :, :, :].rearrange("p a b c -> p (a b c)") for e in E]
        w1s = cwb[:, :, :].rearrange("p a b -> p (a b)")[:, 0:2 * HID]
        w2s = cwb[:, :, :].rearrange("p a b -> p (a b)")[:, 2 * HID:4 * HID]
        w3s = cwb[:, :, :].rearrange("p a b -> p (a b)")[:, 4 * HID:4 * HID + (HK - 1) * L]
        GUW = 4 * P
        chunks = [(c, min(4, NX - c)) for c in range(0, NX, 4)]
        S1a = S1[:, 0, :]

        def vdiag(tl):
            v = vpad[:, tl, :].rearrange("p (s k) -> p s k", s=4)[:, :, 0:P]
            return v.rearrange("p s (g k) -> p s g k", g=4)[:, :, :, 0:DH]

        plan = body_plan()

        def run(eng, handlers, heads=None):
            def body(q, nxt):
                for item in plan:
                    if item[0] in ("A", "H"):
                        if nxt is not None and item[0] in handlers:
                            handlers[item[0]](nxt, *item[1:])
                    elif item[0] in handlers:
                        handlers[item[0]](q, *item[1:])
            for item in plan:
                if item[0] in ("A", "H") and item[0] in handlers:
                    handlers[item[0]](0, *item[1:])
            body(0, 1 if NQ > 1 else None)
            if NQ > 2:
                with eng.Fori(1, NQ - 1) as i:
                    body(i, i + 1)
            if NQ > 1:
                body(NQ - 1, None)

        block = stack.enter_context(nc.Block())

        @block.sync
        def _(sp):
            sp.dma_start(xin[:, :, :], x_q[0]).then_inc(xin_in.sem, 16)
            sp.dma_start(ctxa[:, :, :], c_q[0]).then_inc(ctxa_in.sem, 16)
            sp.dma_start(gw[:, :, :], gate_w).then_inc(const_in.sem, 16)
            sp.dma_start(bias_b[:, :], bias.partition_broadcast(P)).then_inc(const_in.sem, 16)
            sp.dma_start(gamma_b[:, :], gamma.partition_broadcast(P)).then_inc(const_in.sem, 16)
            sp.wait_ge(zeroed.sem, 1)
            for n, wt in enumerate((wq, wk, wv, wo)):
                for b in range(2):
                    sp.dma_start(proj[64 * b:64 * b + 64, n, 64 * b:64 * b + 64], wt).then_inc(const_in.sem, 16)
            for c, (e0, ne) in enumerate(chunks):
                if c >= 2:
                    sp.wait_ge(split_l.sem, c)
                sp.dma_start(stage[c % 2][:, 0:ne * GUW], w_gu[:, e0 * GUW:(e0 + ne) * GUW]).then_inc(gu_in[c % 2].sem, 16)
                if c == 0:
                    sp.dma_start(w1s, w1.rearrange("p c n -> p (c n)")).then_inc(l1w_in.sem, 16)
                    sp.dma_start(w2s, w2.rearrange("p c n -> p (c n)")).then_inc(l1w_in.sem, 16)
                    sp.dma_start(w3s.rearrange("p (c n) -> p c n", n=L),
                                 w3[0:(HK - 1) * P, :].rearrange("(c p) n -> p c n", p=P)).then_inc(l1w_in.sem, 16)
                    sp.dma_start(w3tail[0:HR, :], w3[(HK - 1) * P:HID, :]).then_inc(l1w_in.sem, 16)
            sp.dma_start(wd[:, :, :], w_d).then_inc(wd_in.sem, 16)

            def attention_inputs(q, _=0):
                if not first(q):
                    sp.wait_ge(xn_ready.sem, xn_ready.at(q - 1))
                    sp.dma_start(xin[:, :, :], x_q[bass.ds(q, 1)].rearrange("a p t l -> (a p) t l")
                                 if not isinstance(q, int) else x_q[q]).then_inc(xin_in.sem, 16)
                    sp.wait_ge(vt_ready.sem, vt_ready.at(q - 1))
                    sp.wait_ge(ch_ready.sem, ch_ready.at(q - 1))
                    sp.wait_ge(cl_ready.sem, cl_ready.at(q - 1))
                    sp.dma_start(ctxa[:, :, :], c_q[bass.ds(q, 1)].rearrange("a p t l -> (a p) t l")
                                 if not isinstance(q, int) else c_q[q]).then_inc(ctxa_in.sem, 16)
                    sp.wait_ge(s2_ready.sem, s2_ready.at(q - 1, 15))
                    sp.wait_ge(x1_ready.sem, x1_ready.at(q - 1, 1))
                else:
                    sp.wait_ge(zeroed.sem, 2)
                sp.dma_start(xres[:, :, :], x_q[bass.ds(q, 1)].rearrange("a p t l -> (a p) t l")
                             if not isinstance(q, int) else x_q[q]).then_inc(xres_in.sem, 16)
                for src, ready, side, parts in ((xh, xh_ready, 0, (0, 2)), (ch, ch_ready, 1, (0, 1)),
                                                (cl, cl_ready, 1, (2,)), (xl, xl_ready, 0, (1,))):
                    sp.wait_ge(ready.sem, ready.at(q))
                    for part in parts:
                        sp.dma_start(rows[side, :, part, :, :],
                                     src[:, :, :].rearrange("p t l -> p (t l)").bitcast(F32))\
                          .then_inc(rows_out.sem, 16)
                sp.wait_ge(rows_out.sem, rows_out.at(q, 5))
                for dst, side in ((qaug, 0), (kaug, 1)):
                    for g in range(4):
                        sp.dma_start(dst[32 * g:32 * g + 24, :, :, :].rearrange("r s t l -> r s (t l)").bitcast(F32),
                                     rows[side, 4 * g:4 * g + 4].rearrange("s c r l -> (c r) s l"))\
                          .then_inc(aug_in.sem, 16)

            def head_slot(q, k):
                if k in (8, 16):
                    t = k // 8 - 1
                    sp.wait_ge(mt_copied.sem, mt_copied.at(q, t))
                    for part in range(2):
                        sp.dma_start(qaug[24 + part:P:32, :, t, :].bitcast(F32),
                                     mT[16 * part:16 * part + 16, t, :])\
                          .then_inc(max_in.sem, 16)

            def second_inputs(q, k):
                if k == 0:
                    if not first(q):
                        sp.wait_ge(k_ready.sem, k_ready.at(q - 1, 1))
                    sp.dma_start(ctxb[:, :, :], c_q[bass.ds(q, 1)].rearrange("a p t l -> (a p) t l")
                                 if not isinstance(q, int) else c_q[q]).then_inc(ctxb_in.sem, 16)

            def last_block(q, t, k):
                if t == 1 and k == 2:
                    sp.wait_ge(xo_ready.sem, xo_ready.at(q, 1))
                    sp.dma_start(o_q[bass.ds(q, 1)].rearrange("a p t l -> (a p) t l")
                                 if not isinstance(q, int) else o_q[q], xo[:, :, :]).then_inc(out_sent.sem, 16)

            run(sp, {"A": attention_inputs, "H": head_slot, "R": second_inputs, "D": last_block})
            sp.wait_ge(out_sent.sem, 16 * NQ)

        @block.gpsimd
        def _(pool):
            n = 0

            def setup(ins):
                nonlocal n
                n += 1
                ins.then_inc(pool_setup.sem, 1)

            def settle():
                pool.wait_ge(pool_setup.sem, n)

            pool.memset(proj[:, :, :], 0.0).then_inc(zeroed.sem, 1)
            setup(pool.memset(ident[:, :], 0.0))
            settle()
            setup(pool.affine_select(out=ident[:, :], in_=ident[:, :], compare_op=ALU.not_equal, fill=1.0,
                                     base=0, pattern=[[-1, P]], channel_multiplier=1))
            setup(pool.memset(mhalf[:, :], -0.5))
            setup(pool.memset(ones[:, :], 1.0))
            setup(pool.memset(lower[:, :, :], 1.0))
            settle()
            pool.affine_select(out=lower[:, :, :], in_=lower[:, :, :], compare_op=ALU.is_gt, fill=0.0,
                               base=0, pattern=[[1, NE], [-1, NE]], channel_multiplier=0)\
                .then_inc(ident_ok.sem, 1)
            pool.wait_ge(ident_ok.sem, 1)
            pool.memset(kaug[:, :, :, :].bitcast(F32), 1.0).then_inc(zeroed.sem, 1)

            def attention_norm(q, _=0):
                pool.wait_ge(a_var.sem, a_var.at(q))
                pool.tensor_tensor(a_rstd[:, :], a_ve[:, :], mhalf[:, :], ALU.pow).then_inc(a_rs.sem, 1)

            def router(q, k):
                if k == 0:
                    pool.wait_ge(b_var.sem, b_var.at(q))
                    pool.tensor_tensor(b_rstd[:, :], b_ve[:, :], mhalf[:, :], ALU.pow).then_inc(b_rs.sem, 1)

            def expert(q, n):
                if n >= 1:
                    if n >= 3:
                        pool.wait_ge(h_ready.sem, h_ready.at(q, n - 2))
                    if n == 1:
                        pool.wait_ge(bc_copied.sem, bc_copied.at(q, 7))
                    pool.wait_ge(g1_ready.sem, g1_ready.at(q, n))
                    pool.tensor_tensor(g2[n % 2][:, :], g1[n % 2][:, :], cwb[:, n - 1, :], ALU.mult)\
                        .then_inc(g2_ready.sem, 1)

            def second(q, t, k):
                if t == 0 and k == 0:
                    pool.wait_ge(c_var.sem, c_var.at(q))
                    pool.tensor_tensor(c_rstd[:, :], c_ve[:, :], mhalf[:, :], ALU.pow).then_inc(c_rs.sem, 1)

            def rms(q, which, t):
                s = 2 * t + which
                pool.wait_ge(ms_ready.sem, ms_ready.at(q, s))
                pool.tensor_tensor(rs[:, which, t, 2:3], rs[:, which, t, 1:2], mhalf[:, 0:1], ALU.pow)\
                    .then_inc(rms_ready.sem, 1)

            def last_block(q, t, k):
                if k == 0:
                    pool.wait_ge(d_var.sem, d_var.at(q, t))
                    pool.tensor_tensor(d_rstd[:, t:t + 1], d_ve[:, t:t + 1], mhalf[:, 0:1], ALU.pow)\
                        .then_inc(d_rs.sem, 1)
                    rms(q, 0, t)
                if k == 2:
                    rms(q, 1, t)

            run(pool, {"A": attention_norm, "R": router, "E": expert, "C": second, "D": last_block})

        @block.scalar
        def _(act):
            act.wait_ge(const_in.sem, 16 * 11)
            act.copy(gw_h[:, :, :], gw[:, :, :]).then_inc(split_h.sem, 1)
            for c, (e0, ne) in enumerate(chunks):
                act.wait_ge(gu_in[c % 2].sem, 16 * (c // 2 + 1))
                act.copy(wgu_h[:, e0:e0 + ne, :, :, :].rearrange("p a b c d -> p (a b c d)"),
                         stage[c % 2][:, 0:ne * GUW]).then_inc(split_h.sem, 1)

            def attention_inputs(q, _=0):
                if not first(q):
                    act.wait_ge(aug_in.sem, aug_in.at(q - 1, 7))
                act.wait_ge(xn_ready.sem, xn_ready.at(q))
                act.copy(xh[:, :, :], xn[:, :, :]).then_inc(xh_ready.sem, 1)
                act.wait_ge(ctxa_in.sem, ctxa_in.at(q))
                act.copy(ch[:, :, :], ctxa[:, :, :]).then_inc(ch_ready.sem, 1)
                act.wait_ge(vt_ready.sem, vt_ready.at(q))
                if first(q):
                    act.wait_ge(dve_const.sem, 1)
                else:
                    act.wait_ge(pv_done.sem, pv_done.at(q - 1, 7))
                for tl in range(4):
                    ins = act.copy(vdiag(tl), S1a[:, tl * P:(tl + 1) * P].rearrange("p (g s r) -> p s g r", g=4, s=4))
                ins.then_inc(vpad_ready.sem, 1)

            def head_slot(q, k):
                if k >= 9 and k - 9 < 16:
                    step = k - 9
                    m = step // 2
                    act.wait_ge(s2_ready.sem, s2_ready.at(q, step))
                    if m >= 2:
                        act.wait_ge(pv_done.sem, pv_done.at(q, m - 2))
                    elif first(q):
                        act.wait_ge(split_l.sem, 1 + len(chunks))
                    else:
                        act.wait_ge(pv_done.sem, pv_done.at(q - 1, m + 6))
                    u0 = 2 * (step % 2)
                    act.activation(E[m % 2][:, u0:u0 + 2, :, :].rearrange("p a b c -> p a (b c)"), S2[:, :, :],
                                   ACT.Exp, scale=float(DH) ** -0.5).then_inc(exp_ready.sem, 1)

            def router(q, k):
                if k == 0:
                    act.wait_ge(x1_ready.sem, x1_ready.at(q, 1))
                    if not first(q):
                        act.wait_ge(x2_ready.sem, x2_ready.at(q - 1))
                    act.copy(x1b[:, :, :], x1[:, :, :]).then_inc(x1b_ready.sem, 1)
                    act.wait_ge(yt_ready.sem, yt_ready.at(q))
                    act.copy(yT_h[:, :, :].rearrange("p a b -> p (a b)"), GU[0][:, :]).then_inc(yth_ready.sem, 1)
                if k == 1:
                    act.wait_ge(logits_ready.sem, logits_ready.at(q))
                    act.activation(sc_e[:, :, :].rearrange("p a b -> p (a b)"), GU[1][:, 0:T * NE], ACT.Exp,
                                   scale=-1.0).then_inc(e_ready.sem, 1)
                if k == 3:
                    for r in range(8):
                        act.wait_ge(bc_ready.sem, bc_ready.at(q, r))
                        act.copy(cwb[:, 2 * r:2 * r + 2, :].rearrange("p a b -> p (a b)"), GU[r % 2][:, :])\
                           .then_inc(bc_copied.sem, 1)

            def expert(q, n):
                act.wait_ge(gu_ready.sem, gu_ready.at(q, n))
                if n >= 2:
                    act.wait_ge(g1_ready.sem, g1_ready.at(q, n - 2))
                elif not first(q):
                    act.wait_ge(g1_ready.sem, g1_ready.at(q - 1, NX - 1))
                act.activation(th[n % 2][:, :], GU[n % 2][:, 0:L], ACT.Tanh, scale=0.5).then_inc(th_ready.sem, 1)

            def second(q, t, k):
                if k == 0:
                    act.wait_ge(qv_ready.sem, qv_ready.at(q, t))
                    act.copy(qT[:, :], GU[0][:, 0:2 * P]).then_inc(qt_copied.sem, 1)
                    act.copy(v1[:, :], GU[0][:, L:2 * L]).then_inc(v_copied.sem, 1)
                if k == 1:
                    act.wait_ge(ssub_ready.sem, ssub_ready.at(q, t))
                    for b in range(2):
                        r = slice(64 * b, 64 * b + 64)
                        ins = act.activation(ppad[r, :, b, :], ssub[r, :, :], ACT.Exp, scale=float(NW) ** -0.5)
                    ins.then_inc(p_ready.sem, 1)
                if k == 2:
                    act.wait_ge(pt_ready.sem, pt_ready.at(q, t))
                    act.copy(pT[:, 0:4, :].rearrange("p a b -> p (a b)"), GU[0][:, :]).then_inc(pt_copied0.sem, 1)

            def last_block(q, t, k):
                if k == 0:
                    act.wait_ge(w_ready.sem, w_ready.at(q, t))
                    act.activation(junk[:, 0:L], w[:, t, :], ACT.Square, accum_out=rs[:, 0, t, 0:1])\
                       .then_inc(ss_ready.sem, 1)
                if k == 1:
                    for c in range(2):
                        act.wait_ge(hid_ready.sem, hid_ready.at(q, 2 * t + c))
                        gate = (GU[1], GU[0])[c]
                        act.activation(th2[:, :], gate[:, 0:HC], ACT.Tanh, scale=rs[:, 0, t, 6:7])\
                           .then_inc(th2_ready.sem, 1)
                        act.wait_ge(hg_ready.sem, hg_ready.at(q, 2 * t + c))
                if k == 2:
                    act.wait_ge(hc_ready.sem, hc_ready.at(q, 2 * t + 1))
                    act.activation(junk[:, :], hid[:, :], ACT.Square, accum_out=rs[:, 1, t, 0:1])\
                       .then_inc(ss_ready.sem, 1)

            run(act, {"A": attention_inputs, "H": head_slot, "R": router, "E": expert, "C": second,
                      "D": last_block})

        @block.vector
        def _(dve):
            step = Steps(dve, setup_steps, 0)
            dve.memset(vpad[:, :, :], 0.0)
            dve.memset(kmask[:, :, :, :], 0.0)
            dve.memset(ppad[:, :, :, :], 0.0)
            step.done(dve.memset(ones_pad[:, :, :], 0.0))
            for s in range(4):
                dve.memset(ones_pad[:, s, DH * s:DH * s + DH], 1.0)
            dve.memset(w3tail[HR:P, :], 0.0)
            dve.memset(wabs[:, :], 0.0).then_inc(dve_const.sem, 1)

            def attention_inputs(q, _=0):
                s = Steps(dve, a_steps, q)
                dve.wait_ge(xin_in.sem, xin_in.at(q))
                dve.bn_stats(a_st[:, 0, :], xin[:, 0, :])
                s.done(dve.bn_stats(a_st[:, 1, :], xin[:, 1, :]))
                dve.memset(spare[:, :], 0.0)
                dve.bn_aggr(a_mv[:, 0, :], a_st[:, 0, :])
                s.done(dve.bn_aggr(a_mv[:, 1, :], a_st[:, 1, :]))
                dve.tensor_scalar(a_ve[:, :], a_mv[:, :, 1], LN_EPS, None, ALU.add).then_inc(a_var.sem, 1)
                dve.wait_ge(a_rs.sem, a_rs.at(q))
                if not first(q):
                    dve.wait_ge(xh_ready.sem, xh_ready.at(q - 1))
                for t in range(T):
                    ins = dve.tensor_scalar(xn[:, t, :], xin[:, t, :], a_mv[:, t, 0:1], a_rstd[:, t:t + 1],
                                            ALU.subtract, ALU.mult)
                ins.then_inc(xn_ready.sem, 1)
                if not first(q):
                    dve.wait_ge(aug_in.sem, aug_in.at(q - 1, 7))
                dve.wait_ge(ch_ready.sem, ch_ready.at(q))
                dve.tensor_tensor(cl[:, :, :], ctxa[:, :, :], ch[:, :, :].bitcast(F32), ALU.subtract)\
                   .then_inc(cl_ready.sem, 1)
                dve.wait_ge(xn_ready.sem, xn_ready.at(q))
                dve.wait_ge(xh_ready.sem, xh_ready.at(q))
                dve.tensor_tensor(xl[:, :, :], xn[:, :, :], xh[:, :, :].bitcast(F32), ALU.subtract)\
                   .then_inc(xl_ready.sem, 1)
                s.end()

            def head_slot(q, k):
                if k in (8, 16):
                    t = k // 8 - 1
                    dve.wait_ge(mt_ready.sem, mt_ready.at(q, t))
                    if not first(q):
                        dve.wait_ge(max_in.sem, max_in.at(q - 1, 3))
                    dve.tensor_copy(mT[:, t, :], S1[0:32, 0, 0:L]).then_inc(mt_copied.sem, 1)
                if k < 16:
                    t, s, g0 = k // 8, k // 2 % 4, 2 * (k % 2)
                    dve.wait_ge(s1_ready.sem, s1_ready.at(q, k))
                    dst = mneg[:, t, :, :].rearrange("p c (g s) -> p g c s", g=4)[:, g0:g0 + 2, :, s]
                    dve.tensor_reduce(dst, S1[:, :, :].rearrange("p v (c l) -> p v c l", c=2), AX.X, ALU.max,
                                      negate=True).then_inc(s1_read.sem, 1)
                if k in (7, 15):
                    t = k // 8
                    dve.wait_ge(s1_read.sem, s1_read.at(q, k))
                    dve.tensor_copy(mhl[:, t, :, 0, :].bitcast(F32R), mneg[:, t, :, :]).then_inc(max_steps.sem, 1)
                    dve.wait_ge(max_steps.sem, max_steps.at(q, t))
                    dve.tensor_tensor(mhl[:, t, :, 1, :].bitcast(F32R), mneg[:, t, :, :], mhl[:, t, :, 0, :],
                                      ALU.subtract).then_inc(mhl_ready.sem, 1)
                if k in (18, 25):
                    t = 0 if k == 18 else 1
                    if t == 0:
                        dve.wait_ge(xres_in.sem, xres_in.at(q))
                        if not first(q):
                            dve.wait_ge(x1b_ready.sem, x1b_ready.at(q - 1))
                    dve.wait_ge(pv_done.sem, pv_done.at(q, 4 * t + 3))
                    dve.reciprocal(rden[:, :], OD[:, L:2 * L]).then_inc(fin_steps.sem, 1)
                    dve.wait_ge(fin_steps.sem, fin_steps.at(q, 2 * t))
                    dve.tensor_tensor(attn[:, :], rden[:, :], OD[:, 0:L], ALU.mult).then_inc(fin_steps.sem, 1)
                    dve.wait_ge(fin_steps.sem, fin_steps.at(q, 2 * t + 1))
                    dve.scalar_tensor_tensor(x1[:, t, :], attn[:, :], gamma_b[:, 0:1], xres[:, t, :], ALU.mult,
                                             ALU.add).then_inc(x1_ready.sem, 1)

            def router(q, k):
                if k == 0:
                    dve.wait_ge(x1_ready.sem, x1_ready.at(q, 1))
                    s = Steps(dve, b_steps, q)
                    dve.bn_stats(b_st[:, 0, :], x1[:, 0, :])
                    s.done(dve.bn_stats(b_st[:, 1, :], x1[:, 1, :]))
                    dve.memset(spare[:, :], 0.0)
                    dve.bn_aggr(b_mv[:, 0, :], b_st[:, 0, :])
                    s.done(dve.bn_aggr(b_mv[:, 1, :], b_st[:, 1, :]))
                    dve.tensor_scalar(b_ve[:, :], b_mv[:, :, 1], LN_EPS, None, ALU.add).then_inc(b_var.sem, 1)
                    dve.wait_ge(b_rs.sem, b_rs.at(q))
                    for t in range(T):
                        ins = dve.tensor_scalar(y[:, t, :], x1[:, t, :], b_mv[:, t, 0:1], b_rstd[:, t:t + 1],
                                                ALU.subtract, ALU.mult)
                    ins.then_inc(y_ready.sem, 1)
                    dve.wait_ge(yth_ready.sem, yth_ready.at(q))
                    dve.scalar_tensor_tensor(yT_l[:, :, :].rearrange("p a b -> p (a b)"),
                                             yT_h[:, :, :].rearrange("p a b -> p (a b)").bitcast(F32), -1.0,
                                             GU[0][:, :], ALU.mult, ALU.add).then_inc(ytl_ready.sem, 1)
                    s.end()
                if k == 2:
                    dve.wait_ge(e_ready.sem, e_ready.at(q))
                    s = Steps(dve, route_steps, q)
                    s.done(dve.tensor_scalar(sc_e[:, :, :], sc_e[:, :, :], 1.0, None, ALU.add))
                    s.done(dve.reciprocal(score[:, :, :], sc_e[:, :, :]))
                    s.done(dve.tensor_tensor(sel[:, :, :], score[:, :, :],
                                             bias_b[:, :].unsqueeze(1).to_broadcast([P, T, NE]), ALU.add))
                    of_j = sel[:, :, :].unsqueeze(2).to_broadcast([P, T, NE, NE])
                    of_i = sel[:, :, :].unsqueeze(3).to_broadcast([P, T, NE, NE])
                    s.done(dve.tensor_tensor(cmp_gt[:, :, :, :], of_j, of_i, ALU.is_gt))
                    s.done(dve.tensor_tensor(cmp_eq[:, :, :, :], of_j, of_i, ALU.is_equal))
                    s.done(dve.tensor_tensor(cmp_eq[:, :, :, :], cmp_eq[:, :, :, :],
                                             lower[:, :, :].unsqueeze(1).to_broadcast([P, T, NE, NE]), ALU.mult))
                    s.done(dve.tensor_tensor(cmp_gt[:, :, :, :], cmp_gt[:, :, :, :], cmp_eq[:, :, :, :], ALU.add))
                    s.done(dve.tensor_reduce(rank[:, :, :], cmp_gt[:, :, :, :], AX.X, ALU.add))
                    s.done(dve.scalar_tensor_tensor(cw[:, :, :], rank[:, :, :], TOP_K - 0.5, score[:, :, :],
                                                    ALU.is_lt, ALU.mult))
                    s.done(dve.tensor_reduce(csum[:, :], cw[:, :, :], AX.X, ALU.add))
                    s.done(dve.reciprocal(crec[:, :], csum[:, :]))
                    s.done(dve.scalar_tensor_tensor(cw[:, :, :], cw[:, :, :], 0.5,
                                                    crec[:, :].unsqueeze(2).to_broadcast([P, T, NE]),
                                                    ALU.mult, ALU.mult))
                    s.done(dve.tensor_copy(cwhl[:, :, 0, :].bitcast(F32R), cw[:, :, :]))
                    dve.tensor_tensor(cwhl[:, :, 1, :].bitcast(F32R), cw[:, :, :], cwhl[:, :, 0, :], ALU.subtract)\
                       .then_inc(cwhl_ready.sem, 1)
                    s.end()
                if k == 3:
                    dve.wait_ge(cwt_ready.sem, cwt_ready.at(q))
                    dve.tensor_copy(cwT[:, :], GU[0][0:2 * NE, 0:T * P]).then_inc(cwt_copied.sem, 1)

            def hidden(q, n):
                if n == 0:
                    dve.wait_ge(g1_ready.sem, g1_ready.at(q, 0))
                else:
                    dve.wait_ge(g2_ready.sem, g2_ready.at(q, n - 1))
                if n >= 3:
                    dve.wait_ge(down_done.sem, down_done.at(q, n - 3))
                elif not first(q):
                    dve.wait_ge(down_done.sem, down_done.at(q - 1, NX - 1))
                up = GU[n % 2][:, L:2 * L]
                if n == 0:
                    ins = dve.scalar_tensor_tensor(h[0][:, :], g1[0][:, :], 0.5, up, ALU.mult, ALU.mult)
                else:
                    ins = dve.tensor_tensor(h[n % 3][:, :], g2[n % 2][:, :], up, ALU.mult)
                ins.then_inc(h_ready.sem, 1)

            def expert(q, n):
                dve.wait_ge(th_ready.sem, th_ready.at(q, n))
                dve.scalar_tensor_tensor(g1[n % 2][:, :], th[n % 2][:, :], 1.0, GU[n % 2][:, 0:L], ALU.add,
                                         ALU.mult).then_inc(g1_ready.sem, 1)
                if n >= 1:
                    hidden(q, n - 1)

            def experts_end(q, _=0):
                hidden(q, NX - 1)
                dve.wait_ge(down_done.sem, down_done.at(q, NX - 1))
                dve.wait_ge(x1b_ready.sem, x1b_ready.at(q))
                dve.tensor_tensor(x2[:, :, :].rearrange("p a b -> p (a b)"),
                                  x1b[:, :, :].rearrange("p a b -> p (a b)"), Y[:, :], ALU.add)\
                   .then_inc(x2_ready.sem, 1)

            def second(q, t, k):
                if k == 0:
                    if t == 0:
                        dve.wait_ge(x2_ready.sem, x2_ready.at(q))
                        s = Steps(dve, c_steps, q)
                        dve.bn_stats(c_st[:, 0, :], x2[:, 0, :])
                        s.done(dve.bn_stats(c_st[:, 1, :], x2[:, 1, :]))
                        dve.memset(spare[:, :], 0.0)
                        dve.bn_aggr(c_mv[:, 0, :], c_st[:, 0, :])
                        s.done(dve.bn_aggr(c_mv[:, 1, :], c_st[:, 1, :]))
                        dve.tensor_scalar(c_ve[:, :], c_mv[:, :, 1], LN_EPS, None, ALU.add)\
                           .then_inc(c_var.sem, 1)
                        dve.wait_ge(c_rs.sem, c_rs.at(q))
                        dve.tensor_scalar(z[:, 1, :], x2[:, 1, :], c_mv[:, 1, 0:1], c_rstd[:, 1:2],
                                          ALU.subtract, ALU.mult)
                        dve.tensor_scalar(z[:, 0, :], x2[:, 0, :], c_mv[:, 0, 0:1], c_rstd[:, 0:1],
                                          ALU.subtract, ALU.mult).then_inc(z_ready.sem, 1)
                        s.end()
                    dve.wait_ge(k_ready.sem, k_ready.at(q, t))
                    for j in range(4):
                        r = slice(32 * j, 32 * j + 32)
                        ins = dve.tensor_copy(kmask[r, :, j, :], GU[1][r, 0:2 * P]
                                              .rearrange("p (c n) -> p c n", c=2))
                    ins.then_inc(k_copied.sem, 1)
                if k == 1:
                    dve.wait_ge(sc_ready.sem, sc_ready.at(q, t))
                    scores = Y[:, :].rearrange("p (h e) -> p h e", h=NH1)
                    dve.tensor_reduce(smx[:, :], scores, AX.X, ALU.max).then_inc(smax_steps.sem, 1)
                    dve.wait_ge(smax_steps.sem, smax_steps.at(q, t))
                    dve.tensor_tensor(ssub[:, :, :], scores, smx[:, :].unsqueeze(2).to_broadcast([P, NH1, D]),
                                      ALU.subtract).then_inc(ssub_ready.sem, 1)
                    dve.wait_ge(p_ready.sem, p_ready.at(q, t))
                    for b in range(2):
                        r = slice(64 * b, 64 * b + 64)
                        ins = dve.tensor_reduce(ssum[r, :], ppad[r, :, b, :], AX.X, ALU.add)
                    ins.then_inc(srec_steps.sem, 1)
                    dve.wait_ge(srec_steps.sem, srec_steps.at(q, 2 * t))
                    dve.reciprocal(srec[:, :], ssum[:, :]).then_inc(srec_steps.sem, 1)
                    dve.wait_ge(srec_steps.sem, srec_steps.at(q, 2 * t + 1))
                if k == 2:
                    dve.wait_ge(pt_ready.sem, pt_ready.at(q, t))
                    dve.tensor_copy(pT[:, 4:8, :].rearrange("p a b -> p (a b)"), GU[1][:, :])\
                       .then_inc(pt_copied1.sem, 1)
                    dve.wait_ge(av_ready.sem, av_ready.at(q, t))
                    dve.tensor_tensor(av[:, :].rearrange("p (h n) -> p h n", h=NH1),
                                      srec[:, :].unsqueeze(2).to_broadcast([P, NH1, NW]),
                                      Y[:, 0:L].rearrange("p (h n) -> p h n", h=NH1), ALU.mult)\
                       .then_inc(av_steps.sem, 1)
                    dve.wait_ge(av_steps.sem, av_steps.at(q, t))
                    dve.tensor_tensor(u[:, :], z[:, t, :], av[:, :], ALU.subtract).then_inc(u_ready.sem, 1)
                    dve.wait_ge(o_ready.sem, o_ready.at(q, t))
                    dve.tensor_tensor(x3[:, t, :], x2[:, t, :], Y[:, L:2 * L], ALU.add).then_inc(x3_ready.sem, 1)

            def quantise(q, s, which, t, src, n, dst, ready):
                c = [rs[:, which, t, i:i + 1] for i in range(8)]
                s.done(dve.tensor_reduce(c[3], src, AX.X, ALU.max, apply_absolute_value=True))
                dve.wait_ge(ss_ready.sem, ss_ready.at(q, 2 * t + which))
                dve.tensor_scalar(c[1], c[0], 1.0 / n, RMS_EPS, ALU.mult, ALU.add).then_inc(ms_ready.sem, 1)
                dve.wait_ge(rms_ready.sem, rms_ready.at(q, 2 * t + which))
                s.done(dve.tensor_scalar(c[4], c[3], c[2], QUANT_EPS, ALU.mult, ALU.max))
                s.done(dve.reciprocal(c[5], c[4]))
                s.done(dve.scalar_tensor_tensor(c[5], c[5], 127.0, c[2], ALU.mult, ALU.mult))
                s.done(dve.tensor_scalar(qv[:, 0:n], src, c[5], MAGIC, ALU.mult, ALU.add))
                dve.tensor_scalar(dst, qv[:, 0:n], MAGIC, 127.0, ALU.subtract, ALU.min).then_inc(ready.sem, 1)

            q1 = [None]
            q2 = [None]

            def last_block(q, t, k):
                if k == 0:
                    dve.wait_ge(x3_ready.sem, x3_ready.at(q, t))
                    dve.bn_stats(d_st[:, t, :], x3[:, t, :]).then_inc(d_steps.sem, 1)
                    dve.wait_ge(d_steps.sem, d_steps.at(q, 2 * t))
                    dve.memset(spare[:, :], 0.0)
                    dve.bn_aggr(d_mv[:, t, :], d_st[:, t, :]).then_inc(d_steps.sem, 1)
                    dve.wait_ge(d_steps.sem, d_steps.at(q, 2 * t + 1))
                    dve.tensor_scalar(d_ve[:, t:t + 1], d_mv[:, t, 1:2], LN_EPS, None, ALU.add)\
                       .then_inc(d_var.sem, 1)
                    dve.wait_ge(d_rs.sem, d_rs.at(q, t))
                    dve.tensor_scalar(w[:, t, :], x3[:, t, :], d_mv[:, t, 0:1], d_rstd[:, t:t + 1],
                                      ALU.subtract, ALU.mult).then_inc(w_ready.sem, 1)
                    dve.wait_ge(w_ready.sem, w_ready.at(q, t))
                    if t == 0:
                        q1[0] = Steps(dve, q1_steps, q)
                    s = q1[0]
                    quantise(q, s, 0, t, w[:, t, :], L, qb[:, :], qb_ready)
                    c = [rs[:, 0, t, i:i + 1] for i in range(8)]
                    s.done(dve.tensor_scalar(c[6], c[4], 0.5 / 127.0, wmean[:, 0:1], ALU.mult, ALU.mult))
                    s.done(dve.tensor_scalar(c[7], c[4], 1.0 / 127.0, wmean[:, 1:2], ALU.mult, ALU.mult))
                    s.done(dve.tensor_tensor(c[7], c[6], c[7], ALU.mult))
                    if t == 1:
                        s.end()
                if k == 1:
                    dve.wait_ge(qt_ready.sem, qt_ready.at(q, t))
                    dve.tensor_copy(qbT[:, :, :].rearrange("p a b -> p (a b)"), GU[0][:, 0:P].bitcast(BF16))\
                       .then_inc(qbt_copied.sem, 1)
                    for c in range(2):
                        gate, up = ((GU[1], Y), (GU[0], GU[1]))[c]
                        dve.wait_ge(th2_ready.sem, th2_ready.at(q, 2 * t + c))
                        if c == 1:
                            dve.wait_ge(hc_ready.sem, hc_ready.at(q, 2 * t))
                        dve.scalar_tensor_tensor(hg[:, :], th2[:, :], 1.0, gate[:, 0:HC], ALU.add, ALU.mult)\
                           .then_inc(hg_ready.sem, 1)
                        dve.wait_ge(hg_ready.sem, hg_ready.at(q, 2 * t + c))
                        dve.wait_ge(up_ready.sem, up_ready.at(q, 2 * t + c))
                        dve.scalar_tensor_tensor(hid[:, c * HC:(c + 1) * HC], hg[:, :], rs[:, 0, t, 7:8],
                                                 up[:, 0:HC], ALU.mult, ALU.mult).then_inc(hc_ready.sem, 1)
                if k == 2:
                    dve.wait_ge(hc_ready.sem, hc_ready.at(q, 2 * t + 1))
                    if t == 0:
                        q2[0] = Steps(dve, q2_steps, q)
                    s = q2[0]
                    quantise(q, s, 1, t, hid[:, :], HID, hb[:, :], hb_ready)
                    c = [rs[:, 1, t, i:i + 1] for i in range(8)]
                    s.done(dve.tensor_scalar(c[6], c[4], 1.0 / 127.0, wmean[:, 2:3], ALU.mult, ALU.mult))
                    if t == 1:
                        s.end()
                    dve.wait_ge(hbt_ready.sem, hbt_ready.at(q, t))
                    src = Y[:, 0:HK * P // 2].bitcast(BF16)
                    dve.tensor_copy(hbT[0:HR, HK - 1, :], src[0:HR, (HK - 1) * P:HK * P])
                    dve.tensor_copy(hbT[:, 0:HK - 1, :].rearrange("p a b -> p (a b)"), src[:, 0:(HK - 1) * P])\
                       .then_inc(hbt_copied.sem, 1)
                    if t == 0 and not first(q):
                        dve.wait_ge(out_sent.sem, out_sent.at(q - 1))
                    dve.wait_ge(dn_ready.sem, dn_ready.at(q, t))
                    dve.scalar_tensor_tensor(xo[:, t, :], GU[0][:, 0:L], c[6], x3[:, t, :], ALU.mult, ALU.add)\
                       .then_inc(xo_ready.sem, 1)

            def setup_weights():
                dve.wait_ge(split_h.sem, 1)
                dve.tensor_tensor(gw_l[:, :, :], gw[:, :, :], gw_h[:, :, :].bitcast(F32), ALU.subtract)\
                   .then_inc(split_l.sem, 1)
                for c, (e0, ne) in enumerate(chunks):
                    dve.wait_ge(split_h.sem, c + 2)
                    hi = wgu_h[:, e0:e0 + ne, :, :, :].rearrange("p a b c d -> p (a b c d)").bitcast(F32)
                    dve.tensor_tensor(wgu_l[:, e0:e0 + ne, :, :, :].rearrange("p a b c d -> p (a b c d)"),
                                      stage[c % 2][:, 0:ne * GUW], hi, ALU.subtract).then_inc(split_l.sem, 1)
                dve.wait_ge(ident_ok.sem, 1)
                dve.tensor_copy(ident_bf[:, :], ident[:, :])
                dve.tensor_tensor(pick[:, :, :],
                                  ident[0:2 * NE, 0:NE].unsqueeze(2).to_broadcast([2 * NE, NE, P]),
                                  ident[0:2 * NE, NE:2 * NE].unsqueeze(2).to_broadcast([2 * NE, NE, P]), ALU.add)
                dve.wait_ge(l1w_in.sem, 64)
                dve.tensor_reduce(wabs[:, 0:1], w1s, AX.X, ALU.add, apply_absolute_value=True)
                dve.tensor_reduce(wabs[:, 1:2], w2s, AX.X, ALU.add, apply_absolute_value=True)
                dve.tensor_reduce(wabs[:, 2:3], w3s, AX.X, ALU.add, apply_absolute_value=True)
                dve.tensor_reduce(wabs[:, 3:4], w3tail[:, :], AX.X, ALU.add, apply_absolute_value=True)\
                   .then_inc(wsum_ready.sem, 1)
                dve.wait_ge(wsum_done.sem, 1)
                step.done(dve.tensor_copy(wmean[:, :], GU[0][:, 0:4]))
                step.done(dve.tensor_tensor(wmean[:, 2:3], wmean[:, 2:3], wmean[:, 3:4], ALU.add))
                step.done(dve.tensor_scalar(wmean[:, 0:3], wmean[:, 0:3], 1.0 / (HID * L), QUANT_EPS,
                                            ALU.mult, ALU.max))
                step.done(dve.reciprocal(wscale[:, 0:3], wmean[:, 0:3]))
                for n, src, dst in ((0, w1s, w1q[:, :, :].rearrange("p a b -> p (a b)")),
                                    (1, w2s, w2q[:, :, :].rearrange("p a b -> p (a b)")),
                                    (2, w3s, w3q[:, 0:HK - 1, :].rearrange("p a b -> p (a b)")),
                                    (2, w3tail[:, :], w3q[:, HK - 1, :])):
                    step.done(dve.tensor_scalar(src, src, wscale[:, n:n + 1], MAGIC, ALU.mult, ALU.add))
                    step.done(dve.tensor_scalar(src, src, MAGIC, 1.0, ALU.subtract, ALU.min))
                    step.done(dve.tensor_scalar(dst, src, -1.0, None, ALU.max))
                dve.tensor_copy(wabs[:, 0:1], wabs[:, 0:1]).then_inc(dve_const.sem, 1)

            setup_weights()
            run(dve, {"A": attention_inputs, "H": head_slot, "R": router, "E": expert, "T": experts_end,
                      "C": second, "D": last_block})

        @block.tensor
        def _(pe):
            pe.wait_ge(ident_ok.sem, 1)
            pe.wait_ge(wsum_ready.sem, 1)
            pe.matmul(GU[0][:, 0:4], ones[:, :], wabs[:, :], start=True, stop=True).then_inc(wsum_done.sem, 1)

            def attention_inputs(q, _=0):
                pe.wait_ge(ctxa_in.sem, ctxa_in.at(q))
                if not first(q):
                    pe.wait_ge(mt_copied.sem, mt_copied.at(q - 1, 1))
                    pe.wait_ge(s1_read.sem, s1_read.at(q - 1, 15))
                for t in range(T):
                    for c in range(2):
                        ins = pe.transpose(S1a[:, (2 * t + c) * P:(2 * t + c + 1) * P],
                                           ctxa[:, t, c * P:(c + 1) * P], ident[:, :])
                ins.then_inc(vt_ready.sem, 1)

            def values(q, m):
                t, s = m // 4, m % 4
                pe.wait_ge(exp_ready.sem, exp_ready.at(q, 2 * m + 1))
                if m == 4:
                    pe.wait_ge(x1_ready.sem, x1_ready.at(q, 0))
                elif m == 0 and not first(q):
                    pe.wait_ge(x1_ready.sem, x1_ready.at(q - 1, 1))
                if m == 0:
                    pe.wait_ge(vpad_ready.sem, vpad_ready.at(q))
                for c in range(2):
                    for kind in range(2):
                        for g in range(4):
                            lhs = (vpad[:, 2 * t + c, 136 * s - 8 * s + 32 * g:136 * s - 8 * s + 32 * g + 32]
                                   if kind == 0 else ones_pad[:, s, :])
                            ins = pe.matmul(OD[32 * g:32 * g + 32, kind * L:(kind + 1) * L], lhs,
                                            E[m % 2][:, g, c, :], start=(s == 0 and c == 0 and kind == 0),
                                            stop=(s == 3 and c == 1), skip_group_check=True)
                ins.then_inc(pv_done.sem, 1)

            def head_slot(q, k):
                if k in (8, 16):
                    t = k // 8 - 1
                    pe.wait_ge(mhl_ready.sem, mhl_ready.at(q, t))
                    for c in range(2):
                        ins = pe.transpose(S1[0:32, 0, c * P:(c + 1) * P],
                                           mhl[:, t, c, :, :].rearrange("p a b -> p (a b)"), ident[:, :])
                    ins.then_inc(mt_ready.sem, 1)
                if k < 16:
                    t, s, g0 = k // 8, k // 2 % 4, 2 * (k % 2)
                    if k == 0:
                        pe.wait_ge(vpad_ready.sem, vpad_ready.at(q))
                        pe.wait_ge(aug_in.sem, aug_in.at(q, 7))
                    elif k == 8:
                        pe.wait_ge(mt_copied.sem, mt_copied.at(q, 0))
                    else:
                        pe.wait_ge(s1_read.sem, s1_read.at(q, k - 1))
                    for c in range(2):
                        for v in range(2):
                            r = slice(32 * (g0 + v), 32 * (g0 + v) + 24)
                            ins = pe.matmul(S1[:, v, c * L:(c + 1) * L], qaug[r, s, t, c * P:(c + 1) * P],
                                            kaug[r, s, t, :], start=True, stop=True)
                    ins.then_inc(s1_ready.sem, 1)
                if 9 <= k < 25:
                    step = k - 9
                    t, s, g0 = step // 8, step // 2 % 4, 2 * (step % 2)
                    if step % 8 == 0:
                        pe.wait_ge(max_in.sem, max_in.at(q, 2 * t + 1))
                    if step > 0:
                        pe.wait_ge(exp_ready.sem, exp_ready.at(q, step - 1))
                    elif not first(q):
                        pe.wait_ge(exp_ready.sem, exp_ready.at(q - 1, 15))
                    for c in range(2):
                        for v in range(2):
                            r = slice(32 * (g0 + v), 32 * (g0 + v) + 26)
                            ins = pe.matmul(S2[:, v, c * L:(c + 1) * L], kaug[r, s, t, c * P:(c + 1) * P],
                                            qaug[r, s, t, :], start=True, stop=True)
                    ins.then_inc(s2_ready.sem, 1)
                if k >= 11 and k % 2 == 1:
                    values(q, (k - 11) // 2)

            def router(q, k):
                if k == 0:
                    pe.wait_ge(y_ready.sem, y_ready.at(q))
                    if not first(q):
                        pe.wait_ge(xo_ready.sem, xo_ready.at(q - 1, 1))
                    else:
                        pe.wait_ge(dve_const.sem, 2)
                        pe.wait_ge(split_l.sem, 1 + len(chunks))
                        pe.wait_ge(wd_in.sem, 16)
                        pe.wait_ge(const_in.sem, 16 * 11)
                    for t in range(T):
                        for c in range(2):
                            ins = pe.transpose(GU[0][:, c * L + t * P:c * L + (t + 1) * P],
                                               y[:, t, c * P:(c + 1) * P], ident[:, :])
                    ins.then_inc(yt_ready.sem, 1)
                if k == 1:
                    pe.wait_ge(ytl_ready.sem, ytl_ready.at(q))
                    for t in range(T):
                        parts = [(c, a, b) for c in range(2) for a, b in ((yT_h, gw_h), (yT_l, gw_h), (yT_h, gw_l))]
                        for n, (c, a, b) in enumerate(parts):
                            ins = pe.matmul(GU[1][:, t * NE:(t + 1) * NE], a[:, c, t * P:(t + 1) * P], b[:, c, :],
                                            start=(n == 0), stop=(n == len(parts) - 1))
                    ins.then_inc(logits_ready.sem, 1)
                if k == 3:
                    pe.wait_ge(cwhl_ready.sem, cwhl_ready.at(q))
                    for t in range(T):
                        ins = pe.transpose(GU[0][0:2 * NE, t * P:(t + 1) * P],
                                           cwhl[:, t, :, :].rearrange("p a b -> p (a b)"), ident[:, :])
                    ins.then_inc(cwt_ready.sem, 1)
                    for r in range(8):
                        if r == 0:
                            pe.wait_ge(cwt_copied.sem, cwt_copied.at(q))
                        if r >= 2:
                            pe.wait_ge(bc_copied.sem, bc_copied.at(q, r - 2))
                        for v in range(2):
                            ins = pe.matmul(GU[r % 2][:, v * L:(v + 1) * L], pick[:, 2 * r + v, :], cwT[:, :],
                                            start=True, stop=True)
                        ins.then_inc(bc_ready.sem, 1)

            def down(q, n):
                pe.wait_ge(h_ready.sem, h_ready.at(q, n))
                for t in range(T):
                    ins = pe.matmul(Y[:, t * L:(t + 1) * L], h[n % 3][:, t * P:(t + 1) * P], wd[:, n, :],
                                    start=(n == 0 and t == 0), stop=(n == NX - 1), skip_group_check=True)
                ins.then_inc(down_done.sem, 1)

            def expert(q, n):
                if n < 2:
                    pe.wait_ge(bc_copied.sem, bc_copied.at(q, 6 + n))
                else:
                    pe.wait_ge(h_ready.sem, h_ready.at(q, n - 2))
                for half in range(2):
                    parts = [(c, a, b) for c in range(2) for a, b in ((wgu_h, yT_h), (wgu_h, yT_l), (wgu_l, yT_h))]
                    for i, (c, a, b) in enumerate(parts):
                        ins = pe.matmul(GU[n % 2][:, half * L:(half + 1) * L], a[:, n, c, half, :], b[:, c, :],
                                        start=(i == 0), stop=(i == len(parts) - 1))
                ins.then_inc(gu_ready.sem, 1)
                if n >= 2:
                    down(q, n - 2)

            def experts_end(q, _=0):
                down(q, NX - 2)
                down(q, NX - 1)

            def second(q, t, k):
                if k == 0:
                    if t == 0:
                        pe.wait_ge(z_ready.sem, z_ready.at(q))
                        pe.wait_ge(ctxb_in.sem, ctxb_in.at(q))
                    else:
                        pe.wait_ge(pt_copied0.sem, pt_copied0.at(q, 0))
                        pe.wait_ge(pt_copied1.sem, pt_copied1.at(q, 0))
                    for c in range(2):
                        pe.matmul(GU[0][:, c * P:(c + 1) * P], z[:, t, c * P:(c + 1) * P], proj[:, 0, :],
                                  start=True, stop=True)
                    pe.matmul(GU[0][:, L:2 * L], proj[:, 2, :], ctxb[:, t, :], start=True, stop=True)\
                      .then_inc(qv_ready.sem, 1)
                    for c in range(2):
                        ins = pe.matmul(GU[1][:, c * P:(c + 1) * P], ctxb[:, t, c * P:(c + 1) * P],
                                        proj[:, 1, :], start=True, stop=True)
                    ins.then_inc(k_ready.sem, 1)
                if k == 1:
                    pe.wait_ge(qt_copied.sem, qt_copied.at(q, t))
                    pe.wait_ge(k_copied.sem, k_copied.at(q, t))
                    if t == 0:
                        pe.wait_ge(x2_ready.sem, x2_ready.at(q))
                    else:
                        pe.wait_ge(x3_ready.sem, x3_ready.at(q, 0))
                    for c in range(2):
                        for b in range(2):
                            ins = pe.matmul(Y[64 * b:64 * b + 64, c * L:(c + 1) * L]
                                            .rearrange("p (j e) -> p j e", j=4),
                                            qT[:, c * P + 64 * b:c * P + 64 * b + 64],
                                            kmask[:, c, :, 64 * b:64 * b + 64], start=True, stop=True)
                    ins.then_inc(sc_ready.sem, 1)
                if k == 2:
                    pe.wait_ge(p_ready.sem, p_ready.at(q, t))
                    pe.wait_ge(v_copied.sem, v_copied.at(q, t))
                    for n in range(NH1):
                        ins = pe.transpose(GU[n // 4][:, n % 4 * P:(n % 4 + 1) * P],
                                           ppad[:, n, :, :].rearrange("p a b -> p (a b)"), ident[:, :])
                    ins.then_inc(pt_ready.sem, 1)
                    pe.wait_ge(pt_copied0.sem, pt_copied0.at(q, t))
                    pe.wait_ge(pt_copied1.sem, pt_copied1.at(q, t))
                    for n in range(NH1):
                        ins = pe.matmul(Y[:, n * NW:(n + 1) * NW], pT[:, n, :], v1[:, n * NW:(n + 1) * NW],
                                        start=True, stop=True)
                    ins.then_inc(av_ready.sem, 1)
                    pe.wait_ge(u_ready.sem, u_ready.at(q, t))
                    pe.matmul(Y[:, L:2 * L], proj[:, 3, :], u[:, :], start=True, stop=True)\
                      .then_inc(o_ready.sem, 1)

            def last_block(q, t, k):
                if k == 1:
                    pe.wait_ge(qb_ready.sem, qb_ready.at(q, t))
                    if t == 0:
                        pe.wait_ge(x3_ready.sem, x3_ready.at(q, 1))
                    else:
                        pe.wait_ge(xo_ready.sem, xo_ready.at(q, 0))
                    tr = GU[0][:, 0:P].bitcast(BF16)
                    for c in range(2):
                        ins = pe.transpose(tr[:, c * P:(c + 1) * P], qb[:, c * P:(c + 1) * P], ident_bf[:, :])
                    ins.then_inc(qt_ready.sem, 1)
                    pe.wait_ge(qbt_copied.sem, qbt_copied.at(q, t))
                    for c in range(2):
                        gate, up = ((GU[1], Y), (GU[0], GU[1]))[c]
                        for bank, wt, ready in ((gate, w1q, hid_ready), (up, w2q, up_ready)):
                            if c == 1 and bank is GU[1]:
                                pe.wait_ge(hg_ready.sem, hg_ready.at(q, 2 * t))
                            for i in range(2):
                                ins = pe.matmul(bank[:, 0:HC], qbT[:, i, :], wt[:, i, c * HC:(c + 1) * HC],
                                                start=(i == 0), stop=(i == 1))
                            ins.then_inc(ready.sem, 1)
                if k == 2:
                    pe.wait_ge(hb_ready.sem, hb_ready.at(q, t))
                    tr = Y[:, 0:HK * P // 2].bitcast(BF16)
                    for c in range(HK):
                        n = P if c < HK - 1 else HR
                        ins = pe.transpose(tr[0:n, c * P:(c + 1) * P], hb[:, c * P:c * P + n], ident_bf[:, :])
                    ins.then_inc(hbt_ready.sem, 1)
                    pe.wait_ge(hbt_copied.sem, hbt_copied.at(q, t))
                    for c in range(HK):
                        n = P if c < HK - 1 else HR
                        ins = pe.matmul(GU[0][:, 0:L], hbT[0:n, c, :], w3q[0:n, c, :], start=(c == 0),
                                        stop=(c == HK - 1))
                    ins.then_inc(dn_ready.sem, 1)

            run(pe, {"A": attention_inputs, "H": head_slot, "R": router, "E": expert, "T": experts_end,
                     "C": second, "D": last_block})


_INS = ["x", "ctx", "gamma", "gate_w", "bias", "w_gu", "w_d", "wq", "wk", "wv", "wo", "w1", "w2", "w3"]


def kernel(x, ctx_2048, L0_xattn_gamma, L0_ffn_gate_w, L0_ffn_expert_bias, L0_ffn_w_gate, L0_ffn_w_up,
           L0_ffn_w_down, L0_ffn_sw_gate, L0_ffn_sw_up, L0_ffn_sw_down, L1_xattn_W_q, L1_xattn_W_k, L1_xattn_W_v,
           L1_xattn_W_o, L1_ffn_w1, L1_ffn_w2, L1_ffn_w3):
    import numpy as np
    import concourse.bacc as _bacc
    from concourse.bass_utils import run_bass_kernel_spmd as _run

    f = np.asarray
    gate = np.concatenate([f(L0_ffn_sw_gate)[None], f(L0_ffn_w_gate)])
    up = np.concatenate([f(L0_ffn_sw_up)[None], f(L0_ffn_w_up)])
    down = np.concatenate([f(L0_ffn_sw_down)[None], f(L0_ffn_w_down)])
    nx, hidden, width = gate.shape
    gu = np.stack([gate, up])
    gu = gu.reshape(2, nx, hidden, width // 128, 128).transpose(4, 1, 3, 0, 2)

    def chunked(a):
        return a.reshape(a.shape[0], -1, 128).transpose(2, 1, 0)

    arrays = {
        "x": f(x), "ctx": f(ctx_2048), "gamma": f(L0_xattn_gamma).reshape(1),
        "gate_w": chunked(f(L0_ffn_gate_w)), "bias": f(L0_ffn_expert_bias),
        "w_gu": gu.reshape(128, -1), "w_d": down.transpose(2, 0, 1),
        "wq": f(L1_xattn_W_q).T, "wk": f(L1_xattn_W_k).T, "wv": f(L1_xattn_W_v).T, "wo": f(L1_xattn_W_o).T,
        "w1": chunked(f(L1_ffn_w1)), "w2": chunked(f(L1_ffn_w2)), "w3": f(L1_ffn_w3).T,
    }
    arrays = {k: np.ascontiguousarray(a) for k, a in arrays.items()}
    nc = _bacc.Bacc("TRN2", target_bir_lowering=False, num_devices=1, dynamic_dma_scratch_size=1024)
    args = [nc.dram_tensor(f"in_{n}", arrays[n].shape, mybir.dt.from_np(arrays[n].dtype), kind="ExternalInput").ap()
            for n in _INS]
    out = nc.dram_tensor("out_0", arrays["x"].shape, F32, kind="ExternalOutput").ap()
    program(nc, *args, out)
    r = _run(nc, [{f"in_{n}": arrays[n] for n in _INS}], core_ids=[0])
    return r.results[0]["out_0"]
```

```python
from contextlib import ExitStack

import concourse.bass as bass
from concourse import mybir

F32 = mybir.dt.float32
F32R = mybir.dt.float32r
BF16 = mybir.dt.bfloat16
ALU = mybir.AluOpType
ACT = mybir.ActivationFunctionType
AX = mybir.AxisListType

P = 128
MAGIC = 1.5 * 2.0**23
LN_EPS = 1e-5
RMS_EPS = 1e-6
QUANT_EPS = 1e-5
TOP_K = 4


class Signal:

    def __init__(self, sem, per, unit=1):
        self.sem, self.per, self.unit = sem, per, unit

    def at(self, q, k=0):
        return (q * self.per + (k + 1)) * self.unit


class Steps:

    def __init__(self, eng, chain, q):
        self.eng, self.chain, self.q, self.k = eng, chain, q, 0

    def done(self, ins):
        ins.then_inc(self.chain.sem, 1)
        self.eng.wait_ge(self.chain.sem, self.chain.at(self.q, self.k))
        self.k += 1

    def end(self):
        assert self.k == self.chain.per, (self.k, self.chain.per)


def first(q):
    return isinstance(q, int) and q == 0


PLAN = """
    B0 B1 A0 C0.0 A1 B2 C0.1 A2 B3 C0.2 B4 C0.3 E0 Y0 E1 C0.4 E2 H0 C0.5 H1 Y1 Z0 C0.6 H2 C1.2 Y2 H3
    E3 C1.3 H4 Y3 E4 Z1 H5 C1.4 E5 H6 Z2 Y4 C1.5 H7 E6 C1.6 M0 Y5 Z3 D0.0 H8 D0.1 Y6 D0.2 E7 H9 Z4
    D0.3 Y7 E8 X9 Z5 D0.4 H10 D1.0 Z6 D0.5 Y8 X10 E9 H11 D0.6 Y9 E10 X11 D0.7 Z7 H12 V11 X12 D0.8
    D1.1 D1.2 E11 H13 V13 D1.3 X13 D0.9 Z8 Y10 H14 Y11 E12 X14 D0.10 H15 D1.4 Z9 Y12 D1.5 X15 Z10 M1
    D1.6 X16 V15 X17 V17 X18 F0 E13 X19 D1.7 E14 X20 V19 X21 Y13 D1.8 Z11 X22 V21 X23 Y14 E15 X24
    V23 V25 Z12 F1 R0 E16 Z13 D1.9 Z14 Y15 Z15 R1 R2 Y16 D1.10 R3 R4 R5 R6 Z16 T0 R7
"""


def body_plan():
    return [(item[0], *(int(n) for n in item[1:].split("."))) for item in PLAN.split()]


def program(nc, x, ctx, gamma, gate_w, bias, w_gu, w_d, wq, wk, wv, wo, w1, w2, w3, out):
    B, D, L = x.shape
    QB = 4
    NQ = B // QB
    T = 2
    H0 = 8
    DH = D // H0
    NE = gate_w.shape[2]
    NX = NE + 1
    HID = w1.shape[2]
    HC = HID // 2
    HK = (HID + P - 1) // P
    HR = HID - (HK - 1) * P
    NH1 = 8
    NW = L // NH1
    assert T * P == QB * D and L == 2 * P and P == 2 * D and DH == 8

    x_q = x.rearrange("(q t b) d l -> q (b d) t l", t=T, b=2)
    c_q = ctx.rearrange("(q t b) d l -> q (b d) t l", t=T, b=2)
    o_q = out.rearrange("(q t b) d l -> q (b d) t l", t=T, b=2)

    rows = nc.dram_tensor("rows", (2, 16, 3, DH, T * L), F32).ap()

    with ExitStack() as stack:
        def sb(name, shape, dt=F32):
            return stack.enter_context(nc.sbuf_tensor(name, shape, dt))

        def sig(name, per=1, unit=1):
            return Signal(stack.enter_context(nc.semaphore(name)), per, unit)

        wgu_h = sb("wgu_h", [P, NX, 2, 2, P], F32R)
        wgu_l = sb("wgu_l", [P, NX, 2, 2, P], F32R)
        wd = sb("wd", [P, NX, L])
        gw = sb("gw", [P, 2, NE])
        bias_b = sb("bias_b", [P, NE])
        gamma_b = sb("gamma_b", [P, 1])
        proj = sb("proj", [P, 4, P])
        w1q = sb("w1q", [P, 2, HID], BF16)
        w2q = sb("w2q", [P, 2, HID], BF16)
        w3q = sb("w3q", [P, HK, L], BF16)
        wabs = sb("wabs", [P, 4])
        wmean = sb("wmean", [P, 4])
        wscale = sb("wscale", [P, 4])
        ident = sb("ident", [P, P])
        ident_bf = sb("ident_bf", [P, P], BF16)
        ones = sb("ones", [P, P])
        ones_pad = sb("ones_pad", [P, 4, 32])
        lower = sb("lower", [P, NE, NE])
        pick = sb("pick", [2 * NE, NE, P], F32R)
        mhalf = sb("mhalf", [P, T])
        spare = sb("spare", [P, 1])

        xin = sb("xin", [P, T, L])
        ctxa = sb("ctxa", [P, T, L])
        xres = sb("xres", [P, T, L])
        a_st = sb("a_st", [P, T, 6])
        a_mv = sb("a_mv", [P, T, 2])
        a_ve = sb("a_ve", [P, T])
        a_rstd = sb("a_rstd", [P, T])
        qaug = sb("qaug", [P, 4, T, L], F32R)
        kaug = sb("kaug", [P, 4, T, L], F32R)
        vpad = sb("vpad", [P, T * 2, 4 * 136])
        mneg = sb("mneg", [P, T, 2, 16])
        mhl = sb("mhl", [P, T, 2, 2, 16])
        mT = sb("mT", [32, T, L])
        E = [sb(f"E{i}", [P, 4, 2, L]) for i in range(2)]
        rden = sb("rden", [P, L])
        attn = sb("attn", [P, L])
        x1 = sb("x1", [P, T, L])
        x1b = sb("x1b", [P, T, L])
        b_st = sb("b_st", [P, T, 6])
        b_mv = sb("b_mv", [P, T, 2])
        b_ve = sb("b_ve", [P, T])
        b_rstd = sb("b_rstd", [P, T])
        yT_h = sb("yT_h", [P, 2, T * P], F32R)
        yT_l = sb("yT_l", [P, 2, T * P], F32R)
        sc_e = sb("sc_e", [P, T, NE])
        score = sb("score", [P, T, NE])
        sel = sb("sel", [P, T, NE])
        rank = sb("rank", [P, T, NE])
        cw = sb("cw", [P, T, NE])
        csum = sb("csum", [P, T])
        crec = sb("crec", [P, T])
        cwhl = sb("cwhl", [P, T, 2, NE])
        cwT = sb("cwT", [2 * NE, T * P], F32R)
        cwb = sb("cwb", [P, NE, T * P])
        th_all = sb("th_all", [P, 2 * L])
        g1_all = sb("g1_all", [P, 2 * L])
        th, g1 = ([a[:, i * L:(i + 1) * L] for i in range(2)] for a in (th_all, g1_all))
        g2 = [sb(f"g2_{i}", [P, L]) for i in range(2)]
        h = [sb(f"h{i}", [P, L]) for i in range(3)]
        ctxb = sb("ctxb", [P, T, L])
        x2 = sb("x2", [P, T, L])
        c_st = sb("c_st", [P, T, 6])
        c_mv = sb("c_mv", [P, T, 2])
        c_ve = sb("c_ve", [P, T])
        c_rstd = sb("c_rstd", [P, T])
        z = sb("z", [P, T, L])
        qT = sb("qT", [P, 2 * P])
        kmask = sb("kmask", [P, 2, 4, P])
        v1 = sb("v1", [P, L])
        smx = sb("smx", [P, NH1])
        ppad = sb("ppad", [P, NH1, 2, D])
        ssum = sb("ssum", [P, NH1])
        srec = sb("srec", [P, NH1])
        x3 = sb("x3", [P, T, L])
        d_st = sb("d_st", [P, T, 6])
        d_mv = sb("d_mv", [P, T, 2])
        d_ve = sb("d_ve", [P, T])
        d_rstd = sb("d_rstd", [P, T])
        rs = sb("rs", [P, 2, T, 8])
        qb = sb("qb", [P, L], BF16)
        qbT = sb("qbT", [P, 2, P], BF16)
        hb = sb("hb", [P, HID], BF16)
        hbT = sb("hbT", [P, HK, P], BF16)
        late = sb("late", [P, NH1 * P + NH1 * D + L])

        S = stack.enter_context(nc.psum_tensor("S", [P, 2, 512], F32))
        BA = stack.enter_context(nc.psum_tensor("BA", [P, 512], F32))
        BB = stack.enter_context(nc.psum_tensor("BB", [P, 512], F32))
        OD = stack.enter_context(nc.psum_tensor("OD", [P, 512], F32))
        GU = [stack.enter_context(nc.psum_tensor(f"GU{i}", [P, 512], F32)) for i in range(2)]
        Y = stack.enter_context(nc.psum_tensor("Y", [P, 512], F32))

        const_in = sig("const_in", 1, 16)
        l1w_in = sig("l1w_in", 1, 16)
        gu_in = [sig(f"gu_in{i}", 1, 16) for i in range(2)]
        wd_in = sig("wd_in", 1, 16)
        zeroed = sig("zeroed")
        ident_ok = sig("ident_ok")
        pool_setup = sig("pool_setup", 12)
        setup_steps = sig("setup_steps", 64)
        wsum_ready = sig("wsum_ready")
        wsum_done = sig("wsum_done")
        split_h = sig("split_h", 8)
        split_l = sig("split_l", 8)
        dve_const = sig("dve_const", 1)
        xin_in = sig("xin_in", 1, 16)
        ctxa_in = sig("ctxa_in", 1, 16)
        xres_in = sig("xres_in", 1, 16)
        ctxb_in = sig("ctxb_in", 1, 16)
        rows_out = sig("rows_out", 6, 16)
        aug_in = sig("aug_in", 8, 16)
        max_in = sig("max_in", 4, 16)
        out_sent = sig("out_sent", 1, 16)
        a_steps = sig("a_steps", 2)
        a_var = sig("a_var")
        a_rs = sig("a_rs")
        xn_ready = sig("xn_ready")
        xh_ready = sig("xh_ready")
        ch_ready = sig("ch_ready")
        xl_ready = sig("xl_ready")
        cl_ready = sig("cl_ready")
        vt_ready = sig("vt_ready")
        vpad_ready = sig("vpad_ready")
        s1_ready = sig("s1_ready", 16)
        s1_read = sig("s1_read", 16)
        max_steps = sig("max_steps", 2)
        mhl_ready = sig("mhl_ready", 2)
        mt_ready = sig("mt_ready", 2)
        mt_copied = sig("mt_copied", 2)
        s2_ready = sig("s2_ready", 16)
        exp_ready = sig("exp_ready", 16)
        pv_done = sig("pv_done", 8)
        fin_steps = sig("fin_steps", 4)
        x1_ready = sig("x1_ready", 2)
        x1b_ready = sig("x1b_ready")
        b_steps = sig("b_steps", 2)
        b_var = sig("b_var")
        b_rs = sig("b_rs")
        y_ready = sig("y_ready")
        yt_ready = sig("yt_ready")
        yt_copied = sig("yt_copied")
        yth_ready = sig("yth_ready")
        ytl_ready = sig("ytl_ready")
        logits_ready = sig("logits_ready")
        e_ready = sig("e_ready")
        route_steps = sig("route_steps", 13)
        cwhl_ready = sig("cwhl_ready")
        cwt_ready = sig("cwt_ready")
        cwt_copied = sig("cwt_copied")
        bc_ready = sig("bc_ready", 8)
        bc_copied = sig("bc_copied", 8)
        gu_ready = sig("gu_ready", NX)
        th_ready = sig("th_ready", NX)
        g1_ready = sig("g1_ready", NX)
        g2_ready = sig("g2_ready", NX - 1)
        h_ready = sig("h_ready", NX)
        down_done = sig("down_done", NX)
        x2_ready = sig("x2_ready")
        c_steps = sig("c_steps", 2)
        c_var = sig("c_var")
        c_rs = sig("c_rs")
        z_ready = sig("z_ready")
        qv_ready = sig("qv_ready", 2)
        k_ready = sig("k_ready", 2)
        qt_copied = sig("qt_copied", 2)
        k_copied = sig("k_copied", 2)
        v_copied = sig("v_copied", 2)
        sc_ready = sig("sc_ready", 2)
        smax_steps = sig("smax_steps", 2)
        ssub_ready = sig("ssub_ready", 2)
        p_ready = sig("p_ready", 2)
        srec_steps = sig("srec_steps", 4)
        pt_ready = sig("pt_ready", 2)
        pt_copied0 = sig("pt_copied0", 2)
        pt_copied1 = sig("pt_copied1", 2)
        av_ready = sig("av_ready", 2)
        av_steps = sig("av_steps", 2)
        u_ready = sig("u_ready", 2)
        o_ready = sig("o_ready", 2)
        x3_ready = sig("x3_ready", 2)
        d_steps = sig("d_steps", 4)
        d_var = sig("d_var", 2)
        d_rs = sig("d_rs", 2)
        w_ready = sig("w_ready", 2)
        ss_ready = sig("ss_ready", 4)
        ms_ready = sig("ms_ready", 4)
        rms_ready = sig("rms_ready", 4)
        q1_steps = sig("q1_steps", 16)
        q2_steps = sig("q2_steps", 12)
        qb_ready = sig("qb_ready", 2)
        qt_ready = sig("qt_ready", 2)
        qbt_copied = sig("qbt_copied", 2)
        hid_ready = sig("hid_ready", 4)
        up_ready = sig("up_ready", 4)
        th2_ready = sig("th2_ready", 4)
        hg_ready = sig("hg_ready", 4)
        hc_ready = sig("hc_ready", 4)
        hb_ready = sig("hb_ready", 2)
        hbt_ready = sig("hbt_ready", 2)
        hbt_copied = sig("hbt_copied", 2)
        dn_ready = sig("dn_ready", 2)
        xo_ready = sig("xo_ready", 2)

        pT = late[:, 0:NH1 * P].rearrange("p (h d) -> p h d", h=NH1)
        ssub = late[:, NH1 * P:NH1 * P + NH1 * D].rearrange("p (h e) -> p h e", h=NH1)
        av = late[:, NH1 * P + NH1 * D:NH1 * P + NH1 * D + L]
        qv, hid = (late[:, i * HID:(i + 1) * HID] for i in range(2))
        w = z
        E0, E1 = (e[:, :, :, :].rearrange("p a b c -> p (a b c)") for e in E)
        xh, xl, ch, cl = (E0[:, i * T * L:(i + 1) * T * L].rearrange("p (t l) -> p t l", t=T).bitcast(F32R)
                          for i in range(4))
        xn = E1[:, 0:T * L].rearrange("p (t l) -> p t l", t=T)
        y = E1[:, T * L:2 * T * L].rearrange("p (t l) -> p t l", t=T)
        yT = E1[:, 2 * T * L:3 * T * L].rearrange("p (c n) -> p c n", c=2)
        cmp_gt, cmp_eq = (E0[:, i * T * NE * NE:(i + 1) * T * NE * NE]
                          .rearrange("p (t i j) -> p t i j", t=T, i=NE) for i in range(2))
        stage = [e[:, :, :, :].rearrange("p a b c -> p (a b c)") for e in E]
        w1s = cwb[:, :, :].rearrange("p a b -> p (a b)")[:, 0:2 * HID]
        w2s = cwb[:, :, :].rearrange("p a b -> p (a b)")[:, 2 * HID:4 * HID]
        w3s = cwb[:, :, :].rearrange("p a b -> p (a b)")[:, 4 * HID:4 * HID + (HK - 1) * L]
        w3tail = x3[:, 0, :]
        GUW = 4 * P
        chunks = [(c, min(4, NX - c)) for c in range(0, NX, 4)]
        Sa = S[:, 0, :]

        def vdiag(tl):
            v = vpad[:, tl, :].rearrange("p (s k) -> p s k", s=4)[:, :, 0:P]
            return v.rearrange("p s (g k) -> p s g k", g=4)[:, :, :, 0:DH]

        plan = body_plan()

        def run(eng, handlers):
            def body(mid, heads, behind):
                for item in plan:
                    q = heads if item[0] in "AHMXVFR" else behind if item[0] in "CD" else mid
                    if q is not None and item[0] in handlers:
                        handlers[item[0]](q, *item[1:])
            body(None, 0, None)
            body(0, 1 if NQ > 1 else None, None)
            if NQ > 2:
                body(1, 2, 0)
            if NQ > 3:
                with eng.Fori(2, NQ - 1) as i:
                    body(i, i + 1, i - 1)
            if NQ > 1:
                body(NQ - 1, None, NQ - 2)
            body(None, None, NQ - 1)

        block = stack.enter_context(nc.Block())

        @block.sync
        def _(sp):
            sp.dma_start(xin[:, :, :], x_q[0]).then_inc(xin_in.sem, 16)
            sp.dma_start(ctxa[:, :, :], c_q[0]).then_inc(ctxa_in.sem, 16)
            sp.dma_start(gw[:, :, :], gate_w).then_inc(const_in.sem, 16)
            sp.dma_start(bias_b[:, :], bias.partition_broadcast(P)).then_inc(const_in.sem, 16)
            sp.dma_start(gamma_b[:, :], gamma.partition_broadcast(P)).then_inc(const_in.sem, 16)
            sp.wait_ge(zeroed.sem, 1)
            for n, wt in enumerate((wq, wk, wv, wo)):
                for b in range(2):
                    sp.dma_start(proj[64 * b:64 * b + 64, n, 64 * b:64 * b + 64], wt).then_inc(const_in.sem, 16)
            for c, (e0, ne) in enumerate(chunks):
                if c >= 2:
                    sp.wait_ge(split_l.sem, c - 1)
                sp.dma_start(stage[c % 2][:, 0:ne * GUW], w_gu[:, e0 * GUW:(e0 + ne) * GUW]).then_inc(gu_in[c % 2].sem, 16)
                if c == 0:
                    sp.dma_start(w1s, w1.rearrange("p c n -> p (c n)")).then_inc(l1w_in.sem, 16)
                    sp.dma_start(w2s, w2.rearrange("p c n -> p (c n)")).then_inc(l1w_in.sem, 16)
                    sp.dma_start(w3s.rearrange("p (c n) -> p c n", n=L),
                                 w3[0:(HK - 1) * P, :].rearrange("(c p) n -> p c n", p=P)).then_inc(l1w_in.sem, 16)
                    sp.dma_start(w3tail[0:HR, :], w3[(HK - 1) * P:HID, :]).then_inc(l1w_in.sem, 16)
            sp.dma_start(wd[:, :, :], w_d).then_inc(wd_in.sem, 16)

            def attention_inputs(q, k):
                if k != 0:
                    return
                if not first(q):
                    sp.wait_ge(xn_ready.sem, xn_ready.at(q - 1))
                    sp.dma_start(xin[:, :, :], x_q[bass.ds(q, 1)].rearrange("a p t l -> (a p) t l")
                                 if not isinstance(q, int) else x_q[q]).then_inc(xin_in.sem, 16)
                    sp.wait_ge(vt_ready.sem, vt_ready.at(q - 1))
                    sp.wait_ge(ch_ready.sem, ch_ready.at(q - 1))
                    sp.wait_ge(cl_ready.sem, cl_ready.at(q - 1))
                    sp.dma_start(ctxa[:, :, :], c_q[bass.ds(q, 1)].rearrange("a p t l -> (a p) t l")
                                 if not isinstance(q, int) else c_q[q]).then_inc(ctxa_in.sem, 16)
                    sp.wait_ge(s2_ready.sem, s2_ready.at(q - 1, 15))
                    sp.wait_ge(x1_ready.sem, x1_ready.at(q - 1, 1))
                else:
                    sp.wait_ge(zeroed.sem, 2)
                sp.dma_start(xres[:, :, :], x_q[bass.ds(q, 1)].rearrange("a p t l -> (a p) t l")
                             if not isinstance(q, int) else x_q[q]).then_inc(xres_in.sem, 16)
                for src, ready, side, parts in ((xh, xh_ready, 0, (0, 2)), (ch, ch_ready, 1, (0, 1)),
                                                (cl, cl_ready, 1, (2,)), (xl, xl_ready, 0, (1,))):
                    sp.wait_ge(ready.sem, ready.at(q))
                    for part in parts:
                        sp.dma_start(rows[side, :, part, :, :],
                                     src[:, :, :].rearrange("p t l -> p (t l)").bitcast(F32))\
                          .then_inc(rows_out.sem, 16)
                sp.wait_ge(rows_out.sem, rows_out.at(q, 5))
                for dst, side in ((qaug, 0), (kaug, 1)):
                    for g in range(4):
                        sp.dma_start(dst[32 * g:32 * g + 24, :, :, :].rearrange("r s t l -> r s (t l)").bitcast(F32),
                                     rows[side, 4 * g:4 * g + 4].rearrange("s c r l -> (c r) s l"))\
                          .then_inc(aug_in.sem, 16)

            def maxima(q, t):
                sp.wait_ge(mt_copied.sem, mt_copied.at(q, t))
                for part in range(2):
                    sp.dma_start(qaug[24 + part:P:32, :, t, :].bitcast(F32), mT[16 * part:16 * part + 16, t, :])\
                      .then_inc(max_in.sem, 16)

            def second_inputs(q, _=0):
                if not first(q):
                    sp.wait_ge(k_ready.sem, k_ready.at(q - 1, 1))
                sp.dma_start(ctxb[:, :, :], c_q[bass.ds(q, 1)].rearrange("a p t l -> (a p) t l")
                             if not isinstance(q, int) else c_q[q]).then_inc(ctxb_in.sem, 16)

            def last_block(q, t, k):
                if t == 1 and k == 10:
                    sp.wait_ge(xo_ready.sem, xo_ready.at(q, 1))
                    sp.dma_start(o_q[bass.ds(q, 1)].rearrange("a p t l -> (a p) t l")
                                 if not isinstance(q, int) else o_q[q], x3[:, :, :]).then_inc(out_sent.sem, 16)

            run(sp, {"A": attention_inputs, "M": maxima, "T": second_inputs, "D": last_block})
            sp.wait_ge(out_sent.sem, 16 * NQ)

        @block.gpsimd
        def _(pool):
            n = 0

            def setup(ins):
                nonlocal n
                n += 1
                ins.then_inc(pool_setup.sem, 1)

            def settle():
                pool.wait_ge(pool_setup.sem, n)

            pool.memset(proj[:, :, :], 0.0).then_inc(zeroed.sem, 1)
            setup(pool.memset(ident[:, :], 0.0))
            settle()
            setup(pool.affine_select(out=ident[:, :], in_=ident[:, :], compare_op=ALU.not_equal, fill=1.0,
                                     base=0, pattern=[[-1, P]], channel_multiplier=1))
            setup(pool.memset(mhalf[:, :], -0.5))
            setup(pool.memset(ones[:, :], 1.0))
            setup(pool.memset(lower[:, :, :], 1.0))
            settle()
            pool.affine_select(out=lower[:, :, :], in_=lower[:, :, :], compare_op=ALU.is_gt, fill=0.0,
                               base=0, pattern=[[1, NE], [-1, NE]], channel_multiplier=0)\
                .then_inc(ident_ok.sem, 1)
            pool.wait_ge(ident_ok.sem, 1)
            pool.memset(kaug[:, :, :, :].bitcast(F32), 1.0).then_inc(zeroed.sem, 1)

            def attention_norm(q, k):
                if k != 1:
                    return
                pool.wait_ge(a_var.sem, a_var.at(q))
                pool.tensor_tensor(a_rstd[:, :], a_ve[:, :], mhalf[:, :], ALU.pow).then_inc(a_rs.sem, 1)

            def router(q, k):
                if k == 0:
                    pool.wait_ge(b_var.sem, b_var.at(q))
                    pool.tensor_tensor(b_rstd[:, :], b_ve[:, :], mhalf[:, :], ALU.pow).then_inc(b_rs.sem, 1)

            def expert(q, n):
                if n >= 1:
                    if n >= 3:
                        pool.wait_ge(h_ready.sem, h_ready.at(q, n - 2))
                    if n == 1:
                        pool.wait_ge(bc_copied.sem, bc_copied.at(q, 7))
                    pool.wait_ge(g1_ready.sem, g1_ready.at(q, n))
                    pool.tensor_tensor(g2[n % 2][:, :], g1[n % 2][:, :], cwb[:, n - 1, :], ALU.mult)\
                        .then_inc(g2_ready.sem, 1)

            def second(q, t, k):
                if k == 0:
                    pool.wait_ge(c_var.sem, c_var.at(q))
                    pool.tensor_tensor(c_rstd[:, :], c_ve[:, :], mhalf[:, :], ALU.pow).then_inc(c_rs.sem, 1)

            def rms(q, which, t):
                s = 2 * t + which
                pool.wait_ge(ms_ready.sem, ms_ready.at(q, s))
                pool.tensor_tensor(rs[:, which, t, 2:3], rs[:, which, t, 1:2], mhalf[:, 0:1], ALU.pow)\
                    .then_inc(rms_ready.sem, 1)

            def last_block(q, t, k):
                if k == 0:
                    pool.wait_ge(d_var.sem, d_var.at(q, t))
                    pool.tensor_tensor(d_rstd[:, t:t + 1], d_ve[:, t:t + 1], mhalf[:, 0:1], ALU.pow)\
                        .then_inc(d_rs.sem, 1)
                if k == 2:
                    rms(q, 0, t)
                if k == 7:
                    rms(q, 1, t)

            run(pool, {"A": attention_norm, "R": router, "E": expert, "C": second, "D": last_block})

        @block.scalar
        def _(act):
            for c, (e0, ne) in enumerate(chunks):
                act.wait_ge(gu_in[c % 2].sem, 16 * (c // 2 + 1))
                act.copy(wgu_h[:, e0:e0 + ne, :, :, :].rearrange("p a b c d -> p (a b c d)"),
                         stage[c % 2][:, 0:ne * GUW]).then_inc(split_h.sem, 1)

            def attention_inputs(q, k):
                if k != 2:
                    return
                if not first(q):
                    act.wait_ge(aug_in.sem, aug_in.at(q - 1, 7))
                act.wait_ge(xn_ready.sem, xn_ready.at(q))
                act.copy(xh[:, :, :], xn[:, :, :]).then_inc(xh_ready.sem, 1)
                act.wait_ge(ctxa_in.sem, ctxa_in.at(q))
                act.copy(ch[:, :, :], ctxa[:, :, :]).then_inc(ch_ready.sem, 1)
                act.wait_ge(vt_ready.sem, vt_ready.at(q))
                if first(q):
                    act.wait_ge(dve_const.sem, 1)
                else:
                    act.wait_ge(pv_done.sem, pv_done.at(q - 1, 7))
                for tl in range(4):
                    ins = act.copy(vdiag(tl), Sa[:, tl * P:(tl + 1) * P].rearrange("p (g s r) -> p s g r", g=4, s=4))
                ins.then_inc(vpad_ready.sem, 1)

            def exponentials(q, k):
                step = k - 9
                m = step // 2
                act.wait_ge(s2_ready.sem, s2_ready.at(q, step))
                if m >= 2:
                    act.wait_ge(pv_done.sem, pv_done.at(q, m - 2))
                elif first(q):
                    act.wait_ge(split_l.sem, len(chunks))
                else:
                    act.wait_ge(pv_done.sem, pv_done.at(q - 1, m + 6))
                    if m == 1:
                        act.wait_ge(ytl_ready.sem, ytl_ready.at(q - 1))
                u0 = 2 * (step % 2)
                act.activation(E[m % 2][:, u0:u0 + 2, :, :].rearrange("p a b c -> p a (b c)"), S[:, :, :],
                               ACT.Exp, scale=float(DH) ** -0.5).then_inc(exp_ready.sem, 1)

            def router(q, k):
                if k == 2:
                    act.wait_ge(yt_ready.sem, yt_ready.at(q))
                    act.copy(yT.rearrange("p a b -> p (a b)"), S[:, 0, :]).then_inc(yt_copied.sem, 1)
                if k == 3:
                    act.wait_ge(logits_ready.sem, logits_ready.at(q))
                    act.activation(sc_e[:, :, :].rearrange("p a b -> p (a b)"), S[:, 1, 0:T * NE], ACT.Exp,
                                   scale=-1.0).then_inc(e_ready.sem, 1)
                if k == 7:
                    act.wait_ge(cwt_ready.sem, cwt_ready.at(q))
                    act.copy(cwT[:, :], S[0:2 * NE, 1, 0:T * P]).then_inc(cwt_copied.sem, 1)

            def experts_start(q, k):
                if k == 0:
                    if not first(q):
                        act.wait_ge(gu_ready.sem, gu_ready.at(q - 1, NX - 1))
                    act.wait_ge(yt_copied.sem, yt_copied.at(q))
                    act.copy(yT_h[:, :, :], yT).then_inc(yth_ready.sem, 1)
                    act.wait_ge(x1_ready.sem, x1_ready.at(q, 1))
                    if not first(q):
                        act.wait_ge(x2_ready.sem, x2_ready.at(q - 1))
                    act.copy(x1b[:, :, :], x1[:, :, :]).then_inc(x1b_ready.sem, 1)
                else:
                    for r in (2 * (k - 1), 2 * (k - 1) + 1):
                        act.wait_ge(bc_ready.sem, bc_ready.at(q, r))
                        act.copy(cwb[:, 2 * r:2 * r + 2, :].rearrange("p a b -> p (a b)"), GU[r % 2][:, :])\
                           .then_inc(bc_copied.sem, 1)

            def expert(q, n):
                act.wait_ge(gu_ready.sem, gu_ready.at(q, n))
                if n >= 2:
                    act.wait_ge(g1_ready.sem, g1_ready.at(q, n - 2))
                elif not first(q):
                    act.wait_ge(g1_ready.sem, g1_ready.at(q - 1, NX - 1))
                act.activation(th[n % 2][:, :], GU[n % 2][:, 0:L], ACT.Tanh, scale=0.5).then_inc(th_ready.sem, 1)

            def second(q, t, k):
                if k == 2:
                    act.wait_ge(qv_ready.sem, qv_ready.at(q, t))
                    act.copy(qT[:, :], BA[:, 0:2 * P]).then_inc(qt_copied.sem, 1)
                    act.copy(v1[:, :], BA[:, L:2 * L]).then_inc(v_copied.sem, 1)
                    act.wait_ge(k_ready.sem, k_ready.at(q, t))
                    for j in range(4):
                        r = slice(32 * j, 32 * j + 32)
                        ins = act.copy(kmask[r, :, j, :], BB[r, 0:2 * P].rearrange("p (c n) -> p c n", c=2))
                    ins.then_inc(k_copied.sem, 1)
                if k == 3:
                    act.wait_ge(ssub_ready.sem, ssub_ready.at(q, t))
                    for b in range(2):
                        r = slice(64 * b, 64 * b + 64)
                        ins = act.activation(ppad[r, :, b, :], ssub[r, :, :], ACT.Exp, scale=float(NW) ** -0.5)
                    ins.then_inc(p_ready.sem, 1)
                if k == 4:
                    act.wait_ge(pt_ready.sem, pt_ready.at(q, t))
                    act.copy(pT[:, 0:4, :].rearrange("p a b -> p (a b)"), BA[:, :]).then_inc(pt_copied0.sem, 1)

            def last_block(q, t, k):
                if k == 1:
                    act.wait_ge(w_ready.sem, w_ready.at(q, t))
                    if t == 1:
                        act.wait_ge(hb_ready.sem, hb_ready.at(q, 0))
                    act.activation(qv[:, 0:L], w[:, t, :], ACT.Square, accum_out=rs[:, 0, t, 0:1])\
                       .then_inc(ss_ready.sem, 1)
                if k == 4:
                    act.wait_ge(qt_ready.sem, qt_ready.at(q, t))
                    act.copy(qbT[:, :, :].rearrange("p a b -> p (a b)"), BA[:, 0:P].bitcast(BF16))\
                       .then_inc(qbt_copied.sem, 1)
                if k in (5, 6):
                    c = k - 5
                    act.wait_ge(hid_ready.sem, hid_ready.at(q, 2 * t + c))
                    if c == 0:
                        act.wait_ge(q1_steps.sem, q1_steps.at(q, 8 * t + 5))
                    act.activation(hid[:, c * HC:(c + 1) * HC], BB[:, 0:HC], ACT.Tanh, scale=rs[:, 0, t, 6:7])\
                       .then_inc(th2_ready.sem, 1)
                if k == 7:
                    act.wait_ge(hc_ready.sem, hc_ready.at(q, 2 * t + 1))
                    act.activation(qv[:, :], hid[:, :], ACT.Square, accum_out=rs[:, 1, t, 0:1])\
                       .then_inc(ss_ready.sem, 1)
                if k == 9:
                    act.wait_ge(hbt_ready.sem, hbt_ready.at(q, t))
                    src = BB[:, 0:HK * P // 2].bitcast(BF16)
                    act.copy(hbT[0:HR, HK - 1, :], src[0:HR, (HK - 1) * P:HK * P])
                    act.copy(hbT[:, 0:HK - 1, :].rearrange("p a b -> p (a b)"), src[:, 0:(HK - 1) * P])\
                       .then_inc(hbt_copied.sem, 1)

            run(act, {"A": attention_inputs, "X": exponentials, "R": router, "B": experts_start, "E": expert,
                      "C": second, "D": last_block})

        @block.vector
        def _(dve):
            step = Steps(dve, setup_steps, 0)
            dve.memset(vpad[:, :, :], 0.0)
            dve.memset(kmask[:, :, :, :], 0.0)
            dve.memset(ppad[:, :, :, :], 0.0)
            step.done(dve.memset(ones_pad[:, :, :], 0.0))
            for s in range(4):
                dve.memset(ones_pad[:, s, DH * s:DH * s + DH], 1.0)
            dve.memset(w3tail[HR:P, :], 0.0)
            dve.memset(wabs[:, :], 0.0).then_inc(dve_const.sem, 1)

            def attention_inputs(q, k):
                if k == 1:
                    s = Steps(dve, a_steps, q)
                    dve.wait_ge(xin_in.sem, xin_in.at(q))
                    dve.bn_stats(a_st[:, 0, :], xin[:, 0, :])
                    s.done(dve.bn_stats(a_st[:, 1, :], xin[:, 1, :]))
                    dve.memset(spare[:, :], 0.0)
                    dve.bn_aggr(a_mv[:, 0, :], a_st[:, 0, :])
                    s.done(dve.bn_aggr(a_mv[:, 1, :], a_st[:, 1, :]))
                    dve.tensor_scalar(a_ve[:, :], a_mv[:, :, 1], LN_EPS, None, ALU.add).then_inc(a_var.sem, 1)
                    s.end()
                if k == 2:
                    dve.wait_ge(a_rs.sem, a_rs.at(q))
                    if not first(q):
                        dve.wait_ge(xh_ready.sem, xh_ready.at(q - 1))
                    for t in range(T):
                        ins = dve.tensor_scalar(xn[:, t, :], xin[:, t, :], a_mv[:, t, 0:1], a_rstd[:, t:t + 1],
                                                ALU.subtract, ALU.mult)
                    ins.then_inc(xn_ready.sem, 1)
                    if not first(q):
                        dve.wait_ge(aug_in.sem, aug_in.at(q - 1, 7))
                    dve.wait_ge(ch_ready.sem, ch_ready.at(q))
                    dve.tensor_tensor(cl[:, :, :], ctxa[:, :, :], ch[:, :, :].bitcast(F32), ALU.subtract)\
                       .then_inc(cl_ready.sem, 1)
                    dve.wait_ge(xn_ready.sem, xn_ready.at(q))
                    dve.wait_ge(xh_ready.sem, xh_ready.at(q))
                    dve.tensor_tensor(xl[:, :, :], xn[:, :, :], xh[:, :, :].bitcast(F32), ALU.subtract)\
                       .then_inc(xl_ready.sem, 1)

            def maxima(q, t):
                dve.wait_ge(mt_ready.sem, mt_ready.at(q, t))
                if not first(q):
                    dve.wait_ge(max_in.sem, max_in.at(q - 1, 3))
                dve.tensor_copy(mT[:, t, :], S[0:32, 0, 0:L]).then_inc(mt_copied.sem, 1)

            def head_slot(q, k):
                if k < 16:
                    t, s, g0 = k // 8, k // 2 % 4, 2 * (k % 2)
                    dve.wait_ge(s1_ready.sem, s1_ready.at(q, k))
                    dst = mneg[:, t, :, :].rearrange("p c (g s) -> p g c s", g=4)[:, g0:g0 + 2, :, s]
                    dve.tensor_reduce(dst, S[:, :, :].rearrange("p v (c l) -> p v c l", c=2), AX.X, ALU.max,
                                      negate=True).then_inc(s1_read.sem, 1)
                if k in (7, 15):
                    t = k // 8
                    dve.wait_ge(s1_read.sem, s1_read.at(q, k))
                    dve.tensor_copy(mhl[:, t, :, 0, :].bitcast(F32R), mneg[:, t, :, :]).then_inc(max_steps.sem, 1)
                    dve.wait_ge(max_steps.sem, max_steps.at(q, t))
                    dve.tensor_tensor(mhl[:, t, :, 1, :].bitcast(F32R), mneg[:, t, :, :], mhl[:, t, :, 0, :],
                                      ALU.subtract).then_inc(mhl_ready.sem, 1)

            def heads_end(q, t):
                if t == 0:
                    dve.wait_ge(xres_in.sem, xres_in.at(q))
                    if not first(q):
                        dve.wait_ge(x1b_ready.sem, x1b_ready.at(q - 1))
                dve.wait_ge(pv_done.sem, pv_done.at(q, 4 * t + 3))
                dve.reciprocal(rden[:, :], OD[:, L:2 * L]).then_inc(fin_steps.sem, 1)
                dve.wait_ge(fin_steps.sem, fin_steps.at(q, 2 * t))
                dve.tensor_tensor(attn[:, :], rden[:, :], OD[:, 0:L], ALU.mult).then_inc(fin_steps.sem, 1)
                dve.wait_ge(fin_steps.sem, fin_steps.at(q, 2 * t + 1))
                dve.scalar_tensor_tensor(x1[:, t, :], attn[:, :], gamma_b[:, 0:1], xres[:, t, :], ALU.mult,
                                         ALU.add).then_inc(x1_ready.sem, 1)

            routing = [None]

            def router(q, k):
                if k == 0:
                    dve.wait_ge(x1_ready.sem, x1_ready.at(q, 1))
                    s = Steps(dve, b_steps, q)
                    dve.bn_stats(b_st[:, 0, :], x1[:, 0, :])
                    s.done(dve.bn_stats(b_st[:, 1, :], x1[:, 1, :]))
                    dve.memset(spare[:, :], 0.0)
                    dve.bn_aggr(b_mv[:, 0, :], b_st[:, 0, :])
                    s.done(dve.bn_aggr(b_mv[:, 1, :], b_st[:, 1, :]))
                    dve.tensor_scalar(b_ve[:, :], b_mv[:, :, 1], LN_EPS, None, ALU.add).then_inc(b_var.sem, 1)
                    s.end()
                if k == 1:
                    dve.wait_ge(b_rs.sem, b_rs.at(q))
                    for t in range(T):
                        ins = dve.tensor_scalar(y[:, t, :], x1[:, t, :], b_mv[:, t, 0:1], b_rstd[:, t:t + 1],
                                                ALU.subtract, ALU.mult)
                    ins.then_inc(y_ready.sem, 1)
                if k == 4:
                    dve.wait_ge(e_ready.sem, e_ready.at(q))
                    routing[0] = Steps(dve, route_steps, q)
                s = routing[0]
                if k == 4:
                    s.done(dve.tensor_scalar(sc_e[:, :, :], sc_e[:, :, :], 1.0, None, ALU.add))
                    s.done(dve.reciprocal(score[:, :, :], sc_e[:, :, :]))
                    s.done(dve.tensor_tensor(sel[:, :, :], score[:, :, :],
                                             bias_b[:, :].unsqueeze(1).to_broadcast([P, T, NE]), ALU.add))
                if k == 5:
                    of_j = sel[:, :, :].unsqueeze(2).to_broadcast([P, T, NE, NE])
                    of_i = sel[:, :, :].unsqueeze(3).to_broadcast([P, T, NE, NE])
                    s.done(dve.tensor_tensor(cmp_gt[:, :, :, :], of_j, of_i, ALU.is_gt))
                    s.done(dve.tensor_tensor(cmp_eq[:, :, :, :], of_j, of_i, ALU.is_equal))
                    s.done(dve.tensor_tensor(cmp_eq[:, :, :, :], cmp_eq[:, :, :, :],
                                             lower[:, :, :].unsqueeze(1).to_broadcast([P, T, NE, NE]), ALU.mult))
                    s.done(dve.tensor_tensor(cmp_gt[:, :, :, :], cmp_gt[:, :, :, :], cmp_eq[:, :, :, :], ALU.add))
                    s.done(dve.tensor_reduce(rank[:, :, :], cmp_gt[:, :, :, :], AX.X, ALU.add))
                if k == 6:
                    s.done(dve.scalar_tensor_tensor(cw[:, :, :], rank[:, :, :], TOP_K - 0.5, score[:, :, :],
                                                    ALU.is_lt, ALU.mult))
                    s.done(dve.tensor_reduce(csum[:, :], cw[:, :, :], AX.X, ALU.add))
                    s.done(dve.reciprocal(crec[:, :], csum[:, :]))
                    s.done(dve.scalar_tensor_tensor(cw[:, :, :], cw[:, :, :], 0.5,
                                                    crec[:, :].unsqueeze(2).to_broadcast([P, T, NE]),
                                                    ALU.mult, ALU.mult))
                    s.done(dve.tensor_copy(cwhl[:, :, 0, :].bitcast(F32R), cw[:, :, :]))
                    dve.tensor_tensor(cwhl[:, :, 1, :].bitcast(F32R), cw[:, :, :], cwhl[:, :, 0, :], ALU.subtract)\
                       .then_inc(cwhl_ready.sem, 1)
                    s.end()

            def experts_start(q, k):
                if k == 0:
                    if not first(q):
                        dve.wait_ge(gu_ready.sem, gu_ready.at(q - 1, NX - 1))
                    dve.wait_ge(yth_ready.sem, yth_ready.at(q))
                    dve.tensor_tensor(yT_l[:, :, :], yT, yT_h[:, :, :].bitcast(F32), ALU.subtract)\
                       .then_inc(ytl_ready.sem, 1)

            def hidden(q, n):
                if n == 0:
                    dve.wait_ge(g1_ready.sem, g1_ready.at(q, 0))
                else:
                    dve.wait_ge(g2_ready.sem, g2_ready.at(q, n - 1))
                if n >= 3:
                    dve.wait_ge(down_done.sem, down_done.at(q, n - 3))
                elif not first(q):
                    dve.wait_ge(down_done.sem, down_done.at(q - 1, NX - 1))
                up = GU[n % 2][:, L:2 * L]
                if n == 0:
                    ins = dve.scalar_tensor_tensor(h[0][:, :], g1[0][:, :], 0.5, up, ALU.mult, ALU.mult)
                else:
                    ins = dve.tensor_tensor(h[n % 3][:, :], g2[n % 2][:, :], up, ALU.mult)
                ins.then_inc(h_ready.sem, 1)

            def expert(q, n):
                dve.wait_ge(th_ready.sem, th_ready.at(q, n))
                dve.scalar_tensor_tensor(g1[n % 2][:, :], th[n % 2][:, :], 1.0, GU[n % 2][:, 0:L], ALU.add,
                                         ALU.mult).then_inc(g1_ready.sem, 1)

            def experts_end(q, _=0):
                dve.wait_ge(down_done.sem, down_done.at(q, NX - 1))
                dve.wait_ge(x1b_ready.sem, x1b_ready.at(q))
                dve.tensor_tensor(x2[:, :, :].rearrange("p a b -> p (a b)"),
                                  x1b[:, :, :].rearrange("p a b -> p (a b)"), Y[:, :], ALU.add)\
                   .then_inc(x2_ready.sem, 1)

            def second(q, t, k):
                if k == 0:
                    dve.wait_ge(x2_ready.sem, x2_ready.at(q))
                    s = Steps(dve, c_steps, q)
                    dve.bn_stats(c_st[:, 0, :], x2[:, 0, :])
                    s.done(dve.bn_stats(c_st[:, 1, :], x2[:, 1, :]))
                    dve.memset(spare[:, :], 0.0)
                    dve.bn_aggr(c_mv[:, 0, :], c_st[:, 0, :])
                    s.done(dve.bn_aggr(c_mv[:, 1, :], c_st[:, 1, :]))
                    dve.tensor_scalar(c_ve[:, :], c_mv[:, :, 1], LN_EPS, None, ALU.add)\
                       .then_inc(c_var.sem, 1)
                    s.end()
                if k == 1:
                    dve.wait_ge(c_rs.sem, c_rs.at(q))
                    dve.tensor_scalar(z[:, 1, :], x2[:, 1, :], c_mv[:, 1, 0:1], c_rstd[:, 1:2],
                                      ALU.subtract, ALU.mult)
                    dve.tensor_scalar(z[:, 0, :], x2[:, 0, :], c_mv[:, 0, 0:1], c_rstd[:, 0:1],
                                      ALU.subtract, ALU.mult).then_inc(z_ready.sem, 1)
                if k == 3:
                    dve.wait_ge(sc_ready.sem, sc_ready.at(q, t))
                    scores = BA[:, :].rearrange("p (h e) -> p h e", h=NH1)
                    dve.tensor_reduce(smx[:, :], scores, AX.X, ALU.max).then_inc(smax_steps.sem, 1)
                    dve.wait_ge(smax_steps.sem, smax_steps.at(q, t))
                    dve.tensor_tensor(ssub[:, :, :], scores, smx[:, :].unsqueeze(2).to_broadcast([P, NH1, D]),
                                      ALU.subtract).then_inc(ssub_ready.sem, 1)
                if k == 4:
                    dve.wait_ge(p_ready.sem, p_ready.at(q, t))
                    for b in range(2):
                        r = slice(64 * b, 64 * b + 64)
                        ins = dve.tensor_reduce(ssum[r, :], ppad[r, :, b, :], AX.X, ALU.add)
                    ins.then_inc(srec_steps.sem, 1)
                    dve.wait_ge(pt_ready.sem, pt_ready.at(q, t))
                    dve.tensor_copy(pT[:, 4:8, :].rearrange("p a b -> p (a b)"), BB[:, :])\
                       .then_inc(pt_copied1.sem, 1)
                if k == 5:
                    dve.wait_ge(srec_steps.sem, srec_steps.at(q, 2 * t))
                    dve.reciprocal(srec[:, :], ssum[:, :]).then_inc(srec_steps.sem, 1)
                    dve.wait_ge(srec_steps.sem, srec_steps.at(q, 2 * t + 1))
                    dve.wait_ge(av_ready.sem, av_ready.at(q, t))
                    dve.tensor_tensor(av[:, :].rearrange("p (h n) -> p h n", h=NH1),
                                      srec[:, :].unsqueeze(2).to_broadcast([P, NH1, NW]),
                                      BA[:, 0:L].rearrange("p (h n) -> p h n", h=NH1), ALU.mult)\
                       .then_inc(av_steps.sem, 1)
                    dve.wait_ge(av_steps.sem, av_steps.at(q, t))
                    dve.tensor_tensor(av[:, :], z[:, t, :], av[:, :], ALU.subtract).then_inc(u_ready.sem, 1)
                if k == 6:
                    dve.wait_ge(o_ready.sem, o_ready.at(q, t))
                    if t == 0 and not first(q):
                        dve.wait_ge(out_sent.sem, out_sent.at(q - 1))
                    dve.tensor_tensor(x3[:, t, :], x2[:, t, :], BA[:, L:2 * L], ALU.add).then_inc(x3_ready.sem, 1)

            def column(which, t, i):
                return rs[:, which, t, i:i + 1]

            def magnitudes(q, s, which, t, src, n):
                s.done(dve.tensor_reduce(column(which, t, 3), src, AX.X, ALU.max, apply_absolute_value=True))
                dve.wait_ge(ss_ready.sem, ss_ready.at(q, 2 * t + which))
                dve.tensor_scalar(column(which, t, 1), column(which, t, 0), 1.0 / n, RMS_EPS, ALU.mult, ALU.add)\
                   .then_inc(ms_ready.sem, 1)

            def quantise(q, s, which, t, src, n, dst, ready):
                c = [column(which, t, i) for i in range(8)]
                dve.wait_ge(rms_ready.sem, rms_ready.at(q, 2 * t + which))
                s.done(dve.tensor_scalar(c[4], c[3], c[2], QUANT_EPS, ALU.mult, ALU.max))
                s.done(dve.reciprocal(c[5], c[4]))
                s.done(dve.scalar_tensor_tensor(c[5], c[5], 127.0, c[2], ALU.mult, ALU.mult))
                s.done(dve.tensor_scalar(qv[:, 0:n], src, c[5], MAGIC, ALU.mult, ALU.add))
                dve.tensor_scalar(dst, qv[:, 0:n], MAGIC, 127.0, ALU.subtract, ALU.min).then_inc(ready.sem, 1)

            q1 = [None]
            q2 = [None]

            def last_block(q, t, k):
                if k == 0:
                    dve.wait_ge(x3_ready.sem, x3_ready.at(q, t))
                    dve.bn_stats(d_st[:, t, :], x3[:, t, :]).then_inc(d_steps.sem, 1)
                    dve.wait_ge(d_steps.sem, d_steps.at(q, 2 * t))
                    dve.memset(spare[:, :], 0.0)
                    dve.bn_aggr(d_mv[:, t, :], d_st[:, t, :]).then_inc(d_steps.sem, 1)
                    dve.wait_ge(d_steps.sem, d_steps.at(q, 2 * t + 1))
                    dve.tensor_scalar(d_ve[:, t:t + 1], d_mv[:, t, 1:2], LN_EPS, None, ALU.add)\
                       .then_inc(d_var.sem, 1)
                if k == 1:
                    dve.wait_ge(d_rs.sem, d_rs.at(q, t))
                    dve.tensor_scalar(w[:, t, :], x3[:, t, :], d_mv[:, t, 0:1], d_rstd[:, t:t + 1],
                                      ALU.subtract, ALU.mult).then_inc(w_ready.sem, 1)
                if k == 2:
                    dve.wait_ge(w_ready.sem, w_ready.at(q, t))
                    if t == 0:
                        q1[0] = Steps(dve, q1_steps, q)
                    else:
                        dve.wait_ge(hb_ready.sem, hb_ready.at(q, 0))
                    magnitudes(q, q1[0], 0, t, w[:, t, :], L)
                if k == 3:
                    s = q1[0]
                    quantise(q, s, 0, t, w[:, t, :], L, qb[:, :], qb_ready)
                    c = [column(0, t, i) for i in range(8)]
                    s.done(dve.tensor_scalar(c[6], c[4], 0.5 / 127.0, wmean[:, 0:1], ALU.mult, ALU.mult))
                    s.done(dve.tensor_scalar(c[7], c[4], 1.0 / 127.0, wmean[:, 1:2], ALU.mult, ALU.mult))
                    s.done(dve.tensor_tensor(c[7], c[6], c[7], ALU.mult))
                    if t == 1:
                        s.end()
                if k in (5, 6):
                    c = k - 5
                    part = hid[:, c * HC:(c + 1) * HC]
                    dve.wait_ge(th2_ready.sem, th2_ready.at(q, 2 * t + c))
                    dve.scalar_tensor_tensor(part, part, 1.0, BB[:, 0:HC], ALU.add, ALU.mult)\
                       .then_inc(hg_ready.sem, 1)
                    dve.wait_ge(hg_ready.sem, hg_ready.at(q, 2 * t + c))
                    dve.wait_ge(up_ready.sem, up_ready.at(q, 2 * t + c))
                    dve.scalar_tensor_tensor(part, part, column(0, t, 7), BA[:, 0:HC], ALU.mult, ALU.mult)\
                       .then_inc(hc_ready.sem, 1)
                if k == 7:
                    dve.wait_ge(hc_ready.sem, hc_ready.at(q, 2 * t + 1))
                    if t == 0:
                        q2[0] = Steps(dve, q2_steps, q)
                    magnitudes(q, q2[0], 1, t, hid[:, :], HID)
                if k == 8:
                    s = q2[0]
                    quantise(q, s, 1, t, hid[:, :], HID, hb[:, :], hb_ready)
                    s.done(dve.tensor_scalar(column(1, t, 6), column(1, t, 4), 1.0 / 127.0, wmean[:, 2:3],
                                             ALU.mult, ALU.mult))
                    if t == 1:
                        s.end()
                if k == 10:
                    dve.wait_ge(dn_ready.sem, dn_ready.at(q, t))
                    dve.scalar_tensor_tensor(x3[:, t, :], BA[:, 0:L], column(1, t, 6), x3[:, t, :], ALU.mult,
                                             ALU.add).then_inc(xo_ready.sem, 1)

            def setup_weights():
                for c, (e0, ne) in enumerate(chunks):
                    dve.wait_ge(split_h.sem, c + 1)
                    hi = wgu_h[:, e0:e0 + ne, :, :, :].rearrange("p a b c d -> p (a b c d)").bitcast(F32)
                    dve.tensor_tensor(wgu_l[:, e0:e0 + ne, :, :, :].rearrange("p a b c d -> p (a b c d)"),
                                      stage[c % 2][:, 0:ne * GUW], hi, ALU.subtract).then_inc(split_l.sem, 1)
                dve.wait_ge(ident_ok.sem, 1)
                dve.tensor_copy(ident_bf[:, :], ident[:, :])
                dve.tensor_tensor(pick[:, :, :],
                                  ident[0:2 * NE, 0:NE].unsqueeze(2).to_broadcast([2 * NE, NE, P]),
                                  ident[0:2 * NE, NE:2 * NE].unsqueeze(2).to_broadcast([2 * NE, NE, P]), ALU.add)
                dve.wait_ge(l1w_in.sem, 64)
                dve.tensor_reduce(wabs[:, 0:1], w1s, AX.X, ALU.add, apply_absolute_value=True)
                dve.tensor_reduce(wabs[:, 1:2], w2s, AX.X, ALU.add, apply_absolute_value=True)
                dve.tensor_reduce(wabs[:, 2:3], w3s, AX.X, ALU.add, apply_absolute_value=True)
                dve.tensor_reduce(wabs[:, 3:4], w3tail[:, :], AX.X, ALU.add, apply_absolute_value=True)\
                   .then_inc(wsum_ready.sem, 1)
                dve.wait_ge(wsum_done.sem, 1)
                step.done(dve.tensor_copy(wmean[:, :], GU[0][:, 0:4]))
                step.done(dve.tensor_tensor(wmean[:, 2:3], wmean[:, 2:3], wmean[:, 3:4], ALU.add))
                step.done(dve.tensor_scalar(wmean[:, 0:3], wmean[:, 0:3], 1.0 / (HID * L), QUANT_EPS,
                                            ALU.mult, ALU.max))
                step.done(dve.reciprocal(wscale[:, 0:3], wmean[:, 0:3]))
                for n, src, dst in ((0, w1s, w1q[:, :, :].rearrange("p a b -> p (a b)")),
                                    (1, w2s, w2q[:, :, :].rearrange("p a b -> p (a b)")),
                                    (2, w3s, w3q[:, 0:HK - 1, :].rearrange("p a b -> p (a b)")),
                                    (2, w3tail[:, :], w3q[:, HK - 1, :])):
                    step.done(dve.tensor_scalar(src, src, wscale[:, n:n + 1], MAGIC, ALU.mult, ALU.add))
                    step.done(dve.tensor_scalar(src, src, MAGIC, 1.0, ALU.subtract, ALU.min))
                    step.done(dve.tensor_scalar(dst, src, -1.0, None, ALU.max))
                dve.tensor_copy(wabs[:, 0:1], wabs[:, 0:1]).then_inc(dve_const.sem, 1)

            setup_weights()
            run(dve, {"A": attention_inputs, "H": head_slot, "M": maxima, "F": heads_end, "R": router, "B": experts_start, "E": expert, "Y": hidden, "T": experts_end,
                      "C": second, "D": last_block})

        @block.tensor
        def _(pe):
            pe.wait_ge(ident_ok.sem, 1)
            pe.wait_ge(wsum_ready.sem, 1)
            pe.matmul(GU[0][:, 0:4], ones[:, :], wabs[:, :], start=True, stop=True).then_inc(wsum_done.sem, 1)

            def attention_inputs(q, k):
                if k != 0:
                    return
                pe.wait_ge(ctxa_in.sem, ctxa_in.at(q))
                if not first(q):
                    pe.wait_ge(cwt_copied.sem, cwt_copied.at(q - 1))
                for t in range(T):
                    for c in range(2):
                        ins = pe.transpose(Sa[:, (2 * t + c) * P:(2 * t + c + 1) * P],
                                           ctxa[:, t, c * P:(c + 1) * P], ident[:, :])
                ins.then_inc(vt_ready.sem, 1)

            def values(q, k):
                m = (k - 11) // 2
                t, s = m // 4, m % 4
                pe.wait_ge(exp_ready.sem, exp_ready.at(q, 2 * m + 1))
                if m == 4:
                    pe.wait_ge(x1_ready.sem, x1_ready.at(q, 0))
                elif m == 0 and not first(q):
                    pe.wait_ge(x1_ready.sem, x1_ready.at(q - 1, 1))
                if m == 0:
                    pe.wait_ge(vpad_ready.sem, vpad_ready.at(q))
                for c in range(2):
                    for kind in range(2):
                        for g in range(4):
                            lhs = (vpad[:, 2 * t + c, 136 * s - 8 * s + 32 * g:136 * s - 8 * s + 32 * g + 32]
                                   if kind == 0 else ones_pad[:, s, :])
                            ins = pe.matmul(OD[32 * g:32 * g + 32, kind * L:(kind + 1) * L], lhs,
                                            E[m % 2][:, g, c, :], start=(s == 0 and c == 0 and kind == 0),
                                            stop=(s == 3 and c == 1), skip_group_check=True)
                ins.then_inc(pv_done.sem, 1)

            def maxima(q, t):
                pe.wait_ge(mhl_ready.sem, mhl_ready.at(q, t))
                if t == 1:
                    pe.wait_ge(exp_ready.sem, exp_ready.at(q, 6))
                for c in range(2):
                    ins = pe.transpose(S[0:32, 0, c * P:(c + 1) * P],
                                       mhl[:, t, c, :, :].rearrange("p a b -> p (a b)"), ident[:, :])
                ins.then_inc(mt_ready.sem, 1)

            def head_slot(q, k):
                if k < 16:
                    t, s, g0 = k // 8, k // 2 % 4, 2 * (k % 2)
                    if k == 0:
                        pe.wait_ge(vpad_ready.sem, vpad_ready.at(q))
                        pe.wait_ge(aug_in.sem, aug_in.at(q, 7))
                    elif k == 8:
                        pe.wait_ge(mt_copied.sem, mt_copied.at(q, 0))
                    elif k < 10:
                        pe.wait_ge(s1_read.sem, s1_read.at(q, k - 1))
                    else:
                        pe.wait_ge(exp_ready.sem, exp_ready.at(q, k - 10))
                    for c in range(2):
                        for v in range(2):
                            r = slice(32 * (g0 + v), 32 * (g0 + v) + 24)
                            ins = pe.matmul(S[:, v, c * L:(c + 1) * L], qaug[r, s, t, c * P:(c + 1) * P],
                                            kaug[r, s, t, :], start=True, stop=True)
                    ins.then_inc(s1_ready.sem, 1)

            def transposed_scores(q, k):
                step = k - 9
                t, s, g0 = step // 8, step // 2 % 4, 2 * (step % 2)
                if step % 8 == 0:
                    pe.wait_ge(max_in.sem, max_in.at(q, 2 * t + 1))
                if k < 16:
                    pe.wait_ge(s1_read.sem, s1_read.at(q, k))
                elif k == 16:
                    pe.wait_ge(mt_copied.sem, mt_copied.at(q, 1))
                else:
                    pe.wait_ge(exp_ready.sem, exp_ready.at(q, step - 1))
                for c in range(2):
                    for v in range(2):
                        r = slice(32 * (g0 + v), 32 * (g0 + v) + 26)
                        ins = pe.matmul(S[:, v, c * L:(c + 1) * L], kaug[r, s, t, c * P:(c + 1) * P],
                                        qaug[r, s, t, :], start=True, stop=True)
                ins.then_inc(s2_ready.sem, 1)

            def router(q, k):
                if k == 1:
                    pe.wait_ge(y_ready.sem, y_ready.at(q))
                    if first(q):
                        pe.wait_ge(const_in.sem, 16 * 11)
                    for t in range(T):
                        for c in range(2):
                            ins = pe.transpose(S[:, 0, c * L + t * P:c * L + (t + 1) * P],
                                               y[:, t, c * P:(c + 1) * P], ident[:, :])
                    ins.then_inc(yt_ready.sem, 1)
                if k == 3:
                    pe.wait_ge(yt_copied.sem, yt_copied.at(q))
                    for t in range(T):
                        for c in range(2):
                            ins = pe.matmul(S[:, 1, t * NE:(t + 1) * NE], yT[:, c, t * P:(t + 1) * P], gw[:, c, :],
                                            start=(c == 0), stop=(c == 1))
                    ins.then_inc(logits_ready.sem, 1)
                if k == 7:
                    pe.wait_ge(cwhl_ready.sem, cwhl_ready.at(q))
                    for t in range(T):
                        ins = pe.transpose(S[0:2 * NE, 1, t * P:(t + 1) * P],
                                           cwhl[:, t, :, :].rearrange("p a b -> p (a b)"), ident[:, :])
                    ins.then_inc(cwt_ready.sem, 1)

            def experts_start(q, k):
                if k >= 1:
                    for r in (2 * (k - 1), 2 * (k - 1) + 1):
                        if r == 0:
                            pe.wait_ge(cwt_copied.sem, cwt_copied.at(q))
                            if first(q):
                                pe.wait_ge(dve_const.sem, 2)
                                pe.wait_ge(split_l.sem, len(chunks))
                                pe.wait_ge(wd_in.sem, 16)
                            else:
                                pe.wait_ge(h_ready.sem, h_ready.at(q - 1, NX - 1))
                        if r >= 2:
                            pe.wait_ge(bc_copied.sem, bc_copied.at(q, r - 2))
                        for v in range(2):
                            ins = pe.matmul(GU[r % 2][:, v * L:(v + 1) * L], pick[:, 2 * r + v, :], cwT[:, :],
                                            start=True, stop=True)
                        ins.then_inc(bc_ready.sem, 1)

            def down(q, n):
                pe.wait_ge(h_ready.sem, h_ready.at(q, n))
                if n == 0 and not first(q):
                    pe.wait_ge(x2_ready.sem, x2_ready.at(q - 1))
                for t in range(T):
                    ins = pe.matmul(Y[:, t * L:(t + 1) * L], h[n % 3][:, t * P:(t + 1) * P], wd[:, n, :],
                                    start=(n == 0 and t == 0), stop=(n == NX - 1), skip_group_check=True)
                ins.then_inc(down_done.sem, 1)

            def expert(q, n):
                if n < 2:
                    pe.wait_ge(bc_copied.sem, bc_copied.at(q, 6 + n))
                    if n == 0:
                        pe.wait_ge(ytl_ready.sem, ytl_ready.at(q))
                else:
                    pe.wait_ge(h_ready.sem, h_ready.at(q, n - 2))
                for half in range(2):
                    parts = [(c, a, b) for c in range(2) for a, b in ((wgu_h, yT_h), (wgu_h, yT_l), (wgu_l, yT_h))]
                    for i, (c, a, b) in enumerate(parts):
                        ins = pe.matmul(GU[n % 2][:, half * L:(half + 1) * L], a[:, n, c, half, :], b[:, c, :],
                                        start=(i == 0), stop=(i == len(parts) - 1))
                ins.then_inc(gu_ready.sem, 1)

            def second(q, t, k):
                if k == 2:
                    if t == 0:
                        pe.wait_ge(z_ready.sem, z_ready.at(q))
                        pe.wait_ge(ctxb_in.sem, ctxb_in.at(q))
                        if not first(q):
                            pe.wait_ge(xo_ready.sem, xo_ready.at(q - 1, 1))
                    else:
                        pe.wait_ge(x3_ready.sem, x3_ready.at(q, 0))
                    for c in range(2):
                        pe.matmul(BA[:, c * P:(c + 1) * P], z[:, t, c * P:(c + 1) * P], proj[:, 0, :],
                                  start=True, stop=True)
                    pe.matmul(BA[:, L:2 * L], proj[:, 2, :], ctxb[:, t, :], start=True, stop=True)\
                      .then_inc(qv_ready.sem, 1)
                    for c in range(2):
                        ins = pe.matmul(BB[:, c * P:(c + 1) * P], ctxb[:, t, c * P:(c + 1) * P],
                                        proj[:, 1, :], start=True, stop=True)
                    ins.then_inc(k_ready.sem, 1)
                if k == 3:
                    pe.wait_ge(v_copied.sem, v_copied.at(q, t))
                    pe.wait_ge(k_copied.sem, k_copied.at(q, t))
                    for c in range(2):
                        for b in range(2):
                            ins = pe.matmul(BA[64 * b:64 * b + 64, c * L:(c + 1) * L]
                                            .rearrange("p (j e) -> p j e", j=4),
                                            qT[:, c * P + 64 * b:c * P + 64 * b + 64],
                                            kmask[:, c, :, 64 * b:64 * b + 64], start=True, stop=True)
                    ins.then_inc(sc_ready.sem, 1)
                if k == 4:
                    pe.wait_ge(p_ready.sem, p_ready.at(q, t))
                    for n in range(NH1):
                        ins = pe.transpose((BA, BB)[n // 4][:, n % 4 * P:(n % 4 + 1) * P],
                                           ppad[:, n, :, :].rearrange("p a b -> p (a b)"), ident[:, :])
                    ins.then_inc(pt_ready.sem, 1)
                if k == 5:
                    pe.wait_ge(pt_copied0.sem, pt_copied0.at(q, t))
                    pe.wait_ge(pt_copied1.sem, pt_copied1.at(q, t))
                    for n in range(NH1):
                        ins = pe.matmul(BA[:, n * NW:(n + 1) * NW], pT[:, n, :], v1[:, n * NW:(n + 1) * NW],
                                        start=True, stop=True)
                    ins.then_inc(av_ready.sem, 1)
                if k == 6:
                    pe.wait_ge(u_ready.sem, u_ready.at(q, t))
                    pe.matmul(BA[:, L:2 * L], proj[:, 3, :], av[:, :], start=True, stop=True)\
                      .then_inc(o_ready.sem, 1)

            def last_block(q, t, k):
                if k == 4:
                    pe.wait_ge(qb_ready.sem, qb_ready.at(q, t))
                    if t == 0:
                        pe.wait_ge(x3_ready.sem, x3_ready.at(q, 1))
                    else:
                        pe.wait_ge(xo_ready.sem, xo_ready.at(q, 0))
                    tr = BA[:, 0:P].bitcast(BF16)
                    for c in range(2):
                        ins = pe.transpose(tr[:, c * P:(c + 1) * P], qb[:, c * P:(c + 1) * P], ident_bf[:, :])
                    ins.then_inc(qt_ready.sem, 1)
                if k in (5, 6):
                    c = k - 5
                    if c == 0:
                        pe.wait_ge(qbt_copied.sem, qbt_copied.at(q, t))
                    else:
                        pe.wait_ge(hg_ready.sem, hg_ready.at(q, 2 * t))
                    for i in range(2):
                        ins = pe.matmul(BB[:, 0:HC], qbT[:, i, :], w1q[:, i, c * HC:(c + 1) * HC],
                                        start=(i == 0), stop=(i == 1))
                    ins.then_inc(hid_ready.sem, 1)
                    if c == 1:
                        pe.wait_ge(hc_ready.sem, hc_ready.at(q, 2 * t))
                    for i in range(2):
                        ins = pe.matmul(BA[:, 0:HC], qbT[:, i, :], w2q[:, i, c * HC:(c + 1) * HC],
                                        start=(i == 0), stop=(i == 1))
                    ins.then_inc(up_ready.sem, 1)
                if k == 9:
                    pe.wait_ge(hb_ready.sem, hb_ready.at(q, t))
                    tr = BB[:, 0:HK * P // 2].bitcast(BF16)
                    for c in range(HK):
                        n = P if c < HK - 1 else HR
                        ins = pe.transpose(tr[0:n, c * P:(c + 1) * P], hb[:, c * P:c * P + n], ident_bf[:, :])
                    ins.then_inc(hbt_ready.sem, 1)
                if k == 10:
                    pe.wait_ge(hbt_copied.sem, hbt_copied.at(q, t))
                    for c in range(HK):
                        n = P if c < HK - 1 else HR
                        ins = pe.matmul(BA[:, 0:L], hbT[0:n, c, :], w3q[0:n, c, :], start=(c == 0),
                                        stop=(c == HK - 1))
                    ins.then_inc(dn_ready.sem, 1)

            run(pe, {"A": attention_inputs, "H": head_slot, "M": maxima, "X": transposed_scores, "V": values, "R": router,
                     "B": experts_start, "E": expert, "Z": down,
                     "C": second, "D": last_block})


_INS = ["x", "ctx", "gamma", "gate_w", "bias", "w_gu", "w_d", "wq", "wk", "wv", "wo", "w1", "w2", "w3"]


def kernel(x, ctx_2048, L0_xattn_gamma, L0_ffn_gate_w, L0_ffn_expert_bias, L0_ffn_w_gate, L0_ffn_w_up,
           L0_ffn_w_down, L0_ffn_sw_gate, L0_ffn_sw_up, L0_ffn_sw_down, L1_xattn_W_q, L1_xattn_W_k, L1_xattn_W_v,
           L1_xattn_W_o, L1_ffn_w1, L1_ffn_w2, L1_ffn_w3):
    import numpy as np
    import concourse.bacc as _bacc
    from concourse.bass_utils import run_bass_kernel_spmd as _run

    f = np.asarray
    gate = np.concatenate([f(L0_ffn_sw_gate)[None], f(L0_ffn_w_gate)])
    up = np.concatenate([f(L0_ffn_sw_up)[None], f(L0_ffn_w_up)])
    down = np.concatenate([f(L0_ffn_sw_down)[None], f(L0_ffn_w_down)])
    nx, hidden, width = gate.shape
    gu = np.stack([gate, up])
    gu = gu.reshape(2, nx, hidden, width // 128, 128).transpose(4, 1, 3, 0, 2)

    def chunked(a):
        return a.reshape(a.shape[0], -1, 128).transpose(2, 1, 0)

    arrays = {
        "x": f(x), "ctx": f(ctx_2048), "gamma": f(L0_xattn_gamma).reshape(1),
        "gate_w": chunked(f(L0_ffn_gate_w)), "bias": f(L0_ffn_expert_bias),
        "w_gu": gu.reshape(128, -1), "w_d": down.transpose(2, 0, 1),
        "wq": f(L1_xattn_W_q).T, "wk": f(L1_xattn_W_k).T, "wv": f(L1_xattn_W_v).T, "wo": f(L1_xattn_W_o).T,
        "w1": chunked(f(L1_ffn_w1)), "w2": chunked(f(L1_ffn_w2)), "w3": f(L1_ffn_w3).T,
    }
    arrays = {k: np.ascontiguousarray(a) for k, a in arrays.items()}
    nc = _bacc.Bacc("TRN2", target_bir_lowering=False, num_devices=1, dynamic_dma_scratch_size=1024)
    args = [nc.dram_tensor(f"in_{n}", arrays[n].shape, mybir.dt.from_np(arrays[n].dtype), kind="ExternalInput").ap()
            for n in _INS]
    out = nc.dram_tensor("out_0", arrays["x"].shape, F32, kind="ExternalOutput").ap()
    program(nc, *args, out)
    r = _run(nc, [{f"in_{n}": arrays[n] for n in _INS}], core_ids=[0])
    return r.results[0]["out_0"]
```

```python
from contextlib import ExitStack

import concourse.bass as bass
from concourse import mybir

F32 = mybir.dt.float32
F32R = mybir.dt.float32r
BF16 = mybir.dt.bfloat16
ALU = mybir.AluOpType
ACT = mybir.ActivationFunctionType
AX = mybir.AxisListType

P = 128
MAGIC = 1.5 * 2.0**23
LN_EPS = 1e-5
RMS_EPS = 1e-6
QUANT_EPS = 1e-5
TOP_K = 4


class Signal:

    def __init__(self, sem, per, unit=1):
        self.sem, self.per, self.unit = sem, per, unit

    def at(self, q, k=0):
        return (q * self.per + (k + 1)) * self.unit


class Steps:

    def __init__(self, eng, chain, q, k=0):
        self.eng, self.chain, self.q, self.k = eng, chain, q, k

    def done(self, ins):
        ins.then_inc(self.chain.sem, 1)
        self.eng.wait_ge(self.chain.sem, self.chain.at(self.q, self.k))
        self.k += 1

    def end(self):
        assert self.k == self.chain.per, (self.k, self.chain.per)


def first(q):
    return isinstance(q, int) and q == 0


LAST_OF = {"E": 13, "Y": 12, "Z": 11, "D": (1, 4)}
PLAN = """
    D1.4 K0 R0 D1.5 Y12 E13 H0 D1.6 Y13 D1.7 E14 Z11 Z12 R1 D1.8 R2 Y14 H1 R3 Z13 R4 R5 E15 D1.9 E16
    H2 Y15 D1.10 Y16 Z14 H3 Z15 Z16 R6 T0 B0 H4 C0.0 R7 B1 H5 C0.1 B2 B3 H6 C0.2 H7 B4 C0.3 M0 E0 H8
    Y0 E1 C0.4 H9 Y1 E2 A0 Z0 C0.5 Y2 X9 E3 H10 C0.6 Y3 E4 X10 C1.2 A1 H11 V11 Z1 X11 Y4 C1.3 Z2 H12
    E5 X12 C1.4 Z3 H13 C1.5 A2 X13 E6 H14 C1.6 D0.0 Z4 X14 Y5 V13 Y6 D0.1 D0.2 H15 Z5 Z6 X15 D0.3 E7
    M1 D1.0 D0.4 A3 V15 D0.5 X16 Y7 E8 D0.6 X17 V17 Z7 G0 D0.7 Y8 F0 D0.8 X18 E9 X19 E10 X20 V19 X21
    D1.1 V21 Y9 D1.2 X22 D0.9 Y10 Z8 D1.3 X23 E11 X24 D0.10 P0 Y11 V23 V25 Z9 G1 F1 E12 Z10
"""


def body_plan():
    return [(item[0], *(int(n) for n in item[1:].split("."))) for item in PLAN.split()]


def ahead_of(item):
    if item[0] == "D" and item[1:] >= LAST_OF["D"]:
        return -2
    if item[0] in "CDT" or item[0] in LAST_OF and item[1] >= LAST_OF[item[0]]:
        return -1
    return {"R": 0, "B": 0, "E": 0, "Y": 0, "Z": 0, "A": 2, "P": 2}.get(item[0], 1)


def prologue_plan(plan):
    after = [("H", 1), ("H", 2), ("H", 4), ("H", 5), ("H", 7), ("X", 16), ("X", 18), ("X", 20), ("X", 22)]
    items = []
    for item in plan:
        items.append(item)
        if item in after:
            items.append(("W", after.index(item)))
    return items


def program(nc, x, ctx, gamma, gate_w, bias, w_gu, w_d, wq, wk, wv, wo, w1, w2, w3, out):
    B, D, L = x.shape
    QB = 4
    NQ = B // QB
    T = 2
    H0 = 8
    DH = D // H0
    NE = gate_w.shape[2]
    NX = NE + 1
    HID = w1.shape[2]
    HC = HID // 2
    HK = (HID + P - 1) // P
    HR = HID - (HK - 1) * P
    NH1 = 8
    NW = L // NH1
    assert T * P == QB * D and L == 2 * P and P == 2 * D and DH == 8

    x_q = x.rearrange("(q t b) d l -> q (b d) t l", t=T, b=2)
    c_q = ctx.rearrange("(q t b) d l -> q (b d) t l", t=T, b=2)
    o_q = out.rearrange("(q t b) d l -> q (b d) t l", t=T, b=2)

    rows = nc.dram_tensor("rows", (2, 16, 3, DH, T * L), F32).ap()

    with ExitStack() as stack:
        def sb(name, shape, dt=F32):
            return stack.enter_context(nc.sbuf_tensor(name, shape, dt))

        def sig(name, per=1, unit=1):
            return Signal(stack.enter_context(nc.semaphore(name)), per, unit)

        wgu_h = sb("wgu_h", [P, NX, 2, 2, P], F32R)
        wgu_l = sb("wgu_l", [P, NX, 2, 2, P], F32R)
        wd = sb("wd", [P, NX, L])
        gw = sb("gw", [P, 2, NE])
        bias_b = sb("bias_b", [P, NE])
        gamma_b = sb("gamma_b", [P, 1])
        proj = sb("proj", [P, 4, P])
        w1q = sb("w1q", [P, 2, HID], BF16)
        w2q = sb("w2q", [P, 2, HID], BF16)
        w3q = sb("w3q", [P, HK, L], BF16)
        wabs = sb("wabs", [P, 4])
        wmean = sb("wmean", [P, 4])
        wscale = sb("wscale", [P, 4])
        ident = sb("ident", [P, P])
        ident_bf = sb("ident_bf", [P, P], BF16)
        ones = sb("ones", [P, P])
        take = sb("take", [P, 2, 16 + P])
        lower = sb("lower", [P, NE, NE])
        pick = sb("pick", [2 * NE, NE, P], F32R)
        mhalf = sb("mhalf", [P, T])
        spare = sb("spare", [P, 1])

        xin = sb("xin", [P, T, L])
        ctxa = sb("ctxa", [P, T, L])
        xres = sb("xres", [P, T, L])
        a_st = sb("a_st", [P, T, 6])
        a_mv = sb("a_mv", [P, T, 2])
        a_ve = sb("a_ve", [P, T])
        a_rstd = sb("a_rstd", [P, T])
        qaug = sb("qaug", [P, 4, T, L], F32R)
        kaug = sb("kaug", [P, 4, T, L], F32R)
        vpad = sb("vpad", [P, T * 2, 4 * (16 + P)])
        mneg = sb("mneg", [P, T, 2, 16])
        mhl = sb("mhl", [P, T, 2, 2, 16])
        mT = sb("mT", [32, L])
        E = [sb(f"E{i}", [P, 4, 2, L]) for i in range(2)]
        od_sb = sb("od_sb", [P, 2 * L])
        rden, attn = (od_sb[:, i * L:(i + 1) * L] for i in range(2))
        x1 = sb("x1", [P, T, L])
        x1b = sb("x1b", [P, T, L])
        b_st = sb("b_st", [P, T, 6])
        b_mv = sb("b_mv", [P, T, 2])
        b_ve = sb("b_ve", [P, T])
        b_rstd = sb("b_rstd", [P, T])
        yT_h = sb("yT_h", [P, 2, T * P], F32R)
        yT_l = sb("yT_l", [P, 2, T * P], F32R)
        sc_e = sb("sc_e", [P, T, NE])
        score = sb("score", [P, T, NE])
        sel = sb("sel", [P, T, NE])
        rank = sb("rank", [P, T, NE])
        cw = sb("cw", [P, T, NE])
        csum = sb("csum", [P, T])
        crec = sb("crec", [P, T])
        cwhl = sb("cwhl", [P, T, 2, NE])
        cwT = sb("cwT", [2 * NE, T * P], F32R)
        cwb = sb("cwb", [P, NE, T * P])
        th_all = sb("th_all", [P, 2 * L])
        g1_all = sb("g1_all", [P, 2 * L])
        th, g1 = ([a[:, i * L:(i + 1) * L] for i in range(2)] for a in (th_all, g1_all))
        g2 = [sb(f"g2_{i}", [P, L]) for i in range(2)]
        h = [sb(f"h{i}", [P, L]) for i in range(3)]
        ctxb = sb("ctxb", [P, T, L])
        x2 = sb("x2", [P, T, L])
        c_st = sb("c_st", [P, T, 6])
        c_mv = sb("c_mv", [P, T, 2])
        c_ve = sb("c_ve", [P, T])
        c_rstd = sb("c_rstd", [P, T])
        z = sb("z", [P, T, L])
        qT = sb("qT", [P, 2 * P])
        kmask = sb("kmask", [P, 2, 4, P])
        v1 = sb("v1", [P, L])
        smx = sb("smx", [P, NH1])
        ppad = sb("ppad", [P, NH1, 2, D])
        ssum = sb("ssum", [P, NH1])
        srec = sb("srec", [P, NH1])
        x3 = sb("x3", [P, T, L])
        d_st = sb("d_st", [P, T, 6])
        d_mv = sb("d_mv", [P, T, 2])
        d_ve = sb("d_ve", [P, T])
        d_rstd = sb("d_rstd", [P, T])
        rs = sb("rs", [P, 2, T, 8])
        qb = sb("qb", [P, L], BF16)
        qbT = sb("qbT", [P, 2, P], BF16)
        hb = sb("hb", [P, HID], BF16)
        hbT = sb("hbT", [P, HK, P], BF16)
        late = sb("late", [P, NH1 * P + NH1 * D + L])

        S = stack.enter_context(nc.psum_tensor("S", [P, 2, 512], F32))
        BA = stack.enter_context(nc.psum_tensor("BA", [P, 512], F32))
        BB = stack.enter_context(nc.psum_tensor("BB", [P, 512], F32))
        OD = stack.enter_context(nc.psum_tensor("OD", [P, 512], F32))
        GU = [stack.enter_context(nc.psum_tensor(f"GU{i}", [P, 512], F32)) for i in range(2)]
        Y = stack.enter_context(nc.psum_tensor("Y", [P, 512], F32))

        const_in = sig("const_in", 1, 16)
        l1w_in = sig("l1w_in", 1, 16)
        gu_in = [sig(f"gu_in{i}", 1, 16) for i in range(2)]
        wd_in = sig("wd_in", 1, 16)
        zeroed = sig("zeroed")
        ident_ok = sig("ident_ok")
        pool_setup = sig("pool_setup", 12)
        setup_steps = sig("setup_steps", 64)
        wsum_ready = sig("wsum_ready")
        wsum_done = sig("wsum_done")
        split_h = sig("split_h", 8)
        split_l = sig("split_l", 8)
        dve_const = sig("dve_const", 1)
        xin_in = sig("xin_in", 1, 16)
        ctxa_in = sig("ctxa_in", 2, 16)
        xres_in = sig("xres_in", 1, 16)
        ctxb_in = sig("ctxb_in", 1, 16)
        rows_out = sig("rows_out", 6, 16)
        aug_in = sig("aug_in", 8, 16)
        max_in = sig("max_in", 4, 16)
        out_sent = sig("out_sent", 1, 16)
        a_steps = sig("a_steps", 2)
        a_var = sig("a_var")
        a_rs = sig("a_rs")
        xn_ready = sig("xn_ready")
        xh_ready = sig("xh_ready")
        ch_ready = sig("ch_ready")
        xl_ready = sig("xl_ready")
        cl_ready = sig("cl_ready")
        vt_ready = sig("vt_ready")
        vpad_ready = sig("vpad_ready")
        s1_ready = sig("s1_ready", 16)
        s1_read = sig("s1_read", 16)
        max_steps = sig("max_steps", 2)
        mhl_ready = sig("mhl_ready", 2)
        mt_ready = sig("mt_ready", 2)
        mt_copied = sig("mt_copied", 2)
        s2_ready = sig("s2_ready", 16)
        exp_ready = sig("exp_ready", 16)
        pv_done = sig("pv_done", 8)
        od_copied = sig("od_copied", 2)
        od_taken = sig("od_taken", 2)
        fin_steps = sig("fin_steps", 4)
        x1_ready = sig("x1_ready", 2)
        x1b_ready = sig("x1b_ready")
        b_steps = sig("b_steps", 2)
        b_var = sig("b_var")
        b_rs = sig("b_rs")
        y_ready = sig("y_ready")
        yt_ready = sig("yt_ready")
        yt_copied = sig("yt_copied")
        yth_ready = sig("yth_ready")
        ytl_ready = sig("ytl_ready")
        logits_ready = sig("logits_ready")
        e_ready = sig("e_ready")
        route_steps = sig("route_steps", 13)
        cwhl_ready = sig("cwhl_ready")
        cwt_ready = sig("cwt_ready")
        cwt_copied = sig("cwt_copied")
        bc_ready = sig("bc_ready", 8)
        bc_copied = sig("bc_copied", 8)
        gu_ready = sig("gu_ready", NX)
        th_ready = sig("th_ready", NX)
        g1_ready = sig("g1_ready", NX)
        g2_ready = sig("g2_ready", NX - 1)
        h_ready = sig("h_ready", NX)
        down_done = sig("down_done", NX)
        x2_ready = sig("x2_ready")
        c_steps = sig("c_steps", 2)
        c_var = sig("c_var")
        c_rs = sig("c_rs")
        z_ready = sig("z_ready")
        qv_ready = sig("qv_ready", 2)
        k_ready = sig("k_ready", 2)
        qt_copied = sig("qt_copied", 2)
        k_copied = sig("k_copied", 2)
        v_copied = sig("v_copied", 2)
        sc_ready = sig("sc_ready", 2)
        smax_steps = sig("smax_steps", 2)
        ssub_ready = sig("ssub_ready", 2)
        p_ready = sig("p_ready", 2)
        srec_steps = sig("srec_steps", 4)
        pt_ready = sig("pt_ready", 2)
        pt_copied0 = sig("pt_copied0", 2)
        pt_copied1 = sig("pt_copied1", 2)
        av_ready = sig("av_ready", 2)
        av_steps = sig("av_steps", 2)
        u_ready = sig("u_ready", 2)
        o_ready = sig("o_ready", 2)
        x3_ready = sig("x3_ready", 2)
        d_steps = sig("d_steps", 4)
        d_var = sig("d_var", 2)
        d_rs = sig("d_rs", 2)
        w_ready = sig("w_ready", 2)
        ss_ready = sig("ss_ready", 4)
        ms_ready = sig("ms_ready", 4)
        rms_ready = sig("rms_ready", 4)
        q1_steps = sig("q1_steps", 16)
        q2_steps = sig("q2_steps", 12)
        qb_ready = sig("qb_ready", 2)
        qt_ready = sig("qt_ready", 2)
        qbt_copied = sig("qbt_copied", 2)
        hid_ready = sig("hid_ready", 4)
        up_ready = sig("up_ready", 4)
        th2_ready = sig("th2_ready", 4)
        hg_ready = sig("hg_ready", 4)
        hc_ready = sig("hc_ready", 4)
        hb_ready = sig("hb_ready", 2)
        hbt_ready = sig("hbt_ready", 2)
        hbt_copied = sig("hbt_copied", 2)
        dn_ready = sig("dn_ready", 2)
        xo_ready = sig("xo_ready", 2)

        pT = late[:, 0:NH1 * P].rearrange("p (h d) -> p h d", h=NH1)
        ssub = late[:, NH1 * P:NH1 * P + NH1 * D].rearrange("p (h e) -> p h e", h=NH1)
        av = late[:, NH1 * P + NH1 * D:NH1 * P + NH1 * D + L]
        qv, hid = (late[:, i * HID:(i + 1) * HID] for i in range(2))
        w = z
        E0, E1 = (e[:, :, :, :].rearrange("p a b c -> p (a b c)") for e in E)
        high = od_sb[:, :].rearrange("p (t l) -> p t l", t=T).bitcast(F32R)
        y = E1[:, T * L:2 * T * L].rearrange("p (t l) -> p t l", t=T)
        yT = E1[:, 2 * T * L:3 * T * L].rearrange("p (c n) -> p c n", c=2)
        cmp_gt, cmp_eq = (E0[:, i * T * NE * NE:(i + 1) * T * NE * NE]
                          .rearrange("p (t i j) -> p t i j", t=T, i=NE) for i in range(2))
        stage = [e[:, :, :, :].rearrange("p a b c -> p (a b c)") for e in E]
        w1s = cwb[:, :, :].rearrange("p a b -> p (a b)")[:, 0:2 * HID]
        w2s = cwb[:, :, :].rearrange("p a b -> p (a b)")[:, 2 * HID:4 * HID]
        w3s = cwb[:, :, :].rearrange("p a b -> p (a b)")[:, 4 * HID:4 * HID + (HK - 1) * L]
        w3tail = x3[:, 0, :]
        GUW = 4 * P
        chunks = [(c, min(4, NX - c)) for c in range(0, NX, 4)]
        Sa = S[:, 0, :]

        def vpart(tl, i):
            v = vpad[:, tl, :].rearrange("p (s k) -> p s k", s=4)[:, :, 16:16 + P]
            return v.rearrange("p s (g k) -> p s g k", g=4)[:, :, :, i * DH:(i + 1) * DH]

        plan = body_plan()
        prologue = prologue_plan(plan)

        def run(eng, handlers):
            def body(mid, extra=()):
                def quad(ahead):
                    q = mid + ahead
                    return None if isinstance(q, int) and not 0 <= q < NQ else q
                for item in extra or plan:
                    q = quad(ahead_of(item))
                    if q is not None and item[0] in handlers:
                        handlers[item[0]](q, *item[1:])
            body(-2)
            body(-1, prologue)
            for q in range(min(2, NQ)):
                body(q)
            if NQ > 4:
                with eng.Fori(2, NQ - 2) as i:
                    body(i)
            for q in range(max(2, NQ - 2), NQ + 2):
                body(q)

        block = stack.enter_context(nc.Block())

        @block.sync
        def _(sp):
            sp.dma_start(xin[:, :, :], x_q[0]).then_inc(xin_in.sem, 16)
            sp.dma_start(ctxa[:, :, :], c_q[0]).then_inc(ctxa_in.sem, 16)
            sp.dma_start(gw[:, :, :], gate_w).then_inc(const_in.sem, 16)
            sp.dma_start(bias_b[:, :], bias.partition_broadcast(P)).then_inc(const_in.sem, 16)
            sp.dma_start(gamma_b[:, :], gamma.partition_broadcast(P)).then_inc(const_in.sem, 16)
            sp.wait_ge(zeroed.sem, 1)
            for n, wt in enumerate((wq, wk, wv, wo)):
                for b in range(2):
                    sp.dma_start(proj[64 * b:64 * b + 64, n, 64 * b:64 * b + 64], wt).then_inc(const_in.sem, 16)

            def weights(_, k):
                loads = [(w1s, w1.rearrange("p c n -> p (c n)")), (w2s, w2.rearrange("p c n -> p (c n)")),
                         (w3s.rearrange("p (c n) -> p c n", n=L),
                          w3[0:(HK - 1) * P, :].rearrange("(c p) n -> p c n", p=P)),
                         (w3tail[0:HR, :], w3[(HK - 1) * P:HID, :])]
                if k == 0:
                    sp.wait_ge(dve_const.sem, 1)
                if k < len(chunks):
                    c, (e0, ne) = k, chunks[k]
                    if c >= 2:
                        sp.wait_ge(split_l.sem, c - 1)
                    sp.dma_start(stage[c % 2][:, 0:ne * GUW], w_gu[:, e0 * GUW:(e0 + ne) * GUW])\
                      .then_inc(gu_in[c % 2].sem, 16)
                if k == len(chunks) - 1:
                    for dst, src in loads:
                        sp.dma_start(dst, src).then_inc(l1w_in.sem, 16)
                    sp.dma_start(wd[:, :, :], w_d).then_inc(wd_in.sem, 16)

            def tile(a, q):
                return a[q] if isinstance(q, int) else a[bass.ds(q, 1)].rearrange("a p t l -> (a p) t l")

            def send_rows(src, side, part):
                sp.dma_start(rows[side, :, part, :, :], src.rearrange("p t l -> p (t l)").bitcast(F32))\
                  .then_inc(rows_out.sem, 16)

            def attention_inputs(q, k):
                if k == 0 and not first(q):
                    sp.wait_ge(xl_ready.sem, xl_ready.at(q - 1))
                    sp.dma_start(xin[:, :, :], tile(x_q, q)).then_inc(xin_in.sem, 16)
                    sp.wait_ge(vt_ready.sem, vt_ready.at(q - 1))
                    sp.dma_start(ctxa[:, :, :], tile(c_q, q)).then_inc(ctxa_in.sem, 16)
                if k == 2:
                    sp.wait_ge(xh_ready.sem, xh_ready.at(q))
                    if not first(q):
                        sp.wait_ge(aug_in.sem, aug_in.at(q - 1, 7))
                    send_rows(high, 0, 0)
                    send_rows(high, 0, 2)
                    sp.wait_ge(xl_ready.sem, xl_ready.at(q))
                    send_rows(xin[:, :, :], 0, 1)
                if k == 3:
                    sp.wait_ge(ch_ready.sem, ch_ready.at(q))
                    send_rows(high, 1, 0)
                    send_rows(high, 1, 1)
                    sp.wait_ge(cl_ready.sem, cl_ready.at(q))
                    send_rows(ctxa[:, :, :], 1, 2)
                    sp.wait_ge(rows_out.sem, rows_out.at(q, 5))
                    sp.dma_start(ctxa[:, :, :], tile(c_q, q)).then_inc(ctxa_in.sem, 16)

            def operands(q, _=0):
                if first(q):
                    sp.wait_ge(zeroed.sem, 2)
                else:
                    sp.wait_ge(s2_ready.sem, s2_ready.at(q - 1, 15))
                for dst, side in ((qaug, 0), (kaug, 1)):
                    for g in range(4):
                        sp.dma_start(dst[32 * g:32 * g + 24, :, :, :].rearrange("r s t l -> r s (t l)").bitcast(F32),
                                     rows[side, 4 * g:4 * g + 4].rearrange("s c r l -> (c r) s l"))\
                          .then_inc(aug_in.sem, 16)

            def residual(q, _=0):
                if not first(q):
                    sp.wait_ge(x1_ready.sem, x1_ready.at(q - 1, 1))
                sp.dma_start(xres[:, :, :], tile(x_q, q)).then_inc(xres_in.sem, 16)

            def maxima(q, t):
                sp.wait_ge(mt_copied.sem, mt_copied.at(q, t))
                for part in range(2):
                    sp.dma_start(qaug[24 + part:P:32, :, t, :].bitcast(F32), mT[16 * part:16 * part + 16, :])\
                      .then_inc(max_in.sem, 16)

            def second_inputs(q, _=0):
                if not first(q):
                    sp.wait_ge(k_ready.sem, k_ready.at(q - 1, 1))
                sp.dma_start(ctxb[:, :, :], c_q[bass.ds(q, 1)].rearrange("a p t l -> (a p) t l")
                             if not isinstance(q, int) else c_q[q]).then_inc(ctxb_in.sem, 16)

            def last_block(q, t, k):
                if t == 1 and k == 10:
                    sp.wait_ge(xo_ready.sem, xo_ready.at(q, 1))
                    sp.dma_start(o_q[bass.ds(q, 1)].rearrange("a p t l -> (a p) t l")
                                 if not isinstance(q, int) else o_q[q], x3[:, :, :]).then_inc(out_sent.sem, 16)

            run(sp, {"A": attention_inputs, "P": operands, "K": residual, "W": weights, "M": maxima, "T":
               second_inputs, "D": last_block})
            sp.wait_ge(out_sent.sem, 16 * NQ)

        @block.gpsimd
        def _(pool):
            n = 0

            def setup(ins):
                nonlocal n
                n += 1
                ins.then_inc(pool_setup.sem, 1)

            def settle():
                pool.wait_ge(pool_setup.sem, n)

            pool.memset(proj[:, :, :], 0.0).then_inc(zeroed.sem, 1)
            setup(pool.memset(ident[:, :], 0.0))
            settle()
            setup(pool.affine_select(out=ident[:, :], in_=ident[:, :], compare_op=ALU.not_equal, fill=1.0,
                                     base=0, pattern=[[-1, P]], channel_multiplier=1))
            setup(pool.memset(mhalf[:, :], -0.5))
            setup(pool.memset(ones[:, :], 1.0))
            setup(pool.memset(lower[:, :, :], 1.0))
            settle()
            pool.affine_select(out=lower[:, :, :], in_=lower[:, :, :], compare_op=ALU.is_gt, fill=0.0,
                               base=0, pattern=[[1, NE], [-1, NE]], channel_multiplier=0)\
                .then_inc(ident_ok.sem, 1)
            pool.wait_ge(ident_ok.sem, 1)
            pool.memset(kaug[:, :, :, :].bitcast(F32), 1.0).then_inc(zeroed.sem, 1)

            def attention_norm(q, k):
                if k != 0:
                    return
                pool.wait_ge(a_var.sem, a_var.at(q))
                pool.tensor_tensor(a_rstd[:, :], a_ve[:, :], mhalf[:, :], ALU.pow).then_inc(a_rs.sem, 1)

            def router(q, k):
                if k == 0:
                    pool.wait_ge(b_var.sem, b_var.at(q))
                    pool.tensor_tensor(b_rstd[:, :], b_ve[:, :], mhalf[:, :], ALU.pow).then_inc(b_rs.sem, 1)

            def expert(q, n):
                if n >= 1:
                    if n >= 3:
                        pool.wait_ge(h_ready.sem, h_ready.at(q, n - 2))
                    if n == 1:
                        pool.wait_ge(bc_copied.sem, bc_copied.at(q, 7))
                    pool.wait_ge(g1_ready.sem, g1_ready.at(q, n))
                    pool.tensor_tensor(g2[n % 2][:, :], g1[n % 2][:, :], cwb[:, n - 1, :], ALU.mult)\
                        .then_inc(g2_ready.sem, 1)

            def second(q, t, k):
                if k == 0:
                    pool.wait_ge(c_var.sem, c_var.at(q))
                    pool.tensor_tensor(c_rstd[:, :], c_ve[:, :], mhalf[:, :], ALU.pow).then_inc(c_rs.sem, 1)

            def rms(q, which, t):
                s = 2 * t + which
                pool.wait_ge(ms_ready.sem, ms_ready.at(q, s))
                pool.tensor_tensor(rs[:, which, t, 2:3], rs[:, which, t, 1:2], mhalf[:, 0:1], ALU.pow)\
                    .then_inc(rms_ready.sem, 1)

            def last_block(q, t, k):
                if k == 0:
                    pool.wait_ge(d_var.sem, d_var.at(q, t))
                    pool.tensor_tensor(d_rstd[:, t:t + 1], d_ve[:, t:t + 1], mhalf[:, 0:1], ALU.pow)\
                        .then_inc(d_rs.sem, 1)
                if k == 2:
                    rms(q, 0, t)
                if k == 7:
                    rms(q, 1, t)

            run(pool, {"A": attention_norm, "R": router, "E": expert, "C": second, "D": last_block})

        @block.scalar
        def _(act):
            def weights(_, k):
                if k < len(chunks):
                    c, (e0, ne) = k, chunks[k]
                    act.wait_ge(gu_in[c % 2].sem, 16 * (c // 2 + 1))
                    act.copy(wgu_h[:, e0:e0 + ne, :, :, :].rearrange("p a b c d -> p (a b c d)"),
                             stage[c % 2][:, 0:ne * GUW]).then_inc(split_h.sem, 1)

            def attention_inputs(q, k):
                if k == 1:
                    act.wait_ge(xn_ready.sem, xn_ready.at(q))
                    if not (isinstance(q, int) and q < 2):
                        act.wait_ge(x1_ready.sem, x1_ready.at(q - 2, 1))
                    act.copy(high, xin[:, :, :]).then_inc(xh_ready.sem, 1)
                if k == 3:
                    act.wait_ge(ctxa_in.sem, ctxa_in.at(q, 0))
                    act.wait_ge(rows_out.sem, rows_out.at(q, 2))
                    act.wait_ge(xl_ready.sem, xl_ready.at(q))
                    act.copy(high, ctxa[:, :, :]).then_inc(ch_ready.sem, 1)

            def values_in(q, k):
                if k != 0:
                    return
                act.wait_ge(vt_ready.sem, vt_ready.at(q))
                if first(q):
                    act.wait_ge(dve_const.sem, 1)
                else:
                    act.wait_ge(pv_done.sem, pv_done.at(q - 1, 7))
                for tl in range(4):
                    ins = act.copy(vpart(tl, 0), Sa[:, tl * P:(tl + 1) * P].rearrange("p (g s r) -> p s g r", g=4, s=4))
                ins.then_inc(vpad_ready.sem, 1)

            def quotient_rows(q, t):
                act.wait_ge(pv_done.sem, pv_done.at(q, 4 * t + 3))
                if t == 1:
                    act.wait_ge(x1_ready.sem, x1_ready.at(q, 0))
                elif not isinstance(q, int) or q + 1 < NQ:
                    act.wait_ge(rows_out.sem, rows_out.at(q + 1, 5))
                    act.wait_ge(cl_ready.sem, cl_ready.at(q + 1))
                else:
                    act.wait_ge(x1_ready.sem, x1_ready.at(q - 1, 1))
                act.copy(od_sb[:, :], OD[:, :]).then_inc(od_copied.sem, 1)

            def exponentials(q, k):
                step = k - 9
                m = step // 2
                act.wait_ge(s2_ready.sem, s2_ready.at(q, step))
                if m >= 2:
                    act.wait_ge(pv_done.sem, pv_done.at(q, m - 2))
                elif first(q):
                    act.wait_ge(split_l.sem, len(chunks))
                else:
                    act.wait_ge(pv_done.sem, pv_done.at(q - 1, m + 6))
                    if m == 1:
                        act.wait_ge(ytl_ready.sem, ytl_ready.at(q - 1))
                    if m == 0:
                        act.wait_ge(cwhl_ready.sem, cwhl_ready.at(q - 1))
                u0 = 2 * (step % 2)
                act.activation(E[m % 2][:, u0:u0 + 2, :, :].rearrange("p a b c -> p a (b c)"), S[:, :, :],
                               ACT.Exp, scale=float(DH) ** -0.5).then_inc(exp_ready.sem, 1)

            def router(q, k):
                if k == 2:
                    act.wait_ge(yt_ready.sem, yt_ready.at(q))
                    act.copy(yT.rearrange("p a b -> p (a b)"), OD[:, :]).then_inc(yt_copied.sem, 1)
                if k == 3:
                    act.wait_ge(logits_ready.sem, logits_ready.at(q))
                    act.activation(sc_e[:, :, :].rearrange("p a b -> p (a b)"), OD[:, 0:T * NE], ACT.Exp,
                                   scale=-1.0).then_inc(e_ready.sem, 1)
                if k == 7:
                    act.wait_ge(cwt_ready.sem, cwt_ready.at(q))
                    act.copy(cwT[:, :], OD[0:2 * NE, 0:T * P]).then_inc(cwt_copied.sem, 1)

            def experts_start(q, k):
                if k == 0:
                    if not first(q):
                        act.wait_ge(gu_ready.sem, gu_ready.at(q - 1, NX - 1))
                    act.wait_ge(yt_copied.sem, yt_copied.at(q))
                    act.copy(yT_h[:, :, :], yT).then_inc(yth_ready.sem, 1)
                    act.wait_ge(x1_ready.sem, x1_ready.at(q, 1))
                    if not first(q):
                        act.wait_ge(x2_ready.sem, x2_ready.at(q - 1))
                    act.copy(x1b[:, :, :], x1[:, :, :]).then_inc(x1b_ready.sem, 1)
                else:
                    for r in (2 * (k - 1), 2 * (k - 1) + 1):
                        act.wait_ge(bc_ready.sem, bc_ready.at(q, r))
                        act.copy(cwb[:, 2 * r:2 * r + 2, :].rearrange("p a b -> p (a b)"), GU[r % 2][:, :])\
                           .then_inc(bc_copied.sem, 1)

            def expert(q, n):
                act.wait_ge(gu_ready.sem, gu_ready.at(q, n))
                if n >= 2:
                    act.wait_ge(g1_ready.sem, g1_ready.at(q, n - 2))
                elif not first(q):
                    act.wait_ge(g1_ready.sem, g1_ready.at(q - 1, NX - 1))
                act.activation(th[n % 2][:, :], GU[n % 2][:, 0:L], ACT.Tanh, scale=0.5).then_inc(th_ready.sem, 1)

            def second(q, t, k):
                if k == 2:
                    act.wait_ge(qv_ready.sem, qv_ready.at(q, t))
                    act.copy(qT[:, :], BA[:, 0:2 * P]).then_inc(qt_copied.sem, 1)
                    act.copy(v1[:, :], BA[:, L:2 * L]).then_inc(v_copied.sem, 1)
                    act.wait_ge(k_ready.sem, k_ready.at(q, t))
                    for j in range(4):
                        r = slice(32 * j, 32 * j + 32)
                        ins = act.copy(kmask[r, :, j, :], BB[r, 0:2 * P].rearrange("p (c n) -> p c n", c=2))
                    ins.then_inc(k_copied.sem, 1)
                if k == 3:
                    act.wait_ge(ssub_ready.sem, ssub_ready.at(q, t))
                    for b in range(2):
                        r = slice(64 * b, 64 * b + 64)
                        ins = act.activation(ppad[r, :, b, :], ssub[r, :, :], ACT.Exp, scale=float(NW) ** -0.5)
                    ins.then_inc(p_ready.sem, 1)
                if k == 4:
                    act.wait_ge(pt_ready.sem, pt_ready.at(q, t))
                    act.copy(pT[:, 0:4, :].rearrange("p a b -> p (a b)"), BA[:, :]).then_inc(pt_copied0.sem, 1)

            def last_block(q, t, k):
                if k == 1:
                    act.wait_ge(w_ready.sem, w_ready.at(q, t))
                    if t == 1:
                        act.wait_ge(hb_ready.sem, hb_ready.at(q, 0))
                    act.activation(qv[:, 0:L], w[:, t, :], ACT.Square, accum_out=rs[:, 0, t, 0:1])\
                       .then_inc(ss_ready.sem, 1)
                if k == 4:
                    act.wait_ge(qt_ready.sem, qt_ready.at(q, t))
                    act.copy(qbT[:, :, :].rearrange("p a b -> p (a b)"), BA[:, 0:P].bitcast(BF16))\
                       .then_inc(qbt_copied.sem, 1)
                if k in (5, 6):
                    c = k - 5
                    act.wait_ge(hid_ready.sem, hid_ready.at(q, 2 * t + c))
                    if c == 0:
                        act.wait_ge(q1_steps.sem, q1_steps.at(q, 8 * t + 5))
                    act.activation(hid[:, c * HC:(c + 1) * HC], BB[:, 0:HC], ACT.Tanh, scale=rs[:, 0, t, 6:7])\
                       .then_inc(th2_ready.sem, 1)
                if k == 7:
                    act.wait_ge(hc_ready.sem, hc_ready.at(q, 2 * t + 1))
                    act.activation(qv[:, :], hid[:, :], ACT.Square, accum_out=rs[:, 1, t, 0:1])\
                       .then_inc(ss_ready.sem, 1)
                if k == 9:
                    act.wait_ge(hbt_ready.sem, hbt_ready.at(q, t))
                    src = BB[:, 0:HK * P // 2].bitcast(BF16)
                    act.copy(hbT[0:HR, HK - 1, :], src[0:HR, (HK - 1) * P:HK * P])
                    act.copy(hbT[:, 0:HK - 1, :].rearrange("p a b -> p (a b)"), src[:, 0:(HK - 1) * P])\
                       .then_inc(hbt_copied.sem, 1)

            run(act, {"A": attention_inputs, "K": values_in, "W": weights, "X": exponentials, "G":
                quotient_rows, "R": router, "B": experts_start, "E": expert,
                      "C": second, "D": last_block})

        @block.vector
        def _(dve):
            step = Steps(dve, setup_steps, 0)
            dve.memset(vpad[:, :, :], 0.0)
            dve.memset(kmask[:, :, :, :], 0.0)
            dve.memset(ppad[:, :, :, :], 0.0)
            step.done(dve.memset(take[:, :, :], 0.0))
            for tl in range(2 * T):
                dve.memset(vpart(tl, 1), 1.0)
            dve.memset(w3tail[HR:P, :], 0.0)
            dve.memset(wabs[:, :], 0.0).then_inc(dve_const.sem, 1)

            def attention_inputs(q, k):
                if k == 0:
                    s = Steps(dve, a_steps, q)
                    dve.wait_ge(xin_in.sem, xin_in.at(q))
                    dve.bn_stats(a_st[:, 0, :], xin[:, 0, :])
                    s.done(dve.bn_stats(a_st[:, 1, :], xin[:, 1, :]))
                    dve.memset(spare[:, :], 0.0)
                    dve.bn_aggr(a_mv[:, 0, :], a_st[:, 0, :])
                    s.done(dve.bn_aggr(a_mv[:, 1, :], a_st[:, 1, :]))
                    dve.tensor_scalar(a_ve[:, :], a_mv[:, :, 1], LN_EPS, None, ALU.add).then_inc(a_var.sem, 1)
                    s.end()
                if k == 1:
                    dve.wait_ge(a_rs.sem, a_rs.at(q))
                    for t in range(T):
                        ins = dve.tensor_scalar(xin[:, t, :], xin[:, t, :], a_mv[:, t, 0:1], a_rstd[:, t:t + 1],
                                                ALU.subtract, ALU.mult)
                    ins.then_inc(xn_ready.sem, 1)
                if k == 2:
                    dve.wait_ge(xh_ready.sem, xh_ready.at(q))
                    dve.tensor_tensor(xin[:, :, :].bitcast(F32R), xin[:, :, :], high.bitcast(F32), ALU.subtract)\
                       .then_inc(xl_ready.sem, 1)
                if k == 3:
                    dve.wait_ge(ch_ready.sem, ch_ready.at(q))
                    dve.tensor_tensor(ctxa[:, :, :].bitcast(F32R), ctxa[:, :, :], high.bitcast(F32), ALU.subtract)\
                       .then_inc(cl_ready.sem, 1)

            def maxima(q, t):
                dve.wait_ge(mt_ready.sem, mt_ready.at(q, t))
                if t == 1:
                    dve.wait_ge(max_in.sem, max_in.at(q, 1))
                elif not first(q):
                    dve.wait_ge(max_in.sem, max_in.at(q - 1, 3))
                dve.tensor_copy(mT[:, :], S[0:32, 0, 0:L]).then_inc(mt_copied.sem, 1)

            def head_slot(q, k):
                if k < 16:
                    t, s, g0 = k // 8, k // 2 % 4, 2 * (k % 2)
                    dve.wait_ge(s1_ready.sem, s1_ready.at(q, k))
                    dst = mneg[:, t, :, :].rearrange("p c (g s) -> p g c s", g=4)[:, g0:g0 + 2, :, s]
                    dve.tensor_reduce(dst, S[:, :, :].rearrange("p v (c l) -> p v c l", c=2), AX.X, ALU.max,
                                      negate=True).then_inc(s1_read.sem, 1)
                if k in (7, 15):
                    t = k // 8
                    dve.wait_ge(s1_read.sem, s1_read.at(q, k))
                    dve.tensor_copy(mhl[:, t, :, 0, :].bitcast(F32R), mneg[:, t, :, :]).then_inc(max_steps.sem, 1)
                    dve.wait_ge(max_steps.sem, max_steps.at(q, t))
                    dve.tensor_tensor(mhl[:, t, :, 1, :].bitcast(F32R), mneg[:, t, :, :], mhl[:, t, :, 0, :],
                                      ALU.subtract).then_inc(mhl_ready.sem, 1)

            def heads_end(q, t):
                if t == 0:
                    dve.wait_ge(xres_in.sem, xres_in.at(q))
                    if not first(q):
                        dve.wait_ge(x1b_ready.sem, x1b_ready.at(q - 1))
                dve.wait_ge(od_taken.sem, od_taken.at(q, t))
                dve.reciprocal(rden[:, :], OD[:, L:2 * L]).then_inc(fin_steps.sem, 1)
                dve.wait_ge(fin_steps.sem, fin_steps.at(q, 2 * t))
                dve.tensor_tensor(attn[:, :], rden[:, :], OD[:, 0:L], ALU.mult).then_inc(fin_steps.sem, 1)
                dve.wait_ge(fin_steps.sem, fin_steps.at(q, 2 * t + 1))
                dve.scalar_tensor_tensor(x1[:, t, :], attn[:, :], gamma_b[:, 0:1], xres[:, t, :], ALU.mult,
                                         ALU.add).then_inc(x1_ready.sem, 1)

            routing = [None]

            def router(q, k):
                if k == 0:
                    dve.wait_ge(x1_ready.sem, x1_ready.at(q, 1))
                    s = Steps(dve, b_steps, q)
                    dve.bn_stats(b_st[:, 0, :], x1[:, 0, :])
                    s.done(dve.bn_stats(b_st[:, 1, :], x1[:, 1, :]))
                    dve.memset(spare[:, :], 0.0)
                    dve.bn_aggr(b_mv[:, 0, :], b_st[:, 0, :])
                    s.done(dve.bn_aggr(b_mv[:, 1, :], b_st[:, 1, :]))
                    dve.tensor_scalar(b_ve[:, :], b_mv[:, :, 1], LN_EPS, None, ALU.add).then_inc(b_var.sem, 1)
                    s.end()
                if k == 1:
                    dve.wait_ge(b_rs.sem, b_rs.at(q))
                    for t in range(T):
                        ins = dve.tensor_scalar(y[:, t, :], x1[:, t, :], b_mv[:, t, 0:1], b_rstd[:, t:t + 1],
                                                ALU.subtract, ALU.mult)
                    ins.then_inc(y_ready.sem, 1)
                if k == 4:
                    dve.wait_ge(e_ready.sem, e_ready.at(q))
                    routing[0] = Steps(dve, route_steps, q)
                s = routing[0]
                if k == 4:
                    s.done(dve.tensor_scalar(sc_e[:, :, :], sc_e[:, :, :], 1.0, None, ALU.add))
                    s.done(dve.reciprocal(score[:, :, :], sc_e[:, :, :]))
                    s.done(dve.tensor_tensor(sel[:, :, :], score[:, :, :],
                                             bias_b[:, :].unsqueeze(1).to_broadcast([P, T, NE]), ALU.add))
                if k == 5:
                    of_j = sel[:, :, :].unsqueeze(2).to_broadcast([P, T, NE, NE])
                    of_i = sel[:, :, :].unsqueeze(3).to_broadcast([P, T, NE, NE])
                    s.done(dve.tensor_tensor(cmp_gt[:, :, :, :], of_j, of_i, ALU.is_gt))
                    s.done(dve.tensor_tensor(cmp_eq[:, :, :, :], of_j, of_i, ALU.is_equal))
                    s.done(dve.tensor_tensor(cmp_eq[:, :, :, :], cmp_eq[:, :, :, :],
                                             lower[:, :, :].unsqueeze(1).to_broadcast([P, T, NE, NE]), ALU.mult))
                    s.done(dve.tensor_tensor(cmp_gt[:, :, :, :], cmp_gt[:, :, :, :], cmp_eq[:, :, :, :], ALU.add))
                    s.done(dve.tensor_reduce(rank[:, :, :], cmp_gt[:, :, :, :], AX.X, ALU.add))
                if k == 6:
                    s.done(dve.scalar_tensor_tensor(cw[:, :, :], rank[:, :, :], TOP_K - 0.5, score[:, :, :],
                                                    ALU.is_lt, ALU.mult))
                    s.done(dve.tensor_reduce(csum[:, :], cw[:, :, :], AX.X, ALU.add))
                    s.done(dve.reciprocal(crec[:, :], csum[:, :]))
                    s.done(dve.scalar_tensor_tensor(cw[:, :, :], cw[:, :, :], 0.5,
                                                    crec[:, :].unsqueeze(2).to_broadcast([P, T, NE]),
                                                    ALU.mult, ALU.mult))
                    s.done(dve.tensor_copy(cwhl[:, :, 0, :].bitcast(F32R), cw[:, :, :]))
                    dve.tensor_tensor(cwhl[:, :, 1, :].bitcast(F32R), cw[:, :, :], cwhl[:, :, 0, :], ALU.subtract)\
                       .then_inc(cwhl_ready.sem, 1)
                    s.end()

            def experts_start(q, k):
                if k == 0:
                    if not first(q):
                        dve.wait_ge(gu_ready.sem, gu_ready.at(q - 1, NX - 1))
                    dve.wait_ge(yth_ready.sem, yth_ready.at(q))
                    dve.tensor_tensor(yT_l[:, :, :], yT, yT_h[:, :, :].bitcast(F32), ALU.subtract)\
                       .then_inc(ytl_ready.sem, 1)

            def hidden(q, n):
                if n == 0:
                    dve.wait_ge(g1_ready.sem, g1_ready.at(q, 0))
                else:
                    dve.wait_ge(g2_ready.sem, g2_ready.at(q, n - 1))
                if n >= 3:
                    dve.wait_ge(down_done.sem, down_done.at(q, n - 3))
                elif not first(q):
                    dve.wait_ge(down_done.sem, down_done.at(q - 1, NX - 1))
                up = GU[n % 2][:, L:2 * L]
                if n == 0:
                    ins = dve.scalar_tensor_tensor(h[0][:, :], g1[0][:, :], 0.5, up, ALU.mult, ALU.mult)
                else:
                    ins = dve.tensor_tensor(h[n % 3][:, :], g2[n % 2][:, :], up, ALU.mult)
                ins.then_inc(h_ready.sem, 1)

            def expert(q, n):
                dve.wait_ge(th_ready.sem, th_ready.at(q, n))
                dve.scalar_tensor_tensor(g1[n % 2][:, :], th[n % 2][:, :], 1.0, GU[n % 2][:, 0:L], ALU.add,
                                         ALU.mult).then_inc(g1_ready.sem, 1)

            def experts_end(q, _=0):
                dve.wait_ge(down_done.sem, down_done.at(q, NX - 1))
                dve.wait_ge(x1b_ready.sem, x1b_ready.at(q))
                dve.tensor_tensor(x2[:, :, :].rearrange("p a b -> p (a b)"),
                                  x1b[:, :, :].rearrange("p a b -> p (a b)"), Y[:, :], ALU.add)\
                   .then_inc(x2_ready.sem, 1)

            def second(q, t, k):
                if k == 0:
                    dve.wait_ge(x2_ready.sem, x2_ready.at(q))
                    s = Steps(dve, c_steps, q)
                    dve.bn_stats(c_st[:, 0, :], x2[:, 0, :])
                    s.done(dve.bn_stats(c_st[:, 1, :], x2[:, 1, :]))
                    dve.memset(spare[:, :], 0.0)
                    dve.bn_aggr(c_mv[:, 0, :], c_st[:, 0, :])
                    s.done(dve.bn_aggr(c_mv[:, 1, :], c_st[:, 1, :]))
                    dve.tensor_scalar(c_ve[:, :], c_mv[:, :, 1], LN_EPS, None, ALU.add)\
                       .then_inc(c_var.sem, 1)
                    s.end()
                if k == 1:
                    dve.wait_ge(c_rs.sem, c_rs.at(q))
                    dve.tensor_scalar(z[:, 1, :], x2[:, 1, :], c_mv[:, 1, 0:1], c_rstd[:, 1:2],
                                      ALU.subtract, ALU.mult)
                    dve.tensor_scalar(z[:, 0, :], x2[:, 0, :], c_mv[:, 0, 0:1], c_rstd[:, 0:1],
                                      ALU.subtract, ALU.mult).then_inc(z_ready.sem, 1)
                if k == 3:
                    dve.wait_ge(sc_ready.sem, sc_ready.at(q, t))
                    scores = BA[:, :].rearrange("p (h e) -> p h e", h=NH1)
                    dve.tensor_reduce(smx[:, :], scores, AX.X, ALU.max).then_inc(smax_steps.sem, 1)
                    dve.wait_ge(smax_steps.sem, smax_steps.at(q, t))
                    dve.tensor_tensor(ssub[:, :, :], scores, smx[:, :].unsqueeze(2).to_broadcast([P, NH1, D]),
                                      ALU.subtract).then_inc(ssub_ready.sem, 1)
                if k == 4:
                    dve.wait_ge(p_ready.sem, p_ready.at(q, t))
                    for b in range(2):
                        r = slice(64 * b, 64 * b + 64)
                        ins = dve.tensor_reduce(ssum[r, :], ppad[r, :, b, :], AX.X, ALU.add)
                    ins.then_inc(srec_steps.sem, 1)
                    dve.wait_ge(pt_ready.sem, pt_ready.at(q, t))
                    dve.tensor_copy(pT[:, 4:8, :].rearrange("p a b -> p (a b)"), BB[:, :])\
                       .then_inc(pt_copied1.sem, 1)
                if k == 5:
                    dve.wait_ge(srec_steps.sem, srec_steps.at(q, 2 * t))
                    dve.reciprocal(srec[:, :], ssum[:, :]).then_inc(srec_steps.sem, 1)
                    dve.wait_ge(srec_steps.sem, srec_steps.at(q, 2 * t + 1))
                    dve.wait_ge(av_ready.sem, av_ready.at(q, t))
                    dve.tensor_tensor(av[:, :].rearrange("p (h n) -> p h n", h=NH1),
                                      srec[:, :].unsqueeze(2).to_broadcast([P, NH1, NW]),
                                      BA[:, 0:L].rearrange("p (h n) -> p h n", h=NH1), ALU.mult)\
                       .then_inc(av_steps.sem, 1)
                    dve.wait_ge(av_steps.sem, av_steps.at(q, t))
                    dve.tensor_tensor(av[:, :], z[:, t, :], av[:, :], ALU.subtract).then_inc(u_ready.sem, 1)
                if k == 6:
                    dve.wait_ge(o_ready.sem, o_ready.at(q, t))
                    if t == 0 and not first(q):
                        dve.wait_ge(out_sent.sem, out_sent.at(q - 1))
                    dve.tensor_tensor(x3[:, t, :], x2[:, t, :], BA[:, L:2 * L], ALU.add).then_inc(x3_ready.sem, 1)

            def column(which, t, i):
                return rs[:, which, t, i:i + 1]

            def magnitudes(q, s, which, t, src, n):
                s.done(dve.tensor_reduce(column(which, t, 3), src, AX.X, ALU.max, apply_absolute_value=True))
                dve.wait_ge(ss_ready.sem, ss_ready.at(q, 2 * t + which))
                dve.tensor_scalar(column(which, t, 1), column(which, t, 0), 1.0 / n, RMS_EPS, ALU.mult, ALU.add)\
                   .then_inc(ms_ready.sem, 1)

            def quantise(q, s, which, t, src, n, dst, ready):
                c = [column(which, t, i) for i in range(8)]
                dve.wait_ge(rms_ready.sem, rms_ready.at(q, 2 * t + which))
                s.done(dve.tensor_scalar(c[4], c[3], c[2], QUANT_EPS, ALU.mult, ALU.max))
                s.done(dve.reciprocal(c[5], c[4]))
                s.done(dve.scalar_tensor_tensor(c[5], c[5], 127.0, c[2], ALU.mult, ALU.mult))
                s.done(dve.tensor_scalar(qv[:, 0:n], src, c[5], MAGIC, ALU.mult, ALU.add))
                dve.tensor_scalar(dst, qv[:, 0:n], MAGIC, 127.0, ALU.subtract, ALU.min).then_inc(ready.sem, 1)

            def last_block(q, t, k):
                if k == 0:
                    dve.wait_ge(x3_ready.sem, x3_ready.at(q, t))
                    dve.bn_stats(d_st[:, t, :], x3[:, t, :]).then_inc(d_steps.sem, 1)
                    dve.wait_ge(d_steps.sem, d_steps.at(q, 2 * t))
                    dve.memset(spare[:, :], 0.0)
                    dve.bn_aggr(d_mv[:, t, :], d_st[:, t, :]).then_inc(d_steps.sem, 1)
                    dve.wait_ge(d_steps.sem, d_steps.at(q, 2 * t + 1))
                    dve.tensor_scalar(d_ve[:, t:t + 1], d_mv[:, t, 1:2], LN_EPS, None, ALU.add)\
                       .then_inc(d_var.sem, 1)
                if k == 1:
                    dve.wait_ge(d_rs.sem, d_rs.at(q, t))
                    dve.tensor_scalar(w[:, t, :], x3[:, t, :], d_mv[:, t, 0:1], d_rstd[:, t:t + 1],
                                      ALU.subtract, ALU.mult).then_inc(w_ready.sem, 1)
                if k == 2:
                    dve.wait_ge(w_ready.sem, w_ready.at(q, t))
                    if t == 1:
                        dve.wait_ge(hb_ready.sem, hb_ready.at(q, 0))
                    magnitudes(q, Steps(dve, q1_steps, q, 8 * t), 0, t, w[:, t, :], L)
                if k == 3:
                    s = Steps(dve, q1_steps, q, 8 * t + 1)
                    quantise(q, s, 0, t, w[:, t, :], L, qb[:, :], qb_ready)
                    c = [column(0, t, i) for i in range(8)]
                    s.done(dve.tensor_scalar(c[6], c[4], 0.5 / 127.0, wmean[:, 0:1], ALU.mult, ALU.mult))
                    s.done(dve.tensor_scalar(c[7], c[4], 1.0 / 127.0, wmean[:, 1:2], ALU.mult, ALU.mult))
                    s.done(dve.tensor_tensor(c[7], c[6], c[7], ALU.mult))
                    if t == 1:
                        s.end()
                if k in (5, 6):
                    c = k - 5
                    part = hid[:, c * HC:(c + 1) * HC]
                    dve.wait_ge(th2_ready.sem, th2_ready.at(q, 2 * t + c))
                    dve.scalar_tensor_tensor(part, part, 1.0, BB[:, 0:HC], ALU.add, ALU.mult)\
                       .then_inc(hg_ready.sem, 1)
                    dve.wait_ge(hg_ready.sem, hg_ready.at(q, 2 * t + c))
                    dve.wait_ge(up_ready.sem, up_ready.at(q, 2 * t + c))
                    dve.scalar_tensor_tensor(part, part, column(0, t, 7), BA[:, 0:HC], ALU.mult, ALU.mult)\
                       .then_inc(hc_ready.sem, 1)
                if k == 7:
                    dve.wait_ge(hc_ready.sem, hc_ready.at(q, 2 * t + 1))
                    magnitudes(q, Steps(dve, q2_steps, q, 6 * t), 1, t, hid[:, :], HID)
                if k == 8:
                    s = Steps(dve, q2_steps, q, 6 * t + 1)
                    quantise(q, s, 1, t, hid[:, :], HID, hb[:, :], hb_ready)
                    s.done(dve.tensor_scalar(column(1, t, 6), column(1, t, 4), 1.0 / 127.0, wmean[:, 2:3],
                                             ALU.mult, ALU.mult))
                    if t == 1:
                        s.end()
                if k == 10:
                    dve.wait_ge(dn_ready.sem, dn_ready.at(q, t))
                    dve.scalar_tensor_tensor(x3[:, t, :], BA[:, 0:L], column(1, t, 6), x3[:, t, :], ALU.mult,
                                             ALU.add).then_inc(xo_ready.sem, 1)

            def weights(_, k):
                if k < len(chunks):
                    c, (e0, ne) = k, chunks[k]
                    dve.wait_ge(split_h.sem, c + 1)
                    hi = wgu_h[:, e0:e0 + ne, :, :, :].rearrange("p a b c d -> p (a b c d)").bitcast(F32)
                    dve.tensor_tensor(wgu_l[:, e0:e0 + ne, :, :, :].rearrange("p a b c d -> p (a b c d)"),
                                      stage[c % 2][:, 0:ne * GUW], hi, ALU.subtract).then_inc(split_l.sem, 1)
                if k == 5:
                    dve.tensor_tensor(pick[:, :, :],
                                      ident[0:2 * NE, 0:NE].unsqueeze(2).to_broadcast([2 * NE, NE, P]),
                                      ident[0:2 * NE, NE:2 * NE].unsqueeze(2).to_broadcast([2 * NE, NE, P]), ALU.add)
                    dve.wait_ge(l1w_in.sem, 64)
                    dve.tensor_reduce(wabs[:, 0:1], w1s, AX.X, ALU.add, apply_absolute_value=True)
                    dve.tensor_reduce(wabs[:, 1:2], w2s, AX.X, ALU.add, apply_absolute_value=True)
                    dve.tensor_reduce(wabs[:, 2:3], w3s, AX.X, ALU.add, apply_absolute_value=True)
                    dve.tensor_reduce(wabs[:, 3:4], w3tail[:, :], AX.X, ALU.add, apply_absolute_value=True)\
                       .then_inc(wsum_ready.sem, 1)
                if k == 6:
                    dve.wait_ge(wsum_done.sem, 1)
                    step.done(dve.tensor_copy(wmean[:, :], GU[0][:, 0:4]))
                    step.done(dve.tensor_tensor(wmean[:, 2:3], wmean[:, 2:3], wmean[:, 3:4], ALU.add))
                    step.done(dve.tensor_scalar(wmean[:, 0:3], wmean[:, 0:3], 1.0 / (HID * L), QUANT_EPS,
                                                ALU.mult, ALU.max))
                    step.done(dve.reciprocal(wscale[:, 0:3], wmean[:, 0:3]))
                parts = ((0, w1s, w1q[:, :, :].rearrange("p a b -> p (a b)")),
                         (1, w2s, w2q[:, :, :].rearrange("p a b -> p (a b)")),
                         (2, w3s, w3q[:, 0:HK - 1, :].rearrange("p a b -> p (a b)")),
                         (2, w3tail[:, :], w3q[:, HK - 1, :]))
                for n, src, dst in {6: parts[0:1], 7: parts[1:2], 8: parts[2:4]}.get(k, ()):
                    step.done(dve.tensor_scalar(src, src, wscale[:, n:n + 1], MAGIC, ALU.mult, ALU.add))
                    step.done(dve.tensor_scalar(src, src, MAGIC, 1.0, ALU.subtract, ALU.min))
                    step.done(dve.tensor_scalar(dst, src, -1.0, None, ALU.max))
                if k == 8:
                    dve.tensor_copy(wabs[:, 0:1], wabs[:, 0:1]).then_inc(dve_const.sem, 1)

            dve.wait_ge(ident_ok.sem, 1)
            dve.tensor_copy(ident_bf[:, :], ident[:, :])
            for kind in range(2):
                dve.tensor_copy(take[:, kind, 16:16 + P].rearrange("p (g a r) -> p g a r", g=4, a=4)[:, :, 0:2, :],
                                ident[:, :].rearrange("p (g a b r) -> p g a b r", g=4, a=2, b=2)[:, :, :, kind, :])
            run(dve, {"A": attention_inputs, "W": weights, "H": head_slot, "M": maxima, "F": heads_end, "R":
                router, "B": experts_start, "E": expert, "Y": hidden, "T": experts_end,
                      "C": second, "D": last_block})

        @block.tensor
        def _(pe):
            pe.wait_ge(ident_ok.sem, 1)

            def weights(_, k):
                if k == 6:
                    pe.wait_ge(wsum_ready.sem, 1)
                    pe.matmul(GU[0][:, 0:4], ones[:, :], wabs[:, :], start=True, stop=True).then_inc(wsum_done.sem, 1)

            def values_in(q, k):
                if k != 0:
                    return
                pe.wait_ge(ctxa_in.sem, ctxa_in.at(q, 1))
                if not first(q):
                    pe.wait_ge(exp_ready.sem, exp_ready.at(q - 1, 15))
                for t in range(T):
                    for c in range(2):
                        ins = pe.transpose(Sa[:, (2 * t + c) * P:(2 * t + c + 1) * P],
                                           ctxa[:, t, c * P:(c + 1) * P], ident[:, :])
                ins.then_inc(vt_ready.sem, 1)

            def values(q, k):
                m = (k - 11) // 2
                t, s = m // 4, m % 4
                pe.wait_ge(exp_ready.sem, exp_ready.at(q, 2 * m + 1))
                if m == 4:
                    pe.wait_ge(x1_ready.sem, x1_ready.at(q, 0))
                elif m == 0 and not first(q):
                    pe.wait_ge(cwt_copied.sem, cwt_copied.at(q - 1))
                if m == 0:
                    pe.wait_ge(vpad_ready.sem, vpad_ready.at(q))
                half = slice(s // 2 * L, (s // 2 + 1) * L)
                for c in range(2):
                    for g in range(4):
                        at = s * (16 + P) + 16 + 32 * g - 16 * (s % 2)
                        ins = pe.matmul(OD[32 * g:32 * g + 32, half], vpad[:, 2 * t + c, at:at + 32],
                                        E[m % 2][:, g, c, :], start=(s == 0 and c == 0),
                                        stop=(s % 2 == 1 and c == 1), skip_group_check=True)
                ins.then_inc(pv_done.sem, 1)

            def quotient_rows(q, t):
                pe.wait_ge(od_copied.sem, od_copied.at(q, t))
                for kind in range(2):
                    for half in range(2):
                        ins = pe.matmul(OD[:, kind * L:(kind + 1) * L],
                                        take[:, kind, 16 * (1 - half):16 * (1 - half) + P],
                                        od_sb[:, half * L:(half + 1) * L], start=(half == 0), stop=(half == 1))
                ins.then_inc(od_taken.sem, 1)

            def maxima(q, t):
                pe.wait_ge(mhl_ready.sem, mhl_ready.at(q, t))
                if t == 1:
                    pe.wait_ge(exp_ready.sem, exp_ready.at(q, 6))
                for c in range(2):
                    ins = pe.transpose(S[0:32, 0, c * P:(c + 1) * P],
                                       mhl[:, t, c, :, :].rearrange("p a b -> p (a b)"), ident[:, :])
                ins.then_inc(mt_ready.sem, 1)

            def head_slot(q, k):
                if k < 16:
                    t, s, g0 = k // 8, k // 2 % 4, 2 * (k % 2)
                    if k == 0:
                        pe.wait_ge(vpad_ready.sem, vpad_ready.at(q))
                        pe.wait_ge(aug_in.sem, aug_in.at(q, 7))
                    elif k == 8:
                        pe.wait_ge(mt_copied.sem, mt_copied.at(q, 0))
                    elif k < 10:
                        pe.wait_ge(s1_read.sem, s1_read.at(q, k - 1))
                    else:
                        pe.wait_ge(exp_ready.sem, exp_ready.at(q, k - 10))
                    for c in range(2):
                        for v in range(2):
                            r = slice(32 * (g0 + v), 32 * (g0 + v) + 24)
                            ins = pe.matmul(S[:, v, c * L:(c + 1) * L], qaug[r, s, t, c * P:(c + 1) * P],
                                            kaug[r, s, t, :], start=True, stop=True)
                    ins.then_inc(s1_ready.sem, 1)

            def transposed_scores(q, k):
                step = k - 9
                t, s, g0 = step // 8, step // 2 % 4, 2 * (step % 2)
                if step % 8 == 0:
                    pe.wait_ge(max_in.sem, max_in.at(q, 2 * t + 1))
                if k < 16:
                    pe.wait_ge(s1_read.sem, s1_read.at(q, k))
                elif k == 16:
                    pe.wait_ge(mt_copied.sem, mt_copied.at(q, 1))
                else:
                    pe.wait_ge(exp_ready.sem, exp_ready.at(q, step - 1))
                for c in range(2):
                    for v in range(2):
                        r = slice(32 * (g0 + v), 32 * (g0 + v) + 26)
                        ins = pe.matmul(S[:, v, c * L:(c + 1) * L], kaug[r, s, t, c * P:(c + 1) * P],
                                        qaug[r, s, t, :], start=True, stop=True)
                ins.then_inc(s2_ready.sem, 1)

            def router(q, k):
                if k == 1:
                    pe.wait_ge(y_ready.sem, y_ready.at(q))
                    if first(q):
                        pe.wait_ge(const_in.sem, 16 * 11)
                    for t in range(T):
                        for c in range(2):
                            ins = pe.transpose(OD[:, c * L + t * P:c * L + (t + 1) * P],
                                               y[:, t, c * P:(c + 1) * P], ident[:, :])
                    ins.then_inc(yt_ready.sem, 1)
                if k == 3:
                    pe.wait_ge(yt_copied.sem, yt_copied.at(q))
                    for t in range(T):
                        for c in range(2):
                            ins = pe.matmul(OD[:, t * NE:(t + 1) * NE], yT[:, c, t * P:(t + 1) * P], gw[:, c, :],
                                            start=(c == 0), stop=(c == 1))
                    ins.then_inc(logits_ready.sem, 1)
                if k == 7:
                    pe.wait_ge(cwhl_ready.sem, cwhl_ready.at(q))
                    for t in range(T):
                        ins = pe.transpose(OD[0:2 * NE, t * P:(t + 1) * P],
                                           cwhl[:, t, :, :].rearrange("p a b -> p (a b)"), ident[:, :])
                    ins.then_inc(cwt_ready.sem, 1)

            def experts_start(q, k):
                if k >= 1:
                    for r in (2 * (k - 1), 2 * (k - 1) + 1):
                        if r == 0:
                            pe.wait_ge(cwt_copied.sem, cwt_copied.at(q))
                            if first(q):
                                pe.wait_ge(dve_const.sem, 2)
                                pe.wait_ge(split_l.sem, len(chunks))
                                pe.wait_ge(wd_in.sem, 16)
                            else:
                                pe.wait_ge(h_ready.sem, h_ready.at(q - 1, NX - 1))
                        if r >= 2:
                            pe.wait_ge(bc_copied.sem, bc_copied.at(q, r - 2))
                        for v in range(2):
                            ins = pe.matmul(GU[r % 2][:, v * L:(v + 1) * L], pick[:, 2 * r + v, :], cwT[:, :],
                                            start=True, stop=True)
                        ins.then_inc(bc_ready.sem, 1)

            def down(q, n):
                pe.wait_ge(h_ready.sem, h_ready.at(q, n))
                if n == 0 and not first(q):
                    pe.wait_ge(x2_ready.sem, x2_ready.at(q - 1))
                for t in range(T):
                    ins = pe.matmul(Y[:, t * L:(t + 1) * L], h[n % 3][:, t * P:(t + 1) * P], wd[:, n, :],
                                    start=(n == 0 and t == 0), stop=(n == NX - 1), skip_group_check=True)
                ins.then_inc(down_done.sem, 1)

            def expert(q, n):
                if n < 2:
                    pe.wait_ge(bc_copied.sem, bc_copied.at(q, 6 + n))
                    if n == 0:
                        pe.wait_ge(ytl_ready.sem, ytl_ready.at(q))
                else:
                    pe.wait_ge(h_ready.sem, h_ready.at(q, n - 2))
                for half in range(2):
                    parts = [(c, a, b) for c in range(2) for a, b in ((wgu_h, yT_h), (wgu_h, yT_l), (wgu_l, yT_h))]
                    for i, (c, a, b) in enumerate(parts):
                        ins = pe.matmul(GU[n % 2][:, half * L:(half + 1) * L], a[:, n, c, half, :], b[:, c, :],
                                        start=(i == 0), stop=(i == len(parts) - 1))
                ins.then_inc(gu_ready.sem, 1)

            def second(q, t, k):
                if k == 2:
                    if t == 0:
                        pe.wait_ge(z_ready.sem, z_ready.at(q))
                        pe.wait_ge(ctxb_in.sem, ctxb_in.at(q))
                        if not first(q):
                            pe.wait_ge(xo_ready.sem, xo_ready.at(q - 1, 1))
                    else:
                        pe.wait_ge(x3_ready.sem, x3_ready.at(q, 0))
                    for c in range(2):
                        pe.matmul(BA[:, c * P:(c + 1) * P], z[:, t, c * P:(c + 1) * P], proj[:, 0, :],
                                  start=True, stop=True)
                    pe.matmul(BA[:, L:2 * L], proj[:, 2, :], ctxb[:, t, :], start=True, stop=True)\
                      .then_inc(qv_ready.sem, 1)
                    for c in range(2):
                        ins = pe.matmul(BB[:, c * P:(c + 1) * P], ctxb[:, t, c * P:(c + 1) * P],
                                        proj[:, 1, :], start=True, stop=True)
                    ins.then_inc(k_ready.sem, 1)
                if k == 3:
                    pe.wait_ge(v_copied.sem, v_copied.at(q, t))
                    pe.wait_ge(k_copied.sem, k_copied.at(q, t))
                    for c in range(2):
                        for b in range(2):
                            ins = pe.matmul(BA[64 * b:64 * b + 64, c * L:(c + 1) * L]
                                            .rearrange("p (j e) -> p j e", j=4),
                                            qT[:, c * P + 64 * b:c * P + 64 * b + 64],
                                            kmask[:, c, :, 64 * b:64 * b + 64], start=True, stop=True)
                    ins.then_inc(sc_ready.sem, 1)
                if k == 4:
                    pe.wait_ge(p_ready.sem, p_ready.at(q, t))
                    for n in range(NH1):
                        ins = pe.transpose((BA, BB)[n // 4][:, n % 4 * P:(n % 4 + 1) * P],
                                           ppad[:, n, :, :].rearrange("p a b -> p (a b)"), ident[:, :])
                    ins.then_inc(pt_ready.sem, 1)
                if k == 5:
                    pe.wait_ge(pt_copied0.sem, pt_copied0.at(q, t))
                    pe.wait_ge(pt_copied1.sem, pt_copied1.at(q, t))
                    for n in range(NH1):
                        ins = pe.matmul(BA[:, n * NW:(n + 1) * NW], pT[:, n, :], v1[:, n * NW:(n + 1) * NW],
                                        start=True, stop=True)
                    ins.then_inc(av_ready.sem, 1)
                if k == 6:
                    pe.wait_ge(u_ready.sem, u_ready.at(q, t))
                    pe.matmul(BA[:, L:2 * L], proj[:, 3, :], av[:, :], start=True, stop=True)\
                      .then_inc(o_ready.sem, 1)

            def last_block(q, t, k):
                if k == 4:
                    pe.wait_ge(qb_ready.sem, qb_ready.at(q, t))
                    if t == 0:
                        pe.wait_ge(x3_ready.sem, x3_ready.at(q, 1))
                    else:
                        pe.wait_ge(xo_ready.sem, xo_ready.at(q, 0))
                    tr = BA[:, 0:P].bitcast(BF16)
                    for c in range(2):
                        ins = pe.transpose(tr[:, c * P:(c + 1) * P], qb[:, c * P:(c + 1) * P], ident_bf[:, :])
                    ins.then_inc(qt_ready.sem, 1)
                if k in (5, 6):
                    c = k - 5
                    if c == 0:
                        pe.wait_ge(qbt_copied.sem, qbt_copied.at(q, t))
                    else:
                        pe.wait_ge(hg_ready.sem, hg_ready.at(q, 2 * t))
                    for i in range(2):
                        ins = pe.matmul(BB[:, 0:HC], qbT[:, i, :], w1q[:, i, c * HC:(c + 1) * HC],
                                        start=(i == 0), stop=(i == 1))
                    ins.then_inc(hid_ready.sem, 1)
                    if c == 1:
                        pe.wait_ge(hc_ready.sem, hc_ready.at(q, 2 * t))
                    for i in range(2):
                        ins = pe.matmul(BA[:, 0:HC], qbT[:, i, :], w2q[:, i, c * HC:(c + 1) * HC],
                                        start=(i == 0), stop=(i == 1))
                    ins.then_inc(up_ready.sem, 1)
                if k == 9:
                    pe.wait_ge(hb_ready.sem, hb_ready.at(q, t))
                    tr = BB[:, 0:HK * P // 2].bitcast(BF16)
                    for c in range(HK):
                        n = P if c < HK - 1 else HR
                        ins = pe.transpose(tr[0:n, c * P:(c + 1) * P], hb[:, c * P:c * P + n], ident_bf[:, :])
                    ins.then_inc(hbt_ready.sem, 1)
                if k == 10:
                    pe.wait_ge(hbt_copied.sem, hbt_copied.at(q, t))
                    for c in range(HK):
                        n = P if c < HK - 1 else HR
                        ins = pe.matmul(BA[:, 0:L], hbT[0:n, c, :], w3q[0:n, c, :], start=(c == 0),
                                        stop=(c == HK - 1))
                    ins.then_inc(dn_ready.sem, 1)

            run(pe, {"K": values_in, "W": weights, "H": head_slot, "M": maxima, "X": transposed_scores, "V":
               values, "G": quotient_rows, "R": router,
                     "B": experts_start, "E": expert, "Z": down,
                     "C": second, "D": last_block})


_INS = ["x", "ctx", "gamma", "gate_w", "bias", "w_gu", "w_d", "wq", "wk", "wv", "wo", "w1", "w2", "w3"]


def kernel(x, ctx_2048, L0_xattn_gamma, L0_ffn_gate_w, L0_ffn_expert_bias, L0_ffn_w_gate, L0_ffn_w_up,
           L0_ffn_w_down, L0_ffn_sw_gate, L0_ffn_sw_up, L0_ffn_sw_down, L1_xattn_W_q, L1_xattn_W_k, L1_xattn_W_v,
           L1_xattn_W_o, L1_ffn_w1, L1_ffn_w2, L1_ffn_w3):
    import numpy as np
    import concourse.bacc as _bacc
    from concourse.bass_utils import run_bass_kernel_spmd as _run

    f = np.asarray
    gate = np.concatenate([f(L0_ffn_sw_gate)[None], f(L0_ffn_w_gate)])
    up = np.concatenate([f(L0_ffn_sw_up)[None], f(L0_ffn_w_up)])
    down = np.concatenate([f(L0_ffn_sw_down)[None], f(L0_ffn_w_down)])
    nx, hidden, width = gate.shape
    gu = np.stack([gate, up])
    gu = gu.reshape(2, nx, hidden, width // 128, 128).transpose(4, 1, 3, 0, 2)

    def chunked(a):
        return a.reshape(a.shape[0], -1, 128).transpose(2, 1, 0)

    arrays = {
        "x": f(x), "ctx": f(ctx_2048), "gamma": f(L0_xattn_gamma).reshape(1),
        "gate_w": chunked(f(L0_ffn_gate_w)), "bias": f(L0_ffn_expert_bias),
        "w_gu": gu.reshape(128, -1), "w_d": down.transpose(2, 0, 1),
        "wq": f(L1_xattn_W_q).T, "wk": f(L1_xattn_W_k).T, "wv": f(L1_xattn_W_v).T, "wo": f(L1_xattn_W_o).T,
        "w1": chunked(f(L1_ffn_w1)), "w2": chunked(f(L1_ffn_w2)), "w3": f(L1_ffn_w3).T,
    }
    arrays = {k: np.ascontiguousarray(a) for k, a in arrays.items()}
    nc = _bacc.Bacc("TRN2", target_bir_lowering=False, num_devices=1, dynamic_dma_scratch_size=1024)
    args = [nc.dram_tensor(f"in_{n}", arrays[n].shape, mybir.dt.from_np(arrays[n].dtype), kind="ExternalInput").ap()
            for n in _INS]
    out = nc.dram_tensor("out_0", arrays["x"].shape, F32, kind="ExternalOutput").ap()
    program(nc, *args, out)
    r = _run(nc, [{f"in_{n}": arrays[n] for n in _INS}], core_ids=[0])
    return r.results[0]["out_0"]
```
